# Optimizing a Trainium2 kernel written in Bass

```python
import numpy as np
import jax
import jax.numpy as jnp

def _softmax(x, axis=-1):
    return jax.nn.softmax(x, axis=axis)

def _gelu(x):
    return jax.nn.gelu(x, approximate=True)

def _silu(x):
    return jax.nn.silu(x)

def _sigmoid(x):
    return jax.nn.sigmoid(x)

def _layernorm(x, axis=-1, eps=1e-05):
    m = jnp.mean(x, axis=axis, keepdims=True)
    v = jnp.var(x, axis=axis, keepdims=True)
    return (x - m) / jnp.sqrt(v + eps)

def _scatter_add(tgt, idx, src, axis=0):
    return tgt.at[idx].add(src)

def _segment_sum(src, seg, n):
    return jax.ops.segment_sum(src, seg, n)
kernel_name = 'mk_metaformer_d4_conv_nchw128_r4_93643e'

def setup_inputs(seed: int=0):
    np.random.seed(seed)
    _w = jnp.asarray

    def _rec_inputs():
        import jax
        import jax.numpy as jnp
        _gk = jax.random.key(seed)
        x = -0.0002928 + 1 * jax.random.normal(jax.random.fold_in(_gk, 1), (8, 32, 16, 16), jnp.float32)
        return x
    x = _rec_inputs()

    def _L0_conv_setup():
        import jax, jax.numpy as jnp
        import numpy as np
        K = 7
        PAD = K // 2

        def _unfold(t):
            B, C, H, W = t.shape
            p = jnp.pad(t, ((0, 0), (0, 0), (PAD, PAD), (PAD, PAD)))
            wins = jnp.stack([p[:, :, i:i + H, j:j + W] for i in range(K) for j in range(K)], axis=2)
            return wins
        key = jax.random.key(seed)
        ks = jax.random.split(key, 7)
        B, C, H, W = (8, 32, 16, 16)
        scale = 1.0 / np.sqrt(C)
        x = jax.random.normal(ks[0], (B, C, H, W), dtype=jnp.float32)
        Wq = jax.random.normal(ks[1], (C, C), dtype=jnp.float32) * scale
        Wk = jax.random.normal(ks[2], (C, C), dtype=jnp.float32) * scale
        Wv = jax.random.normal(ks[3], (C, C), dtype=jnp.float32) * scale
        bq = jax.random.normal(ks[4], (C,), dtype=jnp.float32) * 0.01
        bk = jax.random.normal(ks[5], (C,), dtype=jnp.float32) * 0.01
        bv = jax.random.normal(ks[6], (C,), dtype=jnp.float32) * 0.01
        return {'x': x, 'Wq': Wq, 'bq': bq, 'Wk': Wk, 'bk': bk, 'Wv': Wv, 'bv': bv}
    _L0_conv_all = _L0_conv_setup()
    _L0_conv_in = {k: v for k, v in _L0_conv_all.items() if k in ('Wq', 'bq', 'Wk', 'bk', 'Wv', 'bv')}
    del _L0_conv_all

    def _L0_ffn_setup():
        import jax, jax.numpy as jnp
        import numpy as np
        B, N, D, C, E, K = (8, 2048, 32, 32, 8, 2)
        key = jax.random.key(seed)
        k0, k1, k2 = jax.random.split(key, 3)
        x = jax.random.normal(k0, (B, N, D), dtype=jnp.float32)
        router_w = jax.random.normal(k1, (D, E), dtype=jnp.float32) * 0.05
        router_b = jnp.zeros((E,), dtype=jnp.float32)
        expert_w = jax.random.normal(k2, (E, D, C), dtype=jnp.float32) * (1.0 / np.sqrt(D))
        expert_b = jnp.zeros((E, C), dtype=jnp.float32)
        return {'x': x, 'router_w': router_w, 'router_b': router_b, 'expert_w': expert_w, 'expert_b': expert_b}
    _L0_ffn_all = _L0_ffn_setup()
    _L0_ffn_in = {k: v for k, v in _L0_ffn_all.items() if k in ('router_w', 'router_b', 'expert_w', 'expert_b')}
    del _L0_ffn_all

    def _L1_conv_setup():
        import jax, jax.numpy as jnp
        import numpy as np
        B, C, H, W_SP = (16, 32, 28, 28)
        F, KS, STRIDE, PAD = (32, 3, 1, 1)
        CHUNK = 4
        EPS = 1e-12

        def _patches(x):
            p = jax.lax.conv_general_dilated_patches(x, (KS, KS), (STRIDE, STRIDE), [(PAD, PAD), (PAD, PAD)], dimension_numbers=('NCHW', 'OIHW', 'NCHW'))
            b, k, ho, wo = p.shape
            return (p.reshape(b, k, ho * wo), ho, wo)
        key = jax.random.key(seed)
        kx, kw = jax.random.split(key)
        x = jax.random.normal(kx, (B, C, H, W_SP), dtype=jnp.float32)
        std = float(np.sqrt(2.0 / (C * KS * KS)))
        W = jax.random.normal(kw, (F, C, KS, KS), dtype=jnp.float32) * std
        return {'x': x, 'W': W}
    _L1_conv_all = _L1_conv_setup()
    _L1_conv_in = {k: v for k, v in _L1_conv_all.items() if k in ('W',)}
    del _L1_conv_all

    def _L1_ffn_setup():
        import jax, jax.numpy as jnp
        import numpy as np
        B, S, D, E, H, O, K = (128, 512, 32, 16, 128, 32, 8)
        key = jax.random.key(seed)
        k0, k1, k2, k3 = jax.random.split(key, 4)
        x = jax.random.normal(k0, (B, S, D), dtype=jnp.float32)
        gate_w = jax.random.normal(k1, (E, D), dtype=jnp.float32) * (1.0 / np.sqrt(D))
        gate_b = jnp.zeros((E,), dtype=jnp.float32)
        weight1 = jax.random.uniform(k2, (E, D + 1, H), dtype=jnp.float32, minval=-1.0, maxval=1.0) * (1.0 / np.sqrt(D + 1))
        weight2 = jax.random.uniform(k3, (E, H + 1, O), dtype=jnp.float32, minval=-1.0, maxval=1.0) * (1.0 / np.sqrt(H + 1))
        return {'x': x, 'gate_w': gate_w, 'gate_b': gate_b, 'weight1': weight1, 'weight2': weight2}
    _L1_ffn_all = _L1_ffn_setup()
    _L1_ffn_in = {k: v for k, v in _L1_ffn_all.items() if k in ('gate_w', 'gate_b', 'weight1', 'weight2')}
    del _L1_ffn_all

    def _L2_conv_setup():
        import jax, jax.numpy as jnp
        import numpy as np
        G = 4
        K = 9
        EPS = 1e-05

        def _bilinear_gather(value, loc_y, loc_x):
            N, H, W, g, Cg = value.shape
            y0f = jnp.floor(loc_y)
            x0f = jnp.floor(loc_x)
            wy = loc_y - y0f
            wx = loc_x - x0f
            y0 = y0f.astype(jnp.int32)
            x0 = x0f.astype(jnp.int32)
            n_idx = jnp.arange(N).reshape(N, 1, 1, 1, 1)
            g_idx = jnp.arange(g).reshape(1, 1, 1, g, 1)

            def corner(yi, xi, w):
                valid = (yi >= 0) & (yi < H) & (xi >= 0) & (xi < W)
                yc = jnp.clip(yi, 0, H - 1)
                xc = jnp.clip(xi, 0, W - 1)
                v = value[n_idx, yc, xc, g_idx]
                return v * (w * valid)[..., None]
            return corner(y0, x0, (1 - wy) * (1 - wx)) + corner(y0, x0 + 1, (1 - wy) * wx) + corner(y0 + 1, x0, wy * (1 - wx)) + corner(y0 + 1, x0 + 1, wy * wx)

        def _dcnv4(t, H, W, Wv, bv, Wom, bom, Wo):
            N, L, C = t.shape
            Cg = C // G
            value = (t @ Wv + bv).reshape(N, H, W, G, Cg)
            om = (t @ Wom + bom).reshape(N, H, W, G, 3 * K)
            offset = om[..., :2 * K].reshape(N, H, W, G, K, 2)
            mask = om[..., 2 * K:]
            ky, kx = jnp.meshgrid(jnp.arange(-1, 2), jnp.arange(-1, 2), indexing='ij')
            ky = ky.reshape(-1).astype(t.dtype)
            kx = kx.reshape(-1).astype(t.dtype)
            ys = jnp.arange(H, dtype=t.dtype).reshape(1, H, 1, 1, 1)
            xs = jnp.arange(W, dtype=t.dtype).reshape(1, 1, W, 1, 1)
            loc_y = ys + ky + offset[..., 1]
            loc_x = xs + kx + offset[..., 0]
            sampled = _bilinear_gather(value, loc_y, loc_x)
            out = (sampled * mask[..., None]).sum(axis=4)
            return out.reshape(N, L, C) @ Wo

        def _bn(x, gamma, beta):
            mean = x.mean(axis=(0, 2, 3), keepdims=True)
            var = ((x - mean) ** 2).mean(axis=(0, 2, 3), keepdims=True)
            return (x - mean) * jax.lax.rsqrt(var + EPS) * gamma.reshape(1, -1, 1, 1) + beta.reshape(1, -1, 1, 1)
        key = jax.random.key(seed)
        ks = jax.random.split(key, 6)
        N, C, H, W = (4, 32, 16, 16)
        s = 1.0 / np.sqrt(C)
        x = jax.random.normal(ks[0], (N, C, H, W), jnp.float32)
        Wv = jax.random.normal(ks[1], (C, C), jnp.float32) * s
        bv = jnp.zeros((C,), jnp.float32)
        Wom = jax.random.normal(ks[2], (C, G * 3 * K), jnp.float32) * 0.01
        bom = jnp.zeros((G * 3 * K,), jnp.float32)
        Wo = jax.random.normal(ks[3], (C, C), jnp.float32) * s
        gamma = jnp.ones((C,), jnp.float32)
        beta = jnp.zeros((C,), jnp.float32)
        Wc = jax.random.normal(ks[4], (C, C), jnp.float32) * s
        return {'x': x, 'Wv': Wv, 'bv': bv, 'Wom': Wom, 'bom': bom, 'Wo': Wo, 'gamma': gamma, 'beta': beta, 'Wc': Wc}
    _L2_conv_all = _L2_conv_setup()
    _L2_conv_in = {k: v for k, v in _L2_conv_all.items() if k in ('Wv', 'bv', 'Wom', 'bom', 'Wo', 'gamma', 'beta', 'Wc')}
    del _L2_conv_all

    def _L2_ffn_setup():
        import jax, jax.numpy as jnp
        import numpy as np
        B, N, D, C, E, K = (8, 2048, 32, 32, 8, 2)
        key = jax.random.key(seed)
        k0, k1, k2 = jax.random.split(key, 3)
        x = jax.random.normal(k0, (B, N, D), dtype=jnp.float32)
        router_w = jax.random.normal(k1, (D, E), dtype=jnp.float32) * 0.05
        router_b = jnp.zeros((E,), dtype=jnp.float32)
        expert_w = jax.random.normal(k2, (E, D, C), dtype=jnp.float32) * (1.0 / np.sqrt(D))
        expert_b = jnp.zeros((E, C), dtype=jnp.float32)
        return {'x': x, 'router_w': router_w, 'router_b': router_b, 'expert_w': expert_w, 'expert_b': expert_b}
    _L2_ffn_all = _L2_ffn_setup()
    _L2_ffn_in = {k: v for k, v in _L2_ffn_all.items() if k in ('router_w', 'router_b', 'expert_w', 'expert_b')}
    del _L2_ffn_all

    def _L3_conv_setup():
        import jax, jax.numpy as jnp
        import numpy as np
        B, E, H, NY, NX = (16, 32, 4, 32, 32)

        def _conv1x1(x, W, b):
            return jnp.einsum('bcyx,oc->boyx', x, W) + b[None, :, None, None]

        def _rel_indices(ny, nx):
            y = jnp.arange(ny)
            x = jnp.arange(nx)
            y1, x1, y2, x2 = jnp.meshgrid(y, x, y, x, indexing='ij')
            idx = (y1 - y2 + ny - 1) * (2 * nx - 1) + (x1 - x2 + nx - 1)
            return idx.reshape(ny * nx, ny * nx)
        key = jax.random.key(seed)
        ks = jax.random.split(key, 7)
        w = lambda k, shape: jax.random.normal(k, shape, jnp.float32) * 0.02
        return {'x': jax.random.normal(ks[0], (B, E, NY, NX), jnp.float32), 'Wk': w(ks[1], (E, E)), 'bk': jnp.zeros((E,), jnp.float32), 'Wq': w(ks[2], (E, E)), 'bq': jnp.zeros((E,), jnp.float32), 'Wv': w(ks[3], (E, E)), 'bv': jnp.zeros((E,), jnp.float32), 'Wu': w(ks[4], (E, E)), 'bu': jnp.zeros((E,), jnp.float32), 'pos_enc': w(ks[5], (H, (2 * NY - 1) * (2 * NX - 1)))}
    _L3_conv_all = _L3_conv_setup()
    _L3_conv_in = {k: v for k, v in _L3_conv_all.items() if k in ('Wk', 'bk', 'Wq', 'bq', 'Wv', 'bv', 'Wu', 'bu', 'pos_enc')}
    del _L3_conv_all

    def _L3_ffn_setup():
        import jax, jax.numpy as jnp
        import numpy as np
        B, S, D, E, H, O, K = (128, 512, 32, 16, 128, 32, 8)
        key = jax.random.key(seed)
        k0, k1, k2, k3 = jax.random.split(key, 4)
        x = jax.random.normal(k0, (B, S, D), dtype=jnp.float32)
        gate_w = jax.random.normal(k1, (E, D), dtype=jnp.float32) * (1.0 / np.sqrt(D))
        gate_b = jnp.zeros((E,), dtype=jnp.float32)
        weight1 = jax.random.uniform(k2, (E, D + 1, H), dtype=jnp.float32, minval=-1.0, maxval=1.0) * (1.0 / np.sqrt(D + 1))
        weight2 = jax.random.uniform(k3, (E, H + 1, O), dtype=jnp.float32, minval=-1.0, maxval=1.0) * (1.0 / np.sqrt(H + 1))
        return {'x': x, 'gate_w': gate_w, 'gate_b': gate_b, 'weight1': weight1, 'weight2': weight2}
    _L3_ffn_all = _L3_ffn_setup()
    _L3_ffn_in = {k: v for k, v in _L3_ffn_all.items() if k in ('gate_w', 'gate_b', 'weight1', 'weight2')}
    del _L3_ffn_all
    return {'x': x, 'L0_conv_Wq': _L0_conv_in['Wq'], 'L0_conv_bq': _L0_conv_in['bq'], 'L0_conv_Wk': _L0_conv_in['Wk'], 'L0_conv_bk': _L0_conv_in['bk'], 'L0_conv_Wv': _L0_conv_in['Wv'], 'L0_conv_bv': _L0_conv_in['bv'], 'L0_ffn_router_w': _L0_ffn_in['router_w'], 'L0_ffn_router_b': _L0_ffn_in['router_b'], 'L0_ffn_expert_w': _L0_ffn_in['expert_w'], 'L0_ffn_expert_b': _L0_ffn_in['expert_b'], 'L1_conv_W': _L1_conv_in['W'], 'L1_ffn_gate_w': _L1_ffn_in['gate_w'], 'L1_ffn_gate_b': _L1_ffn_in['gate_b'], 'L1_ffn_weight1': _L1_ffn_in['weight1'], 'L1_ffn_weight2': _L1_ffn_in['weight2'], 'L2_conv_Wv': _L2_conv_in['Wv'], 'L2_conv_bv': _L2_conv_in['bv'], 'L2_conv_Wom': _L2_conv_in['Wom'], 'L2_conv_bom': _L2_conv_in['bom'], 'L2_conv_Wo': _L2_conv_in['Wo'], 'L2_conv_gamma': _L2_conv_in['gamma'], 'L2_conv_beta': _L2_conv_in['beta'], 'L2_conv_Wc': _L2_conv_in['Wc'], 'L2_ffn_router_w': _L2_ffn_in['router_w'], 'L2_ffn_router_b': _L2_ffn_in['router_b'], 'L2_ffn_expert_w': _L2_ffn_in['expert_w'], 'L2_ffn_expert_b': _L2_ffn_in['expert_b'], 'L3_conv_Wk': _L3_conv_in['Wk'], 'L3_conv_bk': _L3_conv_in['bk'], 'L3_conv_Wq': _L3_conv_in['Wq'], 'L3_conv_bq': _L3_conv_in['bq'], 'L3_conv_Wv': _L3_conv_in['Wv'], 'L3_conv_bv': _L3_conv_in['bv'], 'L3_conv_Wu': _L3_conv_in['Wu'], 'L3_conv_bu': _L3_conv_in['bu'], 'L3_conv_pos_enc': _L3_conv_in['pos_enc'], 'L3_ffn_gate_w': _L3_ffn_in['gate_w'], 'L3_ffn_gate_b': _L3_ffn_in['gate_b'], 'L3_ffn_weight1': _L3_ffn_in['weight1'], 'L3_ffn_weight2': _L3_ffn_in['weight2']}

def reference(x, L0_conv_Wq, L0_conv_bq, L0_conv_Wk, L0_conv_bk, L0_conv_Wv, L0_conv_bv, L0_ffn_router_w, L0_ffn_router_b, L0_ffn_expert_w, L0_ffn_expert_b, L1_conv_W, L1_ffn_gate_w, L1_ffn_gate_b, L1_ffn_weight1, L1_ffn_weight2, L2_conv_Wv, L2_conv_bv, L2_conv_Wom, L2_conv_bom, L2_conv_Wo, L2_conv_gamma, L2_conv_beta, L2_conv_Wc, L2_ffn_router_w, L2_ffn_router_b, L2_ffn_expert_w, L2_ffn_expert_b, L3_conv_Wk, L3_conv_bk, L3_conv_Wq, L3_conv_bq, L3_conv_Wv, L3_conv_bv, L3_conv_Wu, L3_conv_bu, L3_conv_pos_enc, L3_ffn_gate_w, L3_ffn_gate_b, L3_ffn_weight1, L3_ffn_weight2):
    import jax
    import jax.numpy as jnp

    def _L0_conv_ref(x, Wq, bq, Wk, bk, Wv, bv):
        import jax, jax.numpy as jnp
        import numpy as np
        K = 7
        PAD = K // 2

        def _unfold(t):
            B, C, H, W = t.shape
            p = jnp.pad(t, ((0, 0), (0, 0), (PAD, PAD), (PAD, PAD)))
            wins = jnp.stack([p[:, :, i:i + H, j:j + W] for i in range(K) for j in range(K)], axis=2)
            return wins
        q = jnp.einsum('oc,bchw->bohw', Wq, x) + bq[:, None, None]
        k = jnp.einsum('oc,bchw->bohw', Wk, x) + bk[:, None, None]
        v = jnp.einsum('oc,bchw->bohw', Wv, x) + bv[:, None, None]
        k_unf = _unfold(k)
        v_unf = _unfold(v)
        attn = jnp.einsum('bchw,bcphw->bphw', q, k_unf)
        attn = jax.nn.softmax(attn, axis=1)
        y = jnp.einsum('bphw,bcphw->bchw', attn, v_unf)
        return y

    def _L0_ffn_ref(x, router_w, router_b, expert_w, expert_b):
        import jax, jax.numpy as jnp
        import numpy as np
        B, N, D, C, E, K = (8, 2048, 32, 32, 8, 2)
        router_probs = jax.nn.softmax(x @ router_w + router_b, axis=-1)
        top_p, top_i = jax.lax.top_k(router_probs, K)
        top_p = top_p / jnp.sum(top_p, axis=-1, keepdims=True)
        expert_out = jnp.einsum('bnd,edc->bnec', x, expert_w) + expert_b
        gathered = jnp.take_along_axis(expert_out, top_i[..., None], axis=2)
        return jnp.einsum('bnk,bnkc->bnc', top_p, gathered)

    def _L1_conv_ref(x, W):
        import jax, jax.numpy as jnp
        import numpy as np
        B, C, H, W_SP = (16, 32, 28, 28)
        F, KS, STRIDE, PAD = (32, 3, 1, 1)
        CHUNK = 4
        EPS = 1e-12

        def _patches(x):
            p = jax.lax.conv_general_dilated_patches(x, (KS, KS), (STRIDE, STRIDE), [(PAD, PAD), (PAD, PAD)], dimension_numbers=('NCHW', 'OIHW', 'NCHW'))
            b, k, ho, wo = p.shape
            return (p.reshape(b, k, ho * wo), ho, wo)
        P, ho, wo = _patches(x)
        Wc = W.reshape(F, -1)
        K = Wc.shape[1]
        Wch = Wc.reshape(F // CHUNK, CHUNK, K)

        def chunk_fn(wc):
            return jnp.sum(jnp.abs(wc[None, :, :, None] - P[:, None, :, :]), axis=2)
        neg_l1 = -jax.lax.map(chunk_fn, Wch)
        neg_l1 = jnp.transpose(neg_l1, (1, 0, 2, 3)).reshape(P.shape[0], F, -1)
        d2 = jnp.sum(Wc * Wc, axis=1)[None, :, None] + jnp.sum(P * P, axis=1)[:, None, :] - 2.0 * jnp.einsum('fk,bkl->bfl', Wc, P)
        neg_l2 = -jnp.sqrt(jnp.maximum(d2, EPS))
        out = neg_l2 + jax.lax.stop_gradient(neg_l1 - neg_l2)
        return out.reshape(P.shape[0], F, ho, wo)

    def _L1_ffn_ref(x, gate_w, gate_b, weight1, weight2):
        import jax, jax.numpy as jnp
        import numpy as np
        B, S, D, E, H, O, K = (128, 512, 32, 16, 128, 32, 8)
        Bn, Sn, Dn = x.shape
        logits = jnp.einsum('bsd,ed->bse', x, gate_w) + gate_b
        probs = jax.nn.softmax(logits, axis=1)
        vals, idx = jax.lax.top_k(probs.transpose(0, 2, 1), K)
        topv = vals.transpose(0, 2, 1)
        topi = idx.transpose(0, 2, 1)
        flat_idx = topi.reshape(Bn, K * E)
        gathered = jnp.take_along_axis(x, flat_idx[:, :, None], axis=1)
        gathered = gathered.reshape(Bn, K, E, Dn)
        pooled = jnp.einsum('bked,bke->bed', gathered, topv)
        ones = jnp.ones((E, Bn, 1), dtype=x.dtype)
        h = jnp.concatenate([pooled.transpose(1, 0, 2), ones], axis=-1)
        h = jax.nn.gelu(jnp.einsum('ebd,edh->ebh', h, weight1), approximate=False)
        h = jnp.concatenate([h, ones], axis=-1)
        out = jnp.einsum('ebh,eho->ebo', h, weight2)
        out = out.transpose(1, 0, 2)
        weighted = jnp.einsum('beo,bke->bkeo', out, topv).reshape(Bn, K * E, O)
        outputs = jnp.zeros((Bn, Sn, O), dtype=x.dtype)
        outputs = outputs.at[jnp.arange(Bn)[:, None], flat_idx].add(weighted)
        return outputs

    def _L2_conv_ref(x, Wv, bv, Wom, bom, Wo, gamma, beta, Wc):
        import jax, jax.numpy as jnp
        import numpy as np
        G = 4
        K = 9
        EPS = 1e-05

        def _bilinear_gather(value, loc_y, loc_x):
            N, H, W, g, Cg = value.shape
            y0f = jnp.floor(loc_y)
            x0f = jnp.floor(loc_x)
            wy = loc_y - y0f
            wx = loc_x - x0f
            y0 = y0f.astype(jnp.int32)
            x0 = x0f.astype(jnp.int32)
            n_idx = jnp.arange(N).reshape(N, 1, 1, 1, 1)
            g_idx = jnp.arange(g).reshape(1, 1, 1, g, 1)

            def corner(yi, xi, w):
                valid = (yi >= 0) & (yi < H) & (xi >= 0) & (xi < W)
                yc = jnp.clip(yi, 0, H - 1)
                xc = jnp.clip(xi, 0, W - 1)
                v = value[n_idx, yc, xc, g_idx]
                return v * (w * valid)[..., None]
            return corner(y0, x0, (1 - wy) * (1 - wx)) + corner(y0, x0 + 1, (1 - wy) * wx) + corner(y0 + 1, x0, wy * (1 - wx)) + corner(y0 + 1, x0 + 1, wy * wx)

        def _dcnv4(t, H, W, Wv, bv, Wom, bom, Wo):
            N, L, C = t.shape
            Cg = C // G
            value = (t @ Wv + bv).reshape(N, H, W, G, Cg)
            om = (t @ Wom + bom).reshape(N, H, W, G, 3 * K)
            offset = om[..., :2 * K].reshape(N, H, W, G, K, 2)
            mask = om[..., 2 * K:]
            ky, kx = jnp.meshgrid(jnp.arange(-1, 2), jnp.arange(-1, 2), indexing='ij')
            ky = ky.reshape(-1).astype(t.dtype)
            kx = kx.reshape(-1).astype(t.dtype)
            ys = jnp.arange(H, dtype=t.dtype).reshape(1, H, 1, 1, 1)
            xs = jnp.arange(W, dtype=t.dtype).reshape(1, 1, W, 1, 1)
            loc_y = ys + ky + offset[..., 1]
            loc_x = xs + kx + offset[..., 0]
            sampled = _bilinear_gather(value, loc_y, loc_x)
            out = (sampled * mask[..., None]).sum(axis=4)
            return out.reshape(N, L, C) @ Wo

        def _bn(x, gamma, beta):
            mean = x.mean(axis=(0, 2, 3), keepdims=True)
            var = ((x - mean) ** 2).mean(axis=(0, 2, 3), keepdims=True)
            return (x - mean) * jax.lax.rsqrt(var + EPS) * gamma.reshape(1, -1, 1, 1) + beta.reshape(1, -1, 1, 1)
        N, C, H, W = x.shape
        shortcut = x
        t = x.transpose(0, 2, 3, 1).reshape(N, H * W, C)
        t = _dcnv4(t, H, W, Wv, bv, Wom, bom, Wo)
        y = t.reshape(N, H, W, C).transpose(0, 3, 1, 2)
        y = jax.nn.relu(_bn(y, gamma, beta))
        t = y.transpose(0, 2, 3, 1).reshape(N, H * W, C)
        t = _dcnv4(t, H, W, Wv, bv, Wom, bom, Wo)
        y = t.reshape(N, H, W, C).transpose(0, 3, 1, 2)
        y = _bn(y, gamma, beta)
        y = y + shortcut
        return jnp.einsum('nchw,oc->nohw', y, Wc)

    def _L2_ffn_ref(x, router_w, router_b, expert_w, expert_b):
        import jax, jax.numpy as jnp
        import numpy as np
        B, N, D, C, E, K = (8, 2048, 32, 32, 8, 2)
        router_probs = jax.nn.softmax(x @ router_w + router_b, axis=-1)
        top_p, top_i = jax.lax.top_k(router_probs, K)
        top_p = top_p / jnp.sum(top_p, axis=-1, keepdims=True)
        expert_out = jnp.einsum('bnd,edc->bnec', x, expert_w) + expert_b
        gathered = jnp.take_along_axis(expert_out, top_i[..., None], axis=2)
        return jnp.einsum('bnk,bnkc->bnc', top_p, gathered)

    def _L3_conv_ref(x, Wk, bk, Wq, bq, Wv, bv, Wu, bu, pos_enc):
        import jax, jax.numpy as jnp
        import numpy as np
        B, E, H, NY, NX = (16, 32, 4, 32, 32)

        def _conv1x1(x, W, b):
            return jnp.einsum('bcyx,oc->boyx', x, W) + b[None, :, None, None]

        def _rel_indices(ny, nx):
            y = jnp.arange(ny)
            x = jnp.arange(nx)
            y1, x1, y2, x2 = jnp.meshgrid(y, x, y, x, indexing='ij')
            idx = (y1 - y2 + ny - 1) * (2 * nx - 1) + (x1 - x2 + nx - 1)
            return idx.reshape(ny * nx, ny * nx)
        b, e, ny, nx = x.shape
        h = pos_enc.shape[0]
        hc = e // h
        n = ny * nx
        scale = hc ** (-0.5)
        keys = _conv1x1(x, Wk, bk).reshape(b, h, hc, n)
        queries = _conv1x1(x, Wq, bq).reshape(b, h, hc, n)
        values = _conv1x1(x, Wv, bv).reshape(b, h, hc, n)
        att = jnp.einsum('bhck,bhcq->bhkq', keys, queries) * scale
        idx = _rel_indices(ny, nx)
        rel = pos_enc[:, idx]
        att = att + rel[None]
        att = jax.nn.softmax(att, axis=-2)
        out = jnp.einsum('bhck,bhkq->bhcq', values, att).reshape(b, e, ny, nx)
        return _conv1x1(out, Wu, bu)

    def _L3_ffn_ref(x, gate_w, gate_b, weight1, weight2):
        import jax, jax.numpy as jnp
        import numpy as np
        B, S, D, E, H, O, K = (128, 512, 32, 16, 128, 32, 8)
        Bn, Sn, Dn = x.shape
        logits = jnp.einsum('bsd,ed->bse', x, gate_w) + gate_b
        probs = jax.nn.softmax(logits, axis=1)
        vals, idx = jax.lax.top_k(probs.transpose(0, 2, 1), K)
        topv = vals.transpose(0, 2, 1)
        topi = idx.transpose(0, 2, 1)
        flat_idx = topi.reshape(Bn, K * E)
        gathered = jnp.take_along_axis(x, flat_idx[:, :, None], axis=1)
        gathered = gathered.reshape(Bn, K, E, Dn)
        pooled = jnp.einsum('bked,bke->bed', gathered, topv)
        ones = jnp.ones((E, Bn, 1), dtype=x.dtype)
        h = jnp.concatenate([pooled.transpose(1, 0, 2), ones], axis=-1)
        h = jax.nn.gelu(jnp.einsum('ebd,edh->ebh', h, weight1), approximate=False)
        h = jnp.concatenate([h, ones], axis=-1)
        out = jnp.einsum('ebh,eho->ebo', h, weight2)
        out = out.transpose(1, 0, 2)
        weighted = jnp.einsum('beo,bke->bkeo', out, topv).reshape(Bn, K * E, O)
        outputs = jnp.zeros((Bn, Sn, O), dtype=x.dtype)
        outputs = outputs.at[jnp.arange(Bn)[:, None], flat_idx].add(weighted)
        return outputs

    def _gn(v, G=32, eps=1e-05):
        B_, C_, H_, W_ = v.shape
        g = v.reshape(B_, G, C_ // G, H_, W_)
        m = jnp.mean(g, axis=(2, 3, 4), keepdims=True)
        s = jnp.var(g, axis=(2, 3, 4), keepdims=True)
        return ((g - m) / jnp.sqrt(s + eps)).reshape(v.shape)

    def _ln_c(v, eps=1e-06):
        m = jnp.mean(v, axis=1, keepdims=True)
        s = jnp.var(v, axis=1, keepdims=True)
        return (v - m) / jnp.sqrt(s + eps)

    def _ln_t(v, eps=1e-05):
        m = jnp.mean(v, axis=-1, keepdims=True)
        s = jnp.var(v, axis=-1, keepdims=True)
        return (v - m) / jnp.sqrt(s + eps)

    def _to_tokens(v):
        B_, C_, H_, W_ = v.shape
        return v.reshape(B_, C_, H_ * W_).transpose(0, 2, 1)

    def _from_tokens(t, like):
        B_, C_, H_, W_ = like.shape
        return t.transpose(0, 2, 1).reshape(B_, C_, H_, W_)
    x = x + _L0_conv_ref(_ln_c(x), L0_conv_Wq, L0_conv_bq, L0_conv_Wk, L0_conv_bk, L0_conv_Wv, L0_conv_bv)
    t = _to_tokens(x)
    t = t + _L0_ffn_ref(_ln_t(t), L0_ffn_router_w, L0_ffn_router_b, L0_ffn_expert_w, L0_ffn_expert_b)
    x = _from_tokens(t, x)
    x = x + _L1_conv_ref(_ln_c(x), L1_conv_W)
    t = _to_tokens(x)
    t = t + _L1_ffn_ref(_ln_t(t), L1_ffn_gate_w, L1_ffn_gate_b, L1_ffn_weight1, L1_ffn_weight2)
    x = _from_tokens(t, x)
    x = x + _L2_conv_ref(_ln_c(x), L2_conv_Wv, L2_conv_bv, L2_conv_Wom, L2_conv_bom, L2_conv_Wo, L2_conv_gamma, L2_conv_beta, L2_conv_Wc)
    t = _to_tokens(x)
    t = t + _L2_ffn_ref(_ln_t(t), L2_ffn_router_w, L2_ffn_router_b, L2_ffn_expert_w, L2_ffn_expert_b)
    x = _from_tokens(t, x)
    x = x + _L3_conv_ref(_ln_c(x), L3_conv_Wk, L3_conv_bk, L3_conv_Wq, L3_conv_bq, L3_conv_Wv, L3_conv_bv, L3_conv_Wu, L3_conv_bu, L3_conv_pos_enc)
    t = _to_tokens(x)
    t = t + _L3_ffn_ref(_ln_t(t), L3_ffn_gate_w, L3_ffn_gate_b, L3_ffn_weight1, L3_ffn_weight2)
    x = _from_tokens(t, x)
    return x

_drawn_inputs = setup_inputs


def setup_inputs(seed=0):
    import zlib

    import numpy as np

    out = dict(_drawn_inputs(seed))
    spreads = {'L0_ffn_router_b': (0.0, 0.8),
     'L0_ffn_expert_b': (0.0, 2.0),
     'L1_ffn_gate_b': (0.0, 2.0),
     'L2_conv_bv': (0.0, 2.0),
     'L2_conv_bom': (0.0, 0.8),
     'L2_conv_gamma': (1.0, 0.6),
     'L2_conv_beta': (0.0, 0.8),
     'L2_ffn_router_b': (0.0, 2.0),
     'L2_ffn_expert_b': (0.0, 2.0),
     'L3_conv_bk': (0.0, 2.0),
     'L3_conv_bq': (0.0, 2.0),
     'L3_conv_bv': (0.0, 2.0),
     'L3_conv_bu': (0.0, 2.0),
     'L3_ffn_gate_b': (0.0, 2.0)}
    factors = {'x': 2.809,
     'L0_conv_Wq': 3.363,
     'L0_conv_bq': 24.326,
     'L0_conv_Wk': 3.317,
     'L0_conv_bk': 200.0,
     'L0_conv_Wv': 3.252,
     'L0_conv_bv': 39.815,
     'L0_ffn_router_w': 4.153,
     'L0_ffn_expert_w': 3.59,
     'L1_conv_W': 6.736,
     'L1_ffn_gate_w': 8.0,
     'L1_ffn_weight1': 23.279,
     'L1_ffn_weight2': 8.0,
     'L2_conv_Wv': 8.0,
     'L2_conv_Wom': 8.0,
     'L2_conv_Wo': 8.0,
     'L2_conv_Wc': 7.621,
     'L2_ffn_router_w': 8.0,
     'L2_ffn_expert_w': 8.0,
     'L3_conv_Wk': 64.0,
     'L3_conv_Wq': 64.0,
     'L3_conv_Wv': 64.0,
     'L3_conv_Wu': 64.0,
     'L3_conv_pos_enc': 64.0,
     'L3_ffn_gate_w': 45.201,
     'L3_ffn_weight1': 56.46,
     'L3_ffn_weight2': 49.207}
    for name, (base, spread) in spreads.items():
        noise = np.random.default_rng([zlib.crc32(name.encode()), seed]).standard_normal(out[name].shape)
        drawn = base * np.exp(spread * noise) if base else spread * noise
        out[name] = jnp.asarray(drawn.astype(out[name].dtype))
    for name, factor in factors.items():
        out[name] = (out[name] * factor).astype(out[name].dtype)
    return out
```

```python
import concourse.bass as bass
from concourse import mybir
from contextlib import ExitStack

B, C, HH, WW = 8, 32, 16, 16
NPIX = HH * WW
P = 128
B4 = P // C
NBH = B // B4
NT = B * NPIX // P
F = NT * C
E8 = 8
E16, HID = 16, 128
HEADS, HC = 4, 8
G, CG, K9 = 4, 8, 9
NA, NR = 2, 9
PADW = HH + 2
KG = K9 * G
HXN, HYN = KG * NA * WW, KG * NR
HATS = HXN + HYN
BIG = 1e30
NEG = -3e38
LOOK = 6

UNITS = 9 * 4
DVE_UNITS = 22
ACT_UNITS = UNITS - DVE_UNITS
ON_DVE = [(n + 1) * DVE_UNITS // UNITS > n * DVE_UNITS // UNITS for n in range(UNITS)]
DRING, ARING = DVE_UNITS // 2, ACT_UNITS // 2


def columns(spec):
    at, out = 0, {}
    for name, n in spec:
        out[name] = at
        at += n
    return out, at


CST_SPEC = [("ident", 128), ("mask", 512), ("floor", 2), ("npad", 2), ("top", 2), ("one", 1),
            ("eps6", 1), ("eps5", 1), ("hm", HEADS), ("ones", 512), ("geo", 2 * 3 * KG), ("xg", WW), ("yg", NR),
            ("gmask", 128), ("rep1", 32), ("rep2", 32), ("nrep", 32), ("nhalf", 128), ("avg", 128),
            ("ecmask", B), ("sel", 8), ("keys", E8), ("dtaps", 9)]
CST, NCST = columns(CST_SPEC)
WA_SPEC = [("q0", 128), ("k0", 128), ("v0", 128), ("bq0", 1), ("bk0", 1), ("bv0", 32)]
WA, NWA = columns(WA_SPEC)
WB_SPEC = [("r0", 32), ("rb0", E8), ("ew0", 256), ("eb0", 512),
           ("lw", 288), ("wf", 288), ("w9", 9 * 128),
           ("gw0", 256), ("gb0", 1), ("w10", E16 * HID), ("w20", E16 * C), ("b20", E16)]
WB, NWB = columns(WB_SPEC)
WC_SPEC = [("om", B4 * 3 * KG), ("bom", 3 * KG), ("val", 128), ("bval", 512), ("wo", 128),
           ("gamma", 1), ("beta", 1), ("wc", 128),
           ("r1", 32), ("rb1", E8), ("ew1", 256), ("eb1", 512)]
WC, NWC = columns(WC_SPEC)
WD_SPEC = [("q1", 128), ("k1", 128), ("v1", 128), ("bq1", 1), ("bk1", 1), ("bv1", 32), ("u1", 128),
           ("bu1", 32), ("rel", 2 * HEADS * NPIX),
           ("gw1", 256), ("gb1", 1), ("w11", E16 * HID), ("w21", E16 * C), ("b21", E16)]
WD, NWD = columns(WD_SPEC)


def metaformer(nc, x_in, cst_in, wa_in, wb_in, wc_in, wd_in, out):
    fp32 = mybir.dt.float32
    ALU, ACT, AX = mybir.AluOpType, mybir.ActivationFunctionType, mybir.AxisListType

    with ExitStack() as ctx:
        widths = {}

        def sb(name, cols, parts=P):
            t = ctx.enter_context(nc.sbuf_tensor(name, [parts, cols], fp32))
            widths[name] = cols
            return t

        def view(t, col, dims, p0=0, n=P):
            if isinstance(t, tuple):
                t, first = t
                col = first + col
            w = t.shape[1]
            return bass.AP(t, p0 * w + col, [[w, n]] + [list(d) for d in dims])

        sem = lambda name: ctx.enter_context(nc.semaphore(name))

        XT, XN, XNC, YC = sb("XT", F), sb("XN", F), sb("XNC", F), sb("YC", F)
        SQ = sb("SQ", F)
        XC = sb("XC", F)
        cst, wa, wb, wc, wd = sb("cst", NCST), sb("wa", NWA), sb("wb", NWB), sb("wc", NWC), sb("wd", NWD)
        s16, mean, var, sd, rstd = (sb(n, NT) for n in ("s16", "mean", "var", "sd", "rstd"))
        QC, KC, VT = sb("QC", HEADS * F), sb("KC", F), sb("VT", F)
        SM = sb("SM", 2 * 512)
        PTS = sb("PTS", 2 * 512)
        mx, nm, rs, den, e0 = (sb(n, 64) for n in ("mx", "nm", "rs", "den", "e0"))
        bqh = sb("bqh", HEADS)
        LG, EX, KEY, S1, S2, GW = (sb(n, NT * E8) for n in ("LG", "EX", "KEY", "S1", "S2", "GW"))
        PR = sb("PR", 2 * 512)
        Y2 = sb("Y2", F)
        XP, SQP = sb("XP", NBH * PADW * PADW), sb("SQP", NBH * PADW * PADW)
        RINGS = sb("RINGS", (DRING + ARING) * F)
        ACC, D2 = sb("ACC", F), sb("D2", F)
        w2s, wsd = sb("w2s", 1), sb("wsd", 1)
        PB, MK, GX = sb("PB", NPIX), sb("MK", NPIX), sb("GX", NPIX)
        top8 = sb("top8", 8)
        GT = sb("GT", NPIX)
        PA = sb("PA", P, C + 1)
        HB = sb("HB", P)
        OC = sb("OC", P, C)
        OB = sb("OB", B * C)
        c1, c2 = sb("c1", 4), sb("c2", 4)
        base = sb("base", 2 * 3 * KG)
        OM = sb("OM", NT * 3 * KG)
        AM = sb("AM", NT * KG)
        LXA = sb("LXA", NT * KG * NA)
        VB = sb("VB", B * G * CG * NR)
        DXY, HXY, HXT = (RINGS, 0), (RINGS, 2 * HATS), (RINGS, 4 * HATS)
        HYM = sb("HYM", HYN)
        PRD = sb("PRD", K9 * 288)
        SMP, SMT = sb("SMP", F), sb("SMT", F)
        XW = sb("XW", NBH * NR * P)

        bank = [ctx.enter_context(nc.psum_tensor(f"bank{i}", [P, 512], fp32)) for i in range(8)]

        def cv(name, n, c=0, p0=0, np_=P):
            return cst[p0:p0 + np_, CST[name] + c:CST[name] + c + n]

        ident = cv("ident", 128)

        x_in_s, cst_s, wa_s, wb_s, wc_s, wd_s, out_s = (
            sem(n) for n in ("x_loaded", "cst_loaded", "wa_loaded", "wb_loaded", "wc_loaded", "wd_loaded", "stored"))
        dve_chain, pool_set = sem("dve_chain"), sem("pool_set")
        x_turned, x_ready = sem("x_turned"), sem("x_ready")
        var_ready, sd_ready, xn_ready, xn_turned, xnc_ready = (
            sem(n) for n in ("var_ready", "sd_ready", "xn_ready", "xn_turned", "xnc_ready"))
        q_done, kv_done, qc_ready, kv_ready, bqh_ready = (
            sem(n) for n in ("q_done", "kv_done", "qc_ready", "kv_ready", "bqh_ready"))
        scored, nm_ready, p_ready, pt_done, pts_ready, av_done = (
            sem(n) for n in ("scored", "nm_ready", "p_ready", "pt_done", "pts_ready", "av_done"))
        pad_asked, pad_ready = sem("pad_asked"), sem("pad_ready")
        att_ready, att_turned, attc_ready, u_done = (
            sem(n) for n in ("att_ready", "att_turned", "attc_ready", "u_done"))
        routed, gate_ready, ex_ready, expert_done, expert_used = (
            sem(n) for n in ("routed", "gate_ready", "ex_ready", "expert_done", "expert_used"))
        xp_ready, sqp_ready, cor_done, cor_used, l2_done, d2_ready, l2_ready, lo_ready, lo_turned = (
            sem(n) for n in ("xp_ready", "sqp_ready", "cor_done", "cor_used", "l2_done", "d2_ready", "l2_ready",
                             "lo_ready", "lo_turned"))
        d_ready, d_used, a_ready, a_used, drained = (
            sem(n) for n in ("d_ready", "d_used", "a_ready", "a_used", "drained"))
        ec_logits, ec_max, ec_exp, g_ready, g_turned, gt_ready, pooled, pa_ready = (
            sem(n) for n in ("ec_logits", "ec_max", "ec_exp", "g_ready", "g_turned", "gt_ready", "pooled", "pa_ready"))
        h_done, h_ready, o_done, oc_ready, oc_turned, ob_ready, ec_out = (
            sem(n) for n in ("h_done", "h_ready", "o_done", "oc_ready", "oc_turned", "ob_ready", "ec_out"))
        om_done, om_used, val_done, val_used, lxa_ready, xw_ready, smt_ready = (
            sem(n) for n in ("om_done", "om_used", "val_done", "val_used", "lxa_ready", "xw_ready", "smt_ready"))
        dxy_ready, abs_done, hxy_ready, hym_ready, hx_turned, hxt_ready, prod_done, prod_used = (
            sem(n) for n in ("dxy_ready", "abs_done", "hxy_ready", "hym_ready", "hx_turned", "hxt_ready", "prod_done",
                             "prod_used"))
        smp_ready, smp_turned, sc_ready, y_done, sum_ready, sum_done, cen_ready, sq_ready, sq_done, bn_ready, dc_ready = (
            sem(n) for n in ("smp_ready", "smp_turned", "sc_ready", "y_done", "sum_ready", "sum_done", "cen_ready",
                             "sq_ready", "sq_done", "bn_ready", "dc_ready"))
        bnv_ready, bsd_ready, yc_ready, wc_done = (sem(n) for n in ("bnv_ready", "bsd_ready", "yc_ready", "wc_done"))
        fin_turned, fin_ready = sem("fin_turned"), sem("fin_ready")

        block = ctx.enter_context(nc.Block())

        def after(eng, s, value):
            if not isinstance(value, int) or value > 0:
                eng.wait_ge(s, value)

        @block.sync
        def _(sp):
            for bh in range(NBH):
                sp.dma_start(XC[:, bh * NPIX:(bh + 1) * NPIX],
                             x_in[bh * B4:(bh + 1) * B4].rearrange("b c y x -> (b c) (y x)")).then_inc(x_in_s, 16)
            sp.dma_start(cst[:, :], cst_in).then_inc(cst_s, 16)
            sp.dma_start(wa[:, :], wa_in).then_inc(wa_s, 16)
            sp.dma_start(wb[:, :], wb_in).then_inc(wb_s, 16)
            sp.dma_start(wc[:, :], wc_in).then_inc(wc_s, 16)
            sp.dma_start(wd[:, :], wd_in).then_inc(wd_s, 16)
            sp.wait_ge(fin_ready, 1)
            for bh in range(NBH):
                sp.dma_start(out[bh * B4:(bh + 1) * B4].rearrange("b c y x -> (b c) (y x)"),
                             XC[:, bh * NPIX:(bh + 1) * NPIX]).then_inc(out_s, 16)
            sp.wait_ge(out_s, 16 * NBH)

        @block.gpsimd
        def _(pool):
            pool.memset(XP[:, :], 0.0).then_inc(pool_set, 1)
            pool.memset(SQP[:, :], 0.0).then_inc(pool_set, 1)
            pool.wait_ge(pool_set, 2)
            pool.memset(PA[C:C + 1, :], 1.0).then_inc(pool_set, 1)

            def distances(turn, b, half):
                n = 2 * b + half
                after(pool, hxy_ready, 16 * turn + n - 1)
                o = half * HATS
                pool.tensor_tensor(view(DXY, o, [[WW, KG * NA], [1, WW]]),
                                   view(LXA, n * KG * NA, [[1, KG * NA], [0, WW]]),
                                   view(cst, CST["xg"], [[0, KG * NA], [1, WW]]), ALU.subtract)
                pool.tensor_tensor(view(DXY, o + HXN, [[NR, KG], [1, NR]]),
                                   view(OM, n * 3 * KG + KG, [[1, KG], [0, NR]]),
                                   view(cst, CST["yg"], [[0, KG], [1, NR]]), ALU.subtract).then_inc(dxy_ready, 1)

            for turn in range(2):
                pool.wait_ge(lxa_ready, turn + 1)
                for half in range(2):
                    distances(turn, 0, half)
                with pool.Fori(1, B) as b:
                    for half in range(2):
                        distances(turn, b, half)

        @block.scalar
        def _(act):
            def norm(n, eps, padded=False):
                act.wait_ge(var_ready, n + 1)
                act.activation(sd[:, :], var[:, :], ACT.Sqrt, scale=1.0 / C, bias=cv(eps, 1)).then_inc(sd_ready, 1)
                act.wait_ge(xn_turned, n + 1)
                if not padded:
                    act.activation(XNC[:, :], bank[0][:, :], ACT.Copy).then_inc(xnc_ready, 1)
                    return
                act.wait_ge(pool_set, 3)
                for bh in range(NBH):
                    ins = act.activation(view(XP, bh * PADW * PADW + PADW + 1, [[PADW, HH], [1, WW]]),
                                         view(bank[0], bh * NPIX, [[WW, HH], [1, WW]]), ACT.Copy)
                ins.then_inc(xp_ready, 1)
                for bh in range(NBH):
                    ins = act.activation(view(SQP, bh * PADW * PADW + PADW + 1, [[PADW, HH], [1, WW]]),
                                         view(bank[0], bh * NPIX, [[WW, HH], [1, WW]]), ACT.Square)
                ins.then_inc(sqp_ready, 1)
                ins = None

            def attend(first, steps):
                for s in range(first, first + steps):
                    act.wait_ge(nm_ready, s + 1)
                    for j in range(2):
                        u = 2 * (s - first) + j
                        at = (s % 2) * 512 + j * 256
                        ins = act.activation(SM[:, at:at + 256], SM[:, at:at + 256], ACT.Exp,
                                             bias=nm[:, u:u + 1], accum_out=rs[:, u:u + 1])
                    ins.then_inc(p_ready, 1)

            def top2(turn):
                act.wait_ge(gate_ready, turn + 1)
                act.activation(EX[:, :], LG[:, :], ACT.Exp).then_inc(ex_ready, 1)

            def expert_choice(turn):
                act.wait_ge(ec_max, turn + 1)
                act.activation(PB[:, :], MK[:, :], ACT.Exp, bias=nm[:, 0:1], accum_out=rs[:, 0:1]).then_inc(ec_exp, 1)
                act.wait_ge(g_turned, turn + 1)
                act.activation(GT[:, :], bank[2][:, 0:NPIX], ACT.Copy).then_inc(gt_ready, 1)
                act.wait_ge(pooled, turn + 1)
                act.activation(PA[0:C, :], bank[3][0:C, 0:P], ACT.Copy).then_inc(pa_ready, 1)
                act.wait_ge(h_done, turn + 1)
                act.activation(HB[:, :], bank[4][:, 0:P], ACT.Gelu).then_inc(h_ready, 1)

            norm(0, "eps6")
            act.wait_ge(wa_s, 16)
            act.wait_ge(q_done, 1)
            act.activation(QC[:, 0:F], bank[1][:, :], ACT.Identity, bias=wa[:, WA["bq0"]:WA["bq0"] + 1]).then_inc(qc_ready, 1)
            attend(0, 8)
            act.wait_ge(pad_asked, 1)
            act.activation(e0[:, 0:NT], den[:, 0:NT], ACT.Exp).then_inc(pad_ready, 1)
            norm(1, "eps5")
            top2(0)

            norm(2, "eps6", padded=True)
            act.wait_ge(wb_s, 16)
            act.wait_ge(xp_ready, 1)

            def distances(i):
                k = 0
                for n in range(UNITS):
                    if ON_DVE[n]:
                        continue
                    tap, j = divmod(n, 4)
                    after(act, a_used, ACT_UNITS * i + k + 1 - ARING)
                    slot = (DRING + k % ARING) * F
                    w_at = WB["lw"] + i * UNITS + n
                    act.activation(view(RINGS, slot, [[NPIX, NBH], [WW, HH], [1, WW]]),
                                   view(XP, tap // 3 * PADW + tap % 3, [[PADW * PADW, NBH], [PADW, HH], [1, WW]]),
                                   ACT.Abs, scale=-1.0, bias=view(wb, w_at, [[1, 1]])).then_inc(a_ready, 1)
                    k += 1

            distances(0)
            with act.Fori(1, 8) as i:
                distances(i)
            act.wait_ge(d2_ready, 1)
            act.activation(D2[:, :], D2[:, :], ACT.Sqrt).then_inc(l2_ready, 1)
            norm(3, "eps5")
            expert_choice(0)

            norm(4, "eps6")

            def hats(turn, b, half):
                n = 2 * b + half
                o = half * HATS
                act.wait_ge(dxy_ready, 16 * turn + n + 1)
                act.activation(view(DXY, o, [[1, HATS]]), view(DXY, o, [[1, HATS]]), ACT.Abs).then_inc(abs_done, 1)
                act.wait_ge(abs_done, 16 * turn + n + 1)
                after(act, hx_turned, 3 * (16 * turn + n - 1))
                after(act, hym_ready, 16 * turn + n - 1)
                act.activation(view(HXY, o, [[1, HATS]]), view(DXY, o, [[1, HATS]]), ACT.Relu, scale=-1.0,
                               bias=cv("one", 1)).then_inc(hxy_ready, 1)

            def turned(turn, b, half):
                n = 2 * b + half
                after(act, prod_done, 9 * (16 * turn + n - 1))
                for g in range(3):
                    act.wait_ge(hx_turned, 3 * (16 * turn + n) + g + 1)
                    o = (half * K9 + 3 * g) * P
                    act.activation(view(HXT, o, [[1, 3 * P]]), bank[(3 * half + g) % 2][:, 0:3 * P], ACT.Copy).then_inc(hxt_ready, 1)

            def deform(turn, src, src_ready, count):
                act.wait_ge(src_ready, count)
                after(act, val_done, 6 * turn)
                for bh in range(NBH):
                    for g in range(G):
                        ins = act.activation(view(XW, bh * NR * P + g * NA * WW, [[P, NR], [WW, NA], [1, WW]]),
                                             view(src, bh * NPIX, [[WW, NR], [7 * WW, NA], [1, WW]]), ACT.Copy)
                ins.then_inc(xw_ready, 1)
                hats(turn, 0, 0)
                hats(turn, 0, 1)

                def body(b):
                    for half in range(2):
                        turned(turn, b, half)
                        hats(turn, b + 1, half)
                body(0)
                with act.Fori(1, B - 1) as b:
                    body(b)
                for half in range(2):
                    turned(turn, B - 1, half)
                act.wait_ge(smp_turned, turn + 1)
                act.activation(YC[:, :], bank[0][:, :], ACT.Copy).then_inc(sc_ready, 1)
                act.wait_ge(cen_ready, turn + 1)
                act.activation(D2[:, :], ACC[:, :], ACT.Square, accum_out=c2[:, 0:1]).then_inc(sq_ready, 1)
                act.wait_ge(bnv_ready, turn + 1)
                act.activation(c2[:, 1:2], c2[:, 2:3], ACT.Sqrt).then_inc(bsd_ready, 1)
                act.wait_ge(bn_ready, turn + 1)
                if turn == 0:
                    act.activation(YC[:, :], ACC[:, :], ACT.Relu, scale=c1[:, 2:3],
                                   bias=wc[:, WC["beta"]:WC["beta"] + 1]).then_inc(dc_ready, 1)

            act.wait_ge(wc_s, 16)
            deform(0, XNC, xnc_ready, 4)
            deform(1, YC, dc_ready, 1)
            norm(5, "eps5")
            top2(1)

            norm(6, "eps6")
            act.wait_ge(q_done, 2)
            act.wait_ge(bqh_ready, 1)
            for h in range(HEADS):
                ins = act.activation(QC[:, h * F:(h + 1) * F], bank[1][:, :], ACT.Identity, scale=cv("hm", 1, h),
                                     bias=bqh[:, h:h + 1])
            ins.then_inc(qc_ready, 1)
            attend(8, 32)
            act.wait_ge(att_turned, 1)
            act.activation(YC[:, :], bank[0][:, :], ACT.Copy).then_inc(attc_ready, 1)
            norm(7, "eps5")
            expert_choice(1)

        @block.vector
        def _(dve):
            links = [0]

            def link(ins):
                links[0] += 1
                ins.then_inc(dve_chain, 1)
                dve.wait_ge(dve_chain, links[0])

            def tiles(t, col=0):
                return view(t, col, [[C, NT], [1, C]])

            def per_tile(t):
                return view(t, 0, [[1, NT], [0, C]])

            def norm(n):
                link(dve.tensor_reduce(s16[:, :], tiles(XT), AX.X, ALU.add))
                link(dve.tensor_scalar(mean[:, :], s16[:, :], 1.0 / C, None, ALU.mult))
                link(dve.tensor_tensor(tiles(XN), tiles(XT), per_tile(mean), ALU.subtract))
                link(dve.tensor_tensor(SQ[:, :], XN[:, :], XN[:, :], ALU.mult))
                dve.tensor_reduce(var[:, :], tiles(SQ), AX.X, ALU.add).then_inc(var_ready, 1)
                dve.wait_ge(sd_ready, n + 1)
                link(dve.reciprocal(rstd[:, :], sd[:, :]))
                dve.tensor_tensor(tiles(XN), tiles(XN), per_tile(rstd), ALU.mult).then_inc(xn_ready, 1)
                dve.wait_ge(xn_ready, n + 1)

            def attend(first, steps, l3):
                for s in range(first, first + steps + 1):
                    if s < first + steps:
                        r = s - first
                        dve.wait_ge(scored, s + 1)
                        after(dve, pt_done, s - 1)
                        for j in range(2):
                            u = 2 * r + j
                            half = u // (B4 * HEADS) % 2 if l3 else j
                            at = (s % 2) * 512 + j * 256
                            if l3:
                                add = wd[:, WD["rel"] + (half * HEADS + u % HEADS) * NPIX:][:, 0:NPIX]
                            else:
                                add = cv("mask", NPIX, half * NPIX)
                            ins = dve.tensor_tensor_reduce(SM[:, at:at + 256], bank[4 + s % 2][:, j * 256:j * 256 + 256],
                                                           add, 1.0, NEG, ALU.add, ALU.max, mx[:, u:u + 1])
                        link(ins)
                        dve.scalar_tensor_tensor(nm[:, 2 * r:2 * r + 2], mx[:, 2 * r:2 * r + 2], -1.0,
                                                 cv("top" if l3 else "floor", 2), ALU.mult, ALU.min).then_inc(nm_ready, 1)
                    if s > first:
                        dve.wait_ge(pt_done, s)
                        after(dve, av_done, s - 2)
                        dve.tensor_copy(PTS[:, ((s - 1) % 2) * 512:((s - 1) % 2) * 512 + 512],
                                        bank[6 + (s - 1) % 2][:, :]).then_inc(pts_ready, 1)

            def top2(turn, rb, w):
                by_e = lambda t: view(t, 0, [[E8, NT], [1, E8]])
                one = lambda t: view(t, 0, [[1, NT], [0, E8]])
                keys = view(cst, CST["keys"], [[0, NT], [1, E8]])
                dve.wait_ge(routed, turn + 1)
                link(dve.tensor_tensor(by_e(LG), view(bank[1], 0, [[E8, NT], [1, E8]]),
                                       view(w, rb, [[0, NT], [1, E8]]), ALU.add))
                link(dve.tensor_reduce(s16[:, :], by_e(LG), AX.X, ALU.max))
                dve.tensor_tensor(by_e(LG), by_e(LG), one(s16), ALU.subtract).then_inc(gate_ready, 1)
                dve.wait_ge(gate_ready, turn + 1)
                link(dve.scalar_tensor_tensor(by_e(KEY), by_e(LG), 0.0, keys, ALU.is_ge, ALU.mult))
                link(dve.tensor_reduce(s16[:, :], by_e(KEY), AX.X, ALU.max))
                link(dve.tensor_tensor(by_e(S1), by_e(KEY), one(s16), ALU.is_equal))
                link(dve.scalar_tensor_tensor(by_e(KEY), by_e(S1), -BIG, by_e(LG), ALU.mult, ALU.add))
                link(dve.tensor_reduce(s16[:, :], by_e(KEY), AX.X, ALU.max))
                link(dve.tensor_tensor(by_e(S2), by_e(KEY), one(s16), ALU.is_equal))
                link(dve.tensor_tensor(by_e(KEY), by_e(S2), keys, ALU.mult))
                link(dve.tensor_reduce(s16[:, :], by_e(KEY), AX.X, ALU.max))
                link(dve.tensor_tensor(by_e(S2), by_e(KEY), one(s16), ALU.is_equal))
                link(dve.tensor_tensor(by_e(S1), by_e(S1), by_e(S2), ALU.add))
                dve.wait_ge(ex_ready, turn + 1)
                link(dve.tensor_tensor(by_e(GW), by_e(S1), by_e(EX), ALU.mult))
                link(dve.tensor_reduce(s16[:, :], by_e(GW), AX.X, ALU.add))
                link(dve.reciprocal(mean[:, :], s16[:, :]))
                link(dve.tensor_tensor(by_e(GW), by_e(GW), one(mean), ALU.mult))
                for s in range(NT // 2):
                    dve.wait_ge(expert_done, turn * 8 + s + 1)
                    dve.tensor_tensor(view(PR, (s % 2) * 512, [[256, 2], [E8, C], [1, E8]]),
                                      view(bank[2 + s % 4], 0, [[256, 2], [E8, C], [1, E8]]),
                                      view(GW, (s // 4 * 8 + s % 4) * E8, [[4 * E8, 2], [0, C], [1, E8]]), ALU.mult).then_inc(expert_used, 1)
                    dve.wait_ge(expert_used, turn * 8 + s + 1)
                    ins = dve.tensor_reduce(view(Y2, (s // 4 * 8 + s % 4) * C, [[4 * C, 2], [1, C]]),
                                            view(PR, (s % 2) * 512, [[256, 2], [E8, C], [1, E8]]), AX.X, ALU.add)
                link(ins)
                link(dve.tensor_tensor(XT[:, :], XT[:, :], Y2[:, :], ALU.add))

            def expert_choice(turn, w, at):
                dve.wait_ge(ec_logits, turn + 1)
                link(dve.tensor_scalar(MK[:, :], bank[1][:, 0:NPIX], w[:, at["gb"]:at["gb"] + 1], None, ALU.add))
                link(dve.tensor_reduce(mx[:, 0:1], MK[:, :], AX.X, ALU.max))
                dve.tensor_scalar(nm[:, 0:1], mx[:, 0:1], -1.0, None, ALU.mult).then_inc(ec_max, 1)
                dve.wait_ge(ec_exp, turn + 1)
                link(dve.reciprocal(den[:, 0:1], rs[:, 0:1]))
                link(dve.tensor_scalar(PB[:, :], PB[:, :], den[:, 0:1], None, ALU.mult))
                link(dve.max(top8[:, :], PB[:, :]))
                link(dve.match_replace(out=MK[:, :], in_to_replace=top8[:, :], in_values=PB[:, :], imm_value=-1.0))
                dve.scalar_tensor_tensor(GX[:, :], MK[:, :], 0.0, PB[:, :], ALU.is_lt, ALU.mult).then_inc(g_ready, 1)
                dve.wait_ge(o_done, turn + 1)
                dve.tensor_tensor(view(OC, 0, [[1, E16], [E16, B]], n=C),
                                  view(bank[5], 0, [[B, E16], [1, B]], n=C),
                                  view(w, at["b2"], [[1, E16], [0, B]], n=C), ALU.add).then_inc(oc_ready, 1)
                dve.wait_ge(oc_turned, turn + 1)
                dve.tensor_tensor(view(OB, 0, [[C, B], [1, C]]), view(bank[6], 0, [[0, B], [1, C]]),
                                  view(cst, CST["ecmask"], [[1, B], [0, C]]), ALU.mult).then_inc(ob_ready, 1)
                dve.wait_ge(ec_out, turn + 1)
                link(dve.tensor_tensor(XT[:, :], XT[:, :], bank[7][:, :], ALU.add))

            dve.wait_ge(x_turned, 1)
            link(dve.tensor_copy(XT[:, :], bank[0][:, :]))

            norm(0)
            dve.wait_ge(wa_s, 16)
            dve.wait_ge(kv_done, 1)
            dve.tensor_scalar(KC[:, :], bank[2][:, :], wa[:, WA["bk0"]:WA["bk0"] + 1], None, ALU.add)
            dve.tensor_tensor(tiles(VT), tiles(bank[3]), view(wa, WA["bv0"], [[0, NT], [1, C]]), ALU.add)\
               .then_inc(kv_ready, 1)
            attend(0, 8, False)
            dve.wait_ge(p_ready, 8)
            dve.tensor_scalar(den[:, 0:NT], nm[:, 0:NT], 0.0, None, ALU.min).then_inc(pad_asked, 1)
            dve.wait_ge(pad_ready, 1)
            by_unit = lambda t, o=0: view(t, o, [[8, 2], [1, 2], [2, 4]])
            link(dve.tensor_tensor(by_unit(e0), by_unit(e0), view(cst, CST["npad"], [[0, 2], [1, 2], [0, 4]]), ALU.mult))
            link(dve.tensor_tensor(e0[:, 0:NT], e0[:, 0:NT], rs[:, 0:NT], ALU.add))
            link(dve.reciprocal(view(den, 0, [[8, 2], [4, 2], [1, 4]]), by_unit(e0)))
            dve.wait_ge(av_done, 8)
            link(dve.tensor_tensor(tiles(Y2), tiles(bank[1]), per_tile(den), ALU.mult))
            link(dve.tensor_tensor(XT[:, :], XT[:, :], Y2[:, :], ALU.add))
            norm(1)
            dve.wait_ge(wb_s, 16)
            top2(0, WB["rb0"], wb)

            norm(2)
            link(dve.tensor_tensor(view(RINGS, 0, [[1, 288]]), wb[:, WB["wf"]:WB["wf"] + 288],
                                   wb[:, WB["wf"]:WB["wf"] + 288], ALU.mult))
            link(dve.tensor_reduce(w2s[:, :], view(RINGS, 0, [[1, 288]]), AX.X, ALU.add))
            link(dve.tensor_tensor(view(RINGS, 0, [[C, 9], [1, C]]), view(wb, WB["wf"], [[C, 9], [1, C]]),
                                   view(cst, CST["dtaps"], [[1, 9], [0, C]]), ALU.mult))
            link(dve.tensor_reduce(wsd[:, :], view(RINGS, 0, [[1, 288]]), AX.X, ALU.add))
            dve.wait_ge(xp_ready, 1)

            def maxima(i):
                k = 0
                for n in range(UNITS):
                    if not ON_DVE[n]:
                        continue
                    tap, j = divmod(n, 4)
                    after(dve, d_used, DVE_UNITS * i + k + 1 - DRING)
                    w_at = WB["lw"] + i * UNITS + n
                    dve.tensor_scalar(view(RINGS, (k % DRING) * F, [[NPIX, NBH], [WW, HH], [1, WW]]),
                                      view(XP, tap // 3 * PADW + tap % 3, [[PADW * PADW, NBH], [PADW, HH], [1, WW]]),
                                      view(wb, w_at, [[1, 1]]), None, ALU.max).then_inc(d_ready, 1)
                    k += 1

            def drain(i, b):
                dve.wait_ge(d_used, DVE_UNITS * (i + 1))
                dve.wait_ge(a_used, ACT_UNITS * (i + 1))
                dve.wait_ge(drained, i + 1)
                dve.scalar_tensor_tensor(ACC[:, :], bank[2 + b][:, :], view(cst, CST["sel"] + i, [[1, 1]]), ACC[:, :],
                                         ALU.mult, ALU.add).then_inc(drained, 1)

            maxima(0)
            dve.wait_ge(cor_done, 1)
            dve.tensor_scalar(ACC[:, :], bank[4][:, :], wsd[:, 0:1], None, ALU.subtract).then_inc(drained, 1)
            with dve.Fori(0, 3) as m:
                maxima(2 * m + 1)
                drain(2 * m, 0)
                maxima(2 * m + 2)
                drain(2 * m + 1, 1)
            maxima(7)
            drain(6, 0)
            dve.wait_ge(l2_done, 1)
            link(dve.tensor_scalar(D2[:, :], bank[5][:, :], -2.0, w2s[:, 0:1], ALU.mult, ALU.add))
            dve.tensor_scalar(D2[:, :], D2[:, :], 1e-12, None, ALU.max).then_inc(d2_ready, 1)
            drain(7, 1)
            dve.wait_ge(drained, 9)
            dve.wait_ge(l2_ready, 1)
            link(dve.tensor_tensor(ACC[:, :], D2[:, :], ACC[:, :], ALU.subtract))
            dve.tensor_tensor(ACC[:, :], ACC[:, :], D2[:, :], ALU.subtract).then_inc(lo_ready, 1)
            dve.wait_ge(lo_turned, 1)
            for g in range(4):
                ins = dve.tensor_tensor(view(XT, g * P, [[C, B4], [1, C]]), view(XT, g * P, [[C, B4], [1, C]]),
                                        view(bank[0], g * P, [[1, B4], [B4, C]]), ALU.add)
            link(ins)
            norm(3)
            expert_choice(0, wb, {"gb": WB["gb0"], "b2": WB["b20"]})

            norm(4)
            dve.wait_ge(wc_s, 16)
            link(dve.tensor_tensor(view(base, 0, [[3 * KG, 2], [1, 3 * KG]]), view(cst, CST["geo"], [[3 * KG, 2], [1, 3 * KG]]),
                                   view(wc, WC["bom"], [[0, 2], [1, 3 * KG]]), ALU.add))

            def points(turn):
                for g in range(4):
                    bh, half = divmod(g, 2)
                    dve.wait_ge(om_done, 4 * turn + g + 1)
                    dve.tensor_tensor(view(OM, (8 * bh + half) * 3 * KG, [[2 * 3 * KG, B4], [1, 3 * KG]]),
                                      view(bank[1 + g % 2], 0, [[3 * KG, B4], [1, 3 * KG]]),
                                      view(base, half * 3 * KG, [[0, B4], [1, 3 * KG]]), ALU.add).then_inc(om_used, 1)
                dve.wait_ge(om_used, 4 * turn + 4)
                lx = view(OM, 0, [[3 * KG, NT], [1, KG]])
                ly = view(OM, KG, [[3 * KG, NT], [1, KG]])
                am = view(AM, 0, [[KG, NT], [1, KG]])
                link(dve.tensor_scalar(am, ly, 8.0, None, ALU.is_ge))
                link(dve.scalar_tensor_tensor(view(LXA, 0, [[2 * KG, NT], [2, KG]]), am, BIG, lx, ALU.mult, ALU.add))
                link(dve.scalar_tensor_tensor(ly, am, -7.0, ly, ALU.mult, ALU.add))
                link(dve.tensor_scalar(am, am, -1.0, 1.0, ALU.mult, ALU.add))
                dve.scalar_tensor_tensor(view(LXA, 1, [[2 * KG, NT], [2, KG]]), am, BIG, lx, ALU.mult, ALU.add)\
                   .then_inc(lxa_ready, 1)
                n = 0
                for bh in range(NBH):
                    for r0 in range(0, NR, 4):
                        rows = min(4, NR - r0)
                        dve.wait_ge(val_done, 6 * turn + n + 1)
                        ins = dve.tensor_tensor(view(VB, bh * B4 * 288 + r0, [[1, rows], [NR, P]]),
                                                view(bank[3 + n % 2], 0, [[P, rows], [1, P]]),
                                                view(cst, CST["gmask"], [[0, rows], [1, P]]), ALU.mult)
                        ins.then_inc(val_used, 1)
                        n += 1

            def sample(turn, b, half):
                n = 2 * b + half
                dve.wait_ge(hxy_ready, 16 * turn + n + 1)
                dve.tensor_tensor(view(HYM, 0, [[NR, KG], [1, NR]]), view(HXY, half * HATS + HXN, [[NR, KG], [1, NR]]),
                                  view(OM, n * 3 * KG + 2 * KG, [[1, KG], [0, NR]]), ALU.mult).then_inc(hym_ready, 1)
                dve.wait_ge(hym_ready, 16 * turn + n + 1)
                for k in range(K9):
                    idx = 9 * (16 * turn + n) + k
                    dve.wait_ge(prod_done, idx + 1)
                    dve.tensor_tensor(view(PRD, k * 288, [[72, G], [NR, CG], [1, NR]]),
                                      view(bank[2 + (9 * half + k) % LOOK], 0, [[72, G], [NR, CG], [1, NR]]),
                                      view(HYM, k * G * NR, [[NR, G], [0, CG], [1, NR]]), ALU.mult).then_inc(prod_used, 1)
                dve.wait_ge(prod_used, 9 * (16 * turn + n) + 9)
                dve.tensor_reduce(view(SMP, n * C, [[1, C]]), view(PRD, 0, [[NR, C], [288, K9], [1, NR]]), AX.XY,
                                  ALU.add).then_inc(smp_ready, 1)
                dve.wait_ge(smp_ready, 16 * turn + n + 1)

            def deform(turn):
                points(turn)
                for half in range(2):
                    sample(turn, 0, half)
                with dve.Fori(1, B) as b:
                    for half in range(2):
                        sample(turn, b, half)
                for bh in range(NBH):
                    ins = dve.tensor_copy(view(SMT, bh * NPIX, [[P, 2], [C, B4], [1, C]]),
                                          view(SMP, bh * NPIX, [[C, 2], [2 * C, B4], [1, C]]))
                ins.then_inc(smt_ready, 1)
                dve.wait_ge(y_done, turn + 1)
                dve.tensor_reduce(c1[:, 0:1], bank[1][:, :], AX.X, ALU.add).then_inc(sum_ready, 1)
                dve.wait_ge(sum_done, turn + 1)
                link(dve.tensor_copy(c1[:, 1:2], bank[2][:, 0:1]))
                dve.tensor_scalar(ACC[:, :], bank[1][:, :], c1[:, 1:2], None, ALU.subtract).then_inc(cen_ready, 1)
                dve.wait_ge(sq_done, turn + 1)
                dve.tensor_scalar(c2[:, 2:3], bank[3][:, 0:1], 1e-5, None, ALU.add).then_inc(bnv_ready, 1)
                dve.wait_ge(bsd_ready, turn + 1)
                link(dve.reciprocal(c1[:, 3:4], c2[:, 1:2]))
                link(dve.tensor_tensor(c1[:, 2:3], c1[:, 3:4], wc[:, WC["gamma"]:WC["gamma"] + 1], ALU.mult))

            deform(0)
            dve.tensor_copy(c1[:, 0:1], c1[:, 2:3]).then_inc(bn_ready, 1)
            deform(1)
            link(dve.tensor_scalar(ACC[:, :], ACC[:, :], c1[:, 2:3], wc[:, WC["beta"]:WC["beta"] + 1], ALU.mult, ALU.add))
            dve.tensor_tensor(YC[:, :], ACC[:, :], XNC[:, :], ALU.add).then_inc(yc_ready, 1)
            dve.tensor_copy(c1[:, 0:1], c1[:, 2:3]).then_inc(bn_ready, 1)
            dve.wait_ge(wc_done, 1)
            link(dve.tensor_tensor(XT[:, :], XT[:, :], bank[4][:, :], ALU.add))
            norm(5)
            top2(1, WC["rb1"], wc)

            norm(6)
            dve.wait_ge(wd_s, 16)
            dve.tensor_scalar(bqh[:, :], cv("hm", HEADS), wd[:, WD["bq1"]:WD["bq1"] + 1], None, ALU.mult)\
               .then_inc(bqh_ready, 1)
            dve.wait_ge(kv_done, 2)
            dve.tensor_scalar(KC[:, :], bank[2][:, :], wd[:, WD["bk1"]:WD["bk1"] + 1], None, ALU.add)
            dve.tensor_tensor(tiles(VT), tiles(bank[3]), view(wd, WD["bv1"], [[0, NT], [1, C]]), ALU.add)\
               .then_inc(kv_ready, 1)
            attend(8, 32, True)
            dve.wait_ge(p_ready, 40)
            link(dve.reciprocal(den[:, :], rs[:, :]))
            dve.wait_ge(av_done, 40)
            dve.tensor_tensor(view(Y2, 0, [[HC, 64], [1, HC]]), view(bank[1], 0, [[HC, 64], [1, HC]]),
                              view(den, 0, [[1, 64], [0, HC]]), ALU.mult).then_inc(att_ready, 1)
            link(dve.tensor_tensor(tiles(XT), tiles(XT), view(wd, WD["bu1"], [[0, NT], [1, C]]), ALU.add))
            dve.wait_ge(u_done, 1)
            link(dve.tensor_tensor(XT[:, :], XT[:, :], bank[2][:, :], ALU.add))
            norm(7)
            expert_choice(1, wd, {"gb": WD["gb1"], "b2": WD["b21"]})
            dve.tensor_copy(XT[:, 0:1], XT[:, 0:1]).then_inc(x_ready, 1)
            dve.wait_ge(fin_turned, 1)
            dve.tensor_copy(XC[:, :], bank[0][:, :]).then_inc(fin_ready, 1)

        @block.tensor
        def _(pe):
            def turn4(dst, src, s):
                for g in range(4):
                    ins = pe.transpose(dst[:, g * P:(g + 1) * P], src[:, g * P:(g + 1) * P], ident)
                ins.then_inc(s, 1)

            def norm(n):
                pe.wait_ge(xn_ready, n + 1)
                turn4(bank[0], XN, xn_turned)

            def w_(t, at, n=P, p0=0, np_=P):
                return t[p0:p0 + np_, at:at + n]

            def project(turn, t, at):
                pe.wait_ge(xnc_ready, {0: 1, 1: 6}[turn])
                pe.matmul(bank[1][:, :], w_(t, at["q"]), XNC[:, :], start=True, stop=True).then_inc(q_done, 1)
                pe.matmul(bank[2][:, :], w_(t, at["k"]), XNC[:, :], start=True, stop=True)
                for g in range(4):
                    ins = pe.matmul(bank[3][:, g * P:(g + 1) * P], XNC[:, g * P:(g + 1) * P], w_(t, at["v"]),
                                    start=True, stop=True)
                ins.then_inc(kv_done, 1)
                pe.wait_ge(qc_ready, turn + 1)
                pe.wait_ge(kv_ready, turn + 1)

            def attend(first, steps, l3):
                def unit(s, j):
                    u = 2 * (s - first) + j
                    t, h = divmod(u, HEADS) if l3 else (u // 8 * 8 + u % 2 * 4 + u // 2 % 4, 0)
                    bh, half, b4 = t // 8, t // 4 % 2, t % 4
                    return t, h, bh, half, b4

                def scores(s):
                    after(pe, nm_ready, s - 1)
                    for j in range(2):
                        t, h, bh, half, b4 = unit(s, j)
                        q0 = h * F + bh * NPIX + half * P
                        ins = pe.matmul(bank[4 + s % 2][:, j * 256:j * 256 + 256],
                                        QC[C * b4:C * b4 + C, q0:q0 + P],
                                        KC[C * b4:C * b4 + C, bh * NPIX:(bh + 1) * NPIX], start=True, stop=True)
                    ins.then_inc(scored, 1)

                def turn(s):
                    pe.wait_ge(p_ready, s + 1)
                    after(pe, pts_ready, s - 1)
                    for j in range(2):
                        for kt in range(2):
                            at = (2 * j + kt) * P
                            ins = pe.transpose(bank[6 + s % 2][:, at:at + P],
                                               SM[:, (s % 2) * 512 + at:(s % 2) * 512 + at + P], ident)
                    ins.then_inc(pt_done, 1)

                def values(s):
                    pe.wait_ge(pts_ready, s + 1)
                    for j in range(2):
                        t, h, bh, half, b4 = unit(s, j)
                        c0, cn = (HC * h, HC) if l3 else (0, C)
                        for kt in range(2):
                            at = (s % 2) * 512 + (2 * j + kt) * P
                            v0 = ((2 * bh + kt) * B4 + b4) * C + c0
                            ins = pe.matmul(bank[1][:, t * C + c0:t * C + c0 + cn], PTS[:, at:at + P],
                                            VT[:, v0:v0 + cn], start=(kt == 0), stop=(kt == 1))
                    ins.then_inc(av_done, 1)

                for s in range(first, first + steps + 2):
                    if s < first + steps:
                        scores(s)
                    if first < s <= first + steps:
                        turn(s - 1)
                    if s >= first + 2:
                        values(s - 2)

            def top2(turn, w, at, nx):
                pe.wait_ge(xnc_ready, nx)
                for g in range(4):
                    ins = pe.matmul(bank[1][:, g * 32:g * 32 + 32], XNC[:, g * P:(g + 1) * P], w_(w, at["r"], 32),
                                    start=True, stop=True)
                ins.then_inc(routed, 1)
                for s in range(NT // 2):
                    after(pe, expert_used, 8 * turn + s - 3)
                    bk = bank[2 + s % 4]
                    bh, b4 = divmod(s, B4)
                    pe.matmul(bk[:, :], cst[C * b4:C * b4 + 1, CST["ones"]:CST["ones"] + P],
                              w[C * b4:C * b4 + 1, at["eb"]:at["eb"] + 512],
                              start=True, stop=False, skip_group_check=True)
                    for j in range(2):
                        g = 2 * bh + j
                        ins = pe.matmul(bk[:, j * 256:j * 256 + 256], XNC[C * b4:C * b4 + C, g * P:(g + 1) * P],
                                        w[C * b4:C * b4 + C, at["ew"]:at["ew"] + 256], start=False, stop=True,
                                        skip_group_check=True)
                    ins.then_inc(expert_done, 1)

            def expert_choice(turn, w, at, nx):
                pe.wait_ge(xnc_ready, nx)
                for bh in range(NBH):
                    ins = pe.matmul(bank[1][:, 0:NPIX], w_(w, at["gw"] + bh * P), XNC[:, bh * NPIX:(bh + 1) * NPIX],
                                    start=(bh == 0), stop=(bh == NBH - 1))
                ins.then_inc(ec_logits, 1)
                pe.wait_ge(g_ready, turn + 1)
                for half in range(2):
                    ins = pe.transpose(bank[2][:, half * P:(half + 1) * P], GX[:, half * P:(half + 1) * P], ident)
                ins.then_inc(g_turned, 1)
                pe.wait_ge(gt_ready, turn + 1)
                for b in range(B):
                    for half in range(2):
                        t = b // 4 * 8 + half * 4 + b % 4
                        ins = pe.matmul(bank[3][0:C, b * E16:(b + 1) * E16], XN[:, t * C:(t + 1) * C],
                                        GT[:, half * P + b * E16:half * P + (b + 1) * E16],
                                        start=(half == 0), stop=(half == 1))
                ins.then_inc(pooled, 1)
                pe.wait_ge(pa_ready, turn + 1)
                pe.wait_ge(pool_set, 3)
                for e in range(E16):
                    ins = pe.matmul(bank[4][:, e * B:(e + 1) * B], w[0:C + 1, at["w1"] + e * HID:at["w1"] + (e + 1) * HID],
                                    view(PA, e, [[E16, B]], n=C + 1), start=True, stop=True)
                ins.then_inc(h_done, 1)
                pe.wait_ge(h_ready, turn + 1)
                for e in range(E16):
                    ins = pe.matmul(bank[5][0:C, e * B:(e + 1) * B], w[:, at["w2"] + e * C:at["w2"] + (e + 1) * C],
                                    HB[:, e * B:(e + 1) * B], start=True, stop=True)
                ins.then_inc(o_done, 1)
                pe.wait_ge(oc_ready, turn + 1)
                pe.transpose(bank[6][:, 0:C], OC[:, :], cst[0:C, CST["ident"]:CST["ident"] + C]).then_inc(oc_turned, 1)
                pe.wait_ge(ob_ready, turn + 1)
                for g in range(4):
                    bh, half = divmod(g, 2)
                    ins = pe.matmul(bank[7][:, g * P:(g + 1) * P], GX[:, half * P:(half + 1) * P],
                                    OB[:, bh * P:(bh + 1) * P], start=True, stop=True)
                ins.then_inc(ec_out, 1)

            pe.wait_ge(x_in_s, 16 * NBH)
            pe.wait_ge(cst_s, 16)
            turn4(bank[0], XC, x_turned)

            norm(0)
            pe.wait_ge(wa_s, 16)
            project(0, wa, {"q": WA["q0"], "k": WA["k0"], "v": WA["v0"]})
            attend(0, 8, False)
            norm(1)
            pe.wait_ge(wb_s, 16)
            top2(0, wb, {"r": WB["r0"], "eb": WB["eb0"], "ew": WB["ew0"]}, 2)

            norm(2)
            pe.wait_ge(xp_ready, 1)

            def tap_of(t, tap):
                return view(t, tap // 3 * PADW + tap % 3, [[PADW * PADW, NBH], [PADW, HH], [1, WW]])

            first = [min(n // 4 for n in range(UNITS) if ON_DVE[n] and n % 4 == j) for j in range(4)]
            last = [max(n // 4 for n in range(UNITS) if ON_DVE[n] and n % 4 == j) for j in range(4)]
            for n in range(UNITS):
                if ON_DVE[n]:
                    tap, j = divmod(n, 4)
                    ins = pe.matmul(bank[4][32 * j:32 * j + 32, :], cv("nrep", 32), tap_of(XP, tap),
                                    start=(tap == first[j]), stop=(tap == last[j]), skip_group_check=True)
            ins.then_inc(cor_done, 1)

            def sums(i, b):
                after(pe, drained, i)
                kd = ka = 0
                for n in range(UNITS):
                    tap, j = divmod(n, 4)
                    if ON_DVE[n]:
                        pe.wait_ge(d_ready, DVE_UNITS * i + kd + 1)
                        slot, rep, used = (kd % DRING) * F, "rep2", d_used
                        kd += 1
                    else:
                        pe.wait_ge(a_ready, ACT_UNITS * i + ka + 1)
                        slot, rep, used = (DRING + ka % ARING) * F, "rep1", a_used
                        ka += 1
                    pe.matmul(bank[2 + b][32 * j:32 * j + 32, :], cv(rep, 32), RINGS[:, slot:slot + F],
                              start=(tap == 0), stop=(tap == 8), skip_group_check=True).then_inc(used, 1)

            sums(0, 0)
            sums(1, 1)
            with pe.Fori(1, 4) as m:
                sums(2 * m, 0)
                sums(2 * m + 1, 1)
            pe.wait_ge(sqp_ready, 1)
            for tap in range(9):
                pe.matmul(bank[5][:, :], w_(wb, WB["w9"] + tap * P), tap_of(XP, tap), start=(tap == 0), stop=False)
            for tap in range(9):
                ins = pe.matmul(bank[5][:, :], cv("nhalf", P), tap_of(SQP, tap), start=False, stop=(tap == 8))
            ins.then_inc(l2_done, 1)
            pe.wait_ge(lo_ready, 1)
            turn4(bank[0], ACC, lo_turned)
            norm(3)
            expert_choice(0, wb, {"gw": WB["gw0"], "w1": WB["w10"], "w2": WB["w20"]}, 3)

            norm(4)
            pe.wait_ge(wc_s, 16)

            def turn_hats(turn, b, half):
                n = 2 * b + half
                pe.wait_ge(hxy_ready, 16 * turn + n + 1)
                for g in range(3):
                    after(pe, hxt_ready, 3 * (16 * turn + n) + g - 1)
                    bk = bank[(3 * half + g) % 2]
                    for k in range(3):
                        at = half * HATS + (3 * g + k) * P
                        ins = pe.transpose(bk[:, k * P:(k + 1) * P], view(HXY, at, [[1, P]]), ident)
                    ins.then_inc(hx_turned, 1)

            def products(turn, b, half):
                n = 2 * b + half
                for k in range(K9):
                    if k % 3 == 0:
                        pe.wait_ge(hxt_ready, 3 * (16 * turn + n) + k // 3 + 1)
                    after(pe, prod_used, 9 * (16 * turn + n) + k + 1 - LOOK)
                    pe.matmul(bank[2 + (9 * half + k) % LOOK][:, 0:288], view(HXT, (half * K9 + k) * P, [[1, P]]),
                              view(VB, b * 288, [[1, 288]]), start=True, stop=True).then_inc(prod_done, 1)

            def deform(turn, src):
                for g in range(4):
                    after(pe, om_used, 4 * turn + g - 1)
                    pe.matmul(bank[1 + g % 2][:, 0:B4 * 3 * KG], src[:, g * P:(g + 1) * P], w_(wc, WC["om"], B4 * 3 * KG),
                              start=True, stop=True).then_inc(om_done, 1)
                n = 0
                pe.wait_ge(xw_ready, turn + 1)
                for bh in range(NBH):
                    for r0 in range(0, NR, 4):
                        rows = min(4, NR - r0)
                        after(pe, val_used, 6 * turn + n - 1)
                        bk = bank[3 + n % 2]
                        pe.matmul(bk[:, 0:rows * P], cst[0:1, CST["ones"]:CST["ones"] + P],
                                  wc[0:1, WC["bval"]:WC["bval"] + rows * P], start=True, stop=False, skip_group_check=True)
                        for r in range(rows):
                            ins = pe.matmul(bk[:, r * P:(r + 1) * P],
                                            view(XW, (bh * NR + r0 + r) * P, [[1, P]]),
                                            w_(wc, WC["val"]), start=False, stop=True, skip_group_check=True)
                        ins.then_inc(val_done, 1)
                        n += 1
                turn_hats(turn, 0, 0)
                pe.wait_ge(val_used, 6 * turn + 6)

                def body(b, more):
                    turn_hats(turn, b, 1)
                    products(turn, b, 0)
                    if more:
                        turn_hats(turn, b + 1, 0)
                    products(turn, b, 1)
                body(0, True)
                with pe.Fori(1, B - 1) as b:
                    body(b, True)
                body(B - 1, False)
                pe.wait_ge(smt_ready, turn + 1)
                turn4(bank[0], SMT, smp_turned)
                pe.wait_ge(sc_ready, turn + 1)
                pe.matmul(bank[1][:, :], w_(wc, WC["wo"]), YC[:, :], start=True, stop=True).then_inc(y_done, 1)
                pe.wait_ge(sum_ready, turn + 1)
                pe.matmul(bank[2][:, 0:1], cv("avg", P), c1[:, 0:1], start=True, stop=True).then_inc(sum_done, 1)
                pe.wait_ge(sq_ready, turn + 1)
                pe.matmul(bank[3][:, 0:1], cv("avg", P), c2[:, 0:1], start=True, stop=True).then_inc(sq_done, 1)

            pe.wait_ge(xnc_ready, 4)
            deform(0, XNC)
            pe.wait_ge(dc_ready, 1)
            deform(1, YC)
            pe.wait_ge(yc_ready, 1)
            for g in range(4):
                ins = pe.matmul(bank[4][:, g * P:(g + 1) * P], YC[:, g * P:(g + 1) * P], w_(wc, WC["wc"]),
                                start=True, stop=True)
            ins.then_inc(wc_done, 1)
            norm(5)
            top2(1, wc, {"r": WC["r1"], "eb": WC["eb1"], "ew": WC["ew1"]}, 5)

            norm(6)
            pe.wait_ge(wd_s, 16)
            project(1, wd, {"q": WD["q1"], "k": WD["k1"], "v": WD["v1"]})
            attend(8, 32, True)
            pe.wait_ge(att_ready, 1)
            turn4(bank[0], Y2, att_turned)
            pe.wait_ge(attc_ready, 1)
            for g in range(4):
                ins = pe.matmul(bank[2][:, g * P:(g + 1) * P], YC[:, g * P:(g + 1) * P], w_(wd, WD["u1"]),
                                start=True, stop=True)
            ins.then_inc(u_done, 1)
            norm(7)
            expert_choice(1, wd, {"gw": WD["gw1"], "w1": WD["w11"], "w2": WD["w21"]}, 7)
            pe.wait_ge(x_ready, 1)
            turn4(bank[0], XT, fin_turned)


def _constants(np):
    c = np.zeros((P, NCST), np.float32)

    def put(name, a):
        c[:, CST[name]:CST[name] + a.shape[1]] = a

    p = np.arange(P)
    pix = np.arange(NPIX)
    put("ident", np.eye(P))
    ky, kx = pix // WW, pix % WW
    for half in range(2):
        qy, qx = half * 8 + p // WW, p % WW
        near = (abs(qy[:, None] - ky) <= 3) & (abs(qx[:, None] - kx) <= 3)
        c[:, CST["mask"] + half * NPIX:CST["mask"] + (half + 1) * NPIX] = np.where(near, 0.0, -BIG)
        npad = 49 - near.sum(1)
        c[:, CST["floor"] + half] = np.where(npad > 0, 0.0, -NEG)
        c[:, CST["npad"] + half] = npad
        geo = np.zeros((P, 3, K9, G))
        k = np.arange(K9)
        geo[:, 0] = (qx[:, None] + k % 3 - 1)[:, :, None]
        geo[:, 1] = (qy[:, None] + k // 3 - 1)[:, :, None]
        c[:, CST["geo"] + half * 3 * KG:CST["geo"] + (half + 1) * 3 * KG] = geo.reshape(P, -1)
    put("top", np.full((P, 2), -NEG))
    put("one", np.ones((P, 1)))
    put("eps6", np.full((P, 1), 1e-6))
    put("eps5", np.full((P, 1), 1e-5))
    put("hm", (p[:, None] % C // HC == np.arange(HEADS)) * np.float32(HC ** -0.5))
    put("ones", np.ones((P, 512)))
    put("xg", np.tile(np.arange(WW), (P, 1)))
    put("yg", np.tile(np.arange(NR), (P, 1)))
    put("gmask", p[:, None] // 32 == p[None] % C // CG)
    rep = p[:, None] // C == p[None, :32] % B4
    put("rep1", rep)
    put("rep2", 2.0 * rep)
    put("nrep", -1.0 * rep)
    put("nhalf", -0.5 * (p[:, None] // C == p[None] % B4))
    put("avg", (p[:, None] % C == p[None] % C) / (B * NPIX))
    put("ecmask", p[:, None] // E16 == np.arange(B))
    put("sel", p[:, None] // B4 % 8 == np.arange(8))
    put("keys", np.tile(E8 - np.arange(E8), (P, 1)))
    dt = np.array([[ON_DVE[4 * t + j] for t in range(9)] for j in range(4)])
    put("dtaps", dt[p // 32])
    return c


def _layouts(np, a):
    f = np.float32

    def blocks(w):
        r = np.zeros((P, B4 * w.shape[1]), f)
        for b in range(B4):
            r[b * C:(b + 1) * C, b * w.shape[1]:(b + 1) * w.shape[1]] = w
        return r

    def rows(v):
        return np.tile(v.reshape(1, -1), (P, 1))

    def pack(spec, n, parts):
        out = np.zeros((P, n), f)
        for name, width in spec.items():
            v = parts[name]
            out[0:v.shape[0], width:width + v.shape[1]] = v
        return out

    def top2(i):
        l = f"L{i}_ffn_"
        ew = a[l + "expert_w"].transpose(1, 2, 0).reshape(C, C * E8)
        return (blocks(a[l + "router_w"]), rows(a[l + "router_b"]), np.tile(ew, (B4, 1)),
                np.tile(a[l + "expert_b"].T.reshape(1, -1), (P, 2)))

    def ec(i):
        l = f"L{i}_ffn_"
        gw = np.zeros((P, NBH, B, E16), f)
        for b in range(B):
            gw[b % B4 * C:(b % B4 + 1) * C, b // B4, b] = a[l + "gate_w"].T
        gb = np.tile(a[l + "gate_b"], B).reshape(P, 1)
        w1 = a[l + "weight1"].transpose(1, 0, 2).reshape(C + 1, E16 * HID)
        w2 = a[l + "weight2"][:, :HID].transpose(1, 0, 2).reshape(HID, E16 * C)
        b2 = a[l + "weight2"][:, HID].T
        return gw.reshape(P, NBH * P), gb, w1, w2, b2

    col4 = lambda v: np.tile(v, B4).reshape(P, 1)
    wa = pack(WA, NWA, {"q0": blocks(a["L0_conv_Wq"].T), "k0": blocks(a["L0_conv_Wk"].T),
                        "v0": blocks(a["L0_conv_Wv"].T), "bq0": col4(a["L0_conv_bq"]), "bk0": col4(a["L0_conv_bk"]),
                        "bv0": rows(a["L0_conv_bv"])})
    w = a["L1_conv_W"].reshape(C, C, 9)
    lw = w.reshape(4, 8, C, 9).transpose(2, 1, 3, 0).reshape(C, 288)
    wf = np.repeat(w.transpose(0, 2, 1).reshape(C, 288), B4, axis=0)
    w9 = np.zeros((B4, C, 9, C, B4), f)
    for b in range(B4):
        w9[b, :, :, :, b] = w.transpose(1, 2, 0)
    r0, rb0, ew0, eb0 = top2(0)
    gw, gb, w1, w2, b2 = ec(1)
    wb = pack(WB, NWB, {"r0": r0, "rb0": rb0, "ew0": ew0, "eb0": eb0, "lw": np.tile(lw, (B4, 1)), "wf": wf,
                        "w9": w9.reshape(P, 9 * P), "gw0": gw, "gb0": gb, "w10": w1, "w20": w2, "b20": b2})
    kinds = np.array([[g * 3 * K9 + (2 * k + t if t < 2 else 2 * K9 + k) for k in range(K9) for g in range(G)]
                      for t in range(3)]).reshape(-1)
    r1, rb1, ew1, eb1 = top2(2)
    wc = pack(WC, NWC, {"om": blocks(a["L2_conv_Wom"][:, kinds]), "bom": rows(a["L2_conv_bom"][kinds]),
                        "val": blocks(a["L2_conv_Wv"]), "bval": np.tile(a["L2_conv_bv"].reshape(1, -1), (1, 16)),
                        "wo": blocks(a["L2_conv_Wo"]), "gamma": col4(a["L2_conv_gamma"]),
                        "beta": col4(a["L2_conv_beta"]), "wc": blocks(a["L2_conv_Wc"].T),
                        "r1": r1, "rb1": rb1, "ew1": ew1, "eb1": eb1})
    p, pix = np.arange(P), np.arange(NPIX)
    span = 2 * WW - 1
    rel = np.zeros((P, 2, HEADS, NPIX), f)
    for half in range(2):
        q = half * P + p
        at = (pix[None] // WW - q[:, None] // WW + HH - 1) * span + pix[None] % WW - q[:, None] % WW + WW - 1
        rel[:, half] = a["L3_conv_pos_enc"][:, at].transpose(1, 0, 2)
    gw, gb, w1, w2, b2 = ec(3)
    wd = pack(WD, NWD, {"q1": blocks(a["L3_conv_Wq"].T), "k1": blocks(a["L3_conv_Wk"].T),
                        "v1": blocks(a["L3_conv_Wv"].T), "bq1": col4(a["L3_conv_bq"]), "bk1": col4(a["L3_conv_bk"]),
                        "bv1": rows(a["L3_conv_bv"]), "u1": blocks(a["L3_conv_Wu"].T), "bu1": rows(a["L3_conv_bu"]),
                        "rel": rel.reshape(P, -1), "gw1": gw, "gb1": gb, "w11": w1, "w21": w2, "b21": b2})
    return wa, wb, wc, wd


def kernel(**inputs):
    import numpy as _np
    import concourse.bacc as _bacc
    from concourse import mybir as _mybir
    from concourse.bass_utils import run_bass_kernel_spmd as _run

    a = {k: _np.asarray(v) for k, v in inputs.items()}
    arrays = {"x": _np.ascontiguousarray(a["x"]), "cst": _constants(_np)}
    arrays.update(zip(("wa", "wb", "wc", "wd"), _layouts(_np, a)))
    nc = _bacc.Bacc("TRN2", target_bir_lowering=False, num_devices=1)
    args = [nc.dram_tensor(f"in_{n}", v.shape, _mybir.dt.float32, kind="ExternalInput").ap() for n, v in arrays.items()]
    out = nc.dram_tensor("out_y", a["x"].shape, _mybir.dt.float32, kind="ExternalOutput").ap()
    metaformer(nc, *args, out)
    r = _run(nc, [{f"in_{n}": v for n, v in arrays.items()}], core_ids=[0])
    return r.results[0]["out_y"]
```

```python
import concourse.bass as bass
from concourse import mybir
from contextlib import ExitStack

B, C, HH, WW = 8, 32, 16, 16
NPIX = HH * WW
P = 128
B4 = P // C
NBH = B // B4
NT = B * NPIX // P
F = NT * C
E8 = 8
E16, HID = 16, 128
HEADS, HC = 4, 8
G, CG, K9 = 4, 8, 9
NA, NR = 2, 9
PADW = HH + 2
KG = K9 * G
HXN, HYN = KG * NA * WW, KG * NR
HATS = HXN + HYN
BIG = 1e30
NEG = -3e38
TURNED = 8
TURN_AT = {2: (0,), 5: (1,), 8: (2,)}
LOOK = 6
PAIRS = 3

UNITS = 9 * 4
DVE_UNITS = 22
ACT_UNITS = UNITS - DVE_UNITS
ON_DVE = [(n + 1) * DVE_UNITS // UNITS > n * DVE_UNITS // UNITS for n in range(UNITS)]
DRING, ARING = DVE_UNITS // 2, ACT_UNITS // 2


def columns(spec):
    at, out = 0, {}
    for name, n in spec:
        out[name] = at
        at += n
    return out, at


CST_SPEC = [("ident", 128), ("mask", 512), ("floor", 2), ("npad", 2), ("one", 1),
            ("eps6", 1), ("eps5", 1), ("hm", HEADS), ("ones", 512), ("geo", 2 * 3 * KG), ("xg", WW), ("yg", NR),
            ("gmask", 128), ("rep1", 32), ("rep2", 32), ("nrep", 32), ("nhalf", 128), ("avg", 128),
            ("ecmask", B), ("sel", 8), ("keys", E8), ("dtaps", 9)]
CST, NCST = columns(CST_SPEC)
WA_SPEC = [("q0", 128), ("k0", 128), ("v0", 128), ("bq0", 1), ("bk0", 1), ("bv0", 32)]
WA, NWA = columns(WA_SPEC)
WB_SPEC = [("r0", 32), ("rb0", E8), ("ew0", 256), ("eb0", 512),
           ("lw", 288), ("wf", 288), ("w9", 9 * 128),
           ("gw0", 256), ("gb0", 1), ("w10", E16 * HID), ("w20", E16 * C), ("b20", E16)]
WB, NWB = columns(WB_SPEC)
WC_SPEC = [("om", B4 * 3 * KG), ("bom", 3 * KG), ("val", 128), ("bval", 512), ("wo", 128),
           ("gamma", 1), ("beta", 1), ("wc", 128),
           ("r1", 32), ("rb1", E8), ("ew1", 256), ("eb1", 512)]
WC, NWC = columns(WC_SPEC)
WD_SPEC = [("q1", 128), ("k1", 128), ("v1", 128), ("bq1", 1), ("bk1", 1), ("bv1", 32), ("u1", 128),
           ("bu1", 32), ("rel", 2 * HEADS * NPIX),
           ("gw1", 256), ("gb1", 1), ("w11", E16 * HID), ("w21", E16 * C), ("b21", E16)]
WD, NWD = columns(WD_SPEC)


def metaformer(nc, x_in, cst_in, wa_in, wb_in, wc_in, wd_in, out):
    fp32 = mybir.dt.float32
    ALU, ACT, AX = mybir.AluOpType, mybir.ActivationFunctionType, mybir.AxisListType

    with ExitStack() as ctx:
        widths = {}

        def sb(name, cols, parts=P):
            t = ctx.enter_context(nc.sbuf_tensor(name, [parts, cols], fp32))
            widths[name] = cols
            return t

        def view(t, col, dims, p0=0, n=P):
            if isinstance(t, tuple):
                t, first = t
                col = first + col
            w = t.shape[1]
            return bass.AP(t, p0 * w + col, [[w, n]] + [list(d) for d in dims])

        sem = lambda name: ctx.enter_context(nc.semaphore(name))

        XT, XN, XNC, YC = sb("XT", F), sb("XN", F), sb("XNC", F), sb("YC", F)
        SQ = sb("SQ", F)
        XC = sb("XC", F)
        cst, wa, wb, wc, wd = sb("cst", NCST), sb("wa", NWA), sb("wb", NWB), sb("wc", NWC), sb("wd", NWD)
        s16, mean, var, sd, rstd = (sb(n, NT) for n in ("s16", "mean", "var", "sd", "rstd"))
        QC, VT = sb("QC", HEADS * F), sb("VT", F)
        SM = sb("SM", 3 * 512)
        mx, nm, rs, den, e0 = (sb(n, 64) for n in ("mx", "nm", "rs", "den", "e0"))
        bqh = sb("bqh", HEADS)
        spare = sb("spare", 32)
        LG, EX, KEY, S1, S2, GW = (sb(n, NT * E8) for n in ("LG", "EX", "KEY", "S1", "S2", "GW"))
        PR = sb("PR", 2 * 512)
        Y2 = sb("Y2", F)
        XP, SQP = sb("XP", NBH * PADW * PADW), sb("SQP", NBH * PADW * PADW)
        RINGS = sb("RINGS", (DRING + ARING) * F)
        PTS, YG = (RINGS, 0), (RINGS, TURNED * 512)
        KM = (RINGS, TURNED * 512 + 10 * NPIX)
        ACC, D2 = sb("ACC", F), sb("D2", F)
        w2s, wsd = sb("w2s", 1), sb("wsd", 1)
        PB, MK, GX = sb("PB", NPIX), sb("MK", NPIX), sb("GX", NPIX)
        top8 = sb("top8", 8)
        GT = sb("GT", NPIX)
        PA = sb("PA", P, C + 1)
        HB = sb("HB", P)
        OC = sb("OC", P, C)
        OB = sb("OB", B * C)
        c1, c2 = sb("c1", 4), sb("c2", 4)
        base = sb("base", 2 * 3 * KG)
        OM = sb("OM", NT * 3 * KG)
        AM = sb("AM", NT * KG)
        LXA = sb("LXA", NT * KG * NA)
        VB = sb("VB", B * G * CG * NR)
        DXY, HXY, HXT = (RINGS, 0), (RINGS, 2 * HATS), (RINGS, 4 * HATS)
        HYM = sb("HYM", 2 * HYN)
        PRD = sb("PRD", 2 * K9 * 288)
        SMP, SMT = sb("SMP", F), sb("SMT", F)
        XW = (PRD, 0)

        bank = [ctx.enter_context(nc.psum_tensor(f"bank{i}", [P, 512], fp32)) for i in range(8)]

        def cv(name, n, c=0, p0=0, np_=P):
            return cst[p0:p0 + np_, CST[name] + c:CST[name] + c + n]

        ident = cv("ident", 128)

        x_in_s, cst_s, wa_s, wb_s, wc_s, wd_s, out_s = (
            sem(n) for n in ("x_loaded", "cst_loaded", "wa_loaded", "wb_loaded", "wc_loaded", "wd_loaded", "stored"))
        dve_chain, pool_set, km_clear = sem("dve_chain"), sem("pool_set"), sem("km_clear")
        x_turned, x_ready = sem("x_turned"), sem("x_ready")
        var_ready, sd_ready, xn_ready, xn_turned, xnc_ready = (
            sem(n) for n in ("var_ready", "sd_ready", "xn_ready", "xn_turned", "xnc_ready"))
        q_done, kv_done, qc_ready, kv_ready, bqh_ready = (
            sem(n) for n in ("q_done", "kv_done", "qc_ready", "kv_ready", "bqh_ready"))
        scored, nm_ready, p_ready, pt_done, pts_ready, av_done = (
            sem(n) for n in ("scored", "nm_ready", "p_ready", "pt_done", "pts_ready", "av_done"))
        yg_ready, yg_turned = sem("yg_ready"), sem("yg_turned")
        pad_asked, pad_ready = sem("pad_asked"), sem("pad_ready")
        att_ready, att_turned, attc_ready, u_done = (
            sem(n) for n in ("att_ready", "att_turned", "attc_ready", "u_done"))
        routed, gate_ready, ex_ready, expert_done, expert_used = (
            sem(n) for n in ("routed", "gate_ready", "ex_ready", "expert_done", "expert_used"))
        gw_ready, gw_turned, gwt_ready, bias_done, bias_ready, xt_biased = (
            sem(n) for n in ("gw_ready", "gw_turned", "gwt_ready", "bias_done", "bias_ready", "xt_biased"))
        xp_ready, sqp_ready, cor_done, cor_used, l2_done, d2_ready, l2_ready, lo_ready, lo_turned = (
            sem(n) for n in ("xp_ready", "sqp_ready", "cor_done", "cor_used", "l2_done", "d2_ready", "l2_ready",
                             "lo_ready", "lo_turned"))
        d_ready, d_used, a_ready, a_used, drained = (
            sem(n) for n in ("d_ready", "d_used", "a_ready", "a_used", "drained"))
        ec_logits, ec_max, ec_exp, g_ready, g_turned, gt_ready, pooled, pa_ready = (
            sem(n) for n in ("ec_logits", "ec_max", "ec_exp", "g_ready", "g_turned", "gt_ready", "pooled", "pa_ready"))
        h_done, h_ready, o_done, oc_ready, oc_turned, ob_ready, ec_out = (
            sem(n) for n in ("h_done", "h_ready", "o_done", "oc_ready", "oc_turned", "ob_ready", "ec_out"))
        om_done, om_used, val_done, val_used, lxa_ready, xw_ready, smt_ready = (
            sem(n) for n in ("om_done", "om_used", "val_done", "val_used", "lxa_ready", "xw_ready", "smt_ready"))
        dxy_ready, abs_done, hxy_ready, hym_ready, hx_turned, hxt_ready, prod_done, prod_used = (
            sem(n) for n in ("dxy_ready", "abs_done", "hxy_ready", "hym_ready", "hx_turned", "hxt_ready", "prod_done",
                             "prod_used"))
        paired = sem("paired")
        smp_ready, smp_turned, sc_ready, y_done, sum_ready, sum_done, cen_ready, sq_ready, sq_done, bn_ready, dc_ready = (
            sem(n) for n in ("smp_ready", "smp_turned", "sc_ready", "y_done", "sum_ready", "sum_done", "cen_ready",
                             "sq_ready", "sq_done", "bn_ready", "dc_ready"))
        bnv_ready, bsd_ready, yc_ready, wc_done = (sem(n) for n in ("bnv_ready", "bsd_ready", "yc_ready", "wc_done"))
        fin_turned, fin_ready = sem("fin_turned"), sem("fin_ready")

        block = ctx.enter_context(nc.Block())

        def after(eng, s, value):
            if not isinstance(value, int) or value > 0:
                eng.wait_ge(s, value)

        @block.sync
        def _(sp):
            for bh in range(NBH):
                sp.dma_start(XC[:, bh * NPIX:(bh + 1) * NPIX],
                             x_in[bh * B4:(bh + 1) * B4].rearrange("b c y x -> (b c) (y x)")).then_inc(x_in_s, 16)
            sp.dma_start(cst[:, :], cst_in).then_inc(cst_s, 16)
            sp.dma_start(wa[:, :], wa_in).then_inc(wa_s, 16)
            sp.dma_start(wb[:, :], wb_in).then_inc(wb_s, 16)
            sp.dma_start(wc[:, :], wc_in).then_inc(wc_s, 16)
            sp.dma_start(wd[:, :], wd_in).then_inc(wd_s, 16)
            sp.wait_ge(fin_ready, 1)
            for bh in range(NBH):
                sp.dma_start(out[bh * B4:(bh + 1) * B4].rearrange("b c y x -> (b c) (y x)"),
                             XC[:, bh * NPIX:(bh + 1) * NPIX]).then_inc(out_s, 16)
            sp.wait_ge(out_s, 16 * NBH)

        @block.gpsimd
        def _(pool):
            pool.memset(view(KM, 0, [[1, B * NPIX]]), 0.0).then_inc(km_clear, 1)
            pool.memset(XP[:, :], 0.0).then_inc(pool_set, 1)
            pool.memset(SQP[:, :], 0.0).then_inc(pool_set, 1)
            pool.wait_ge(pool_set, 2)
            pool.memset(PA[C:C + 1, :], 1.0).then_inc(pool_set, 1)

            def distances(turn, b, half):
                n = 2 * b + half
                after(pool, hxy_ready, 16 * turn + n - 1)
                o = half * HATS
                pool.tensor_tensor(view(DXY, o, [[WW, KG * NA], [1, WW]]),
                                   view(LXA, n * KG * NA, [[1, KG * NA], [0, WW]]),
                                   view(cst, CST["xg"], [[0, KG * NA], [1, WW]]), ALU.subtract)
                pool.tensor_tensor(view(DXY, o + HXN, [[NR, KG], [1, NR]]),
                                   view(OM, n * 3 * KG + KG, [[1, KG], [0, NR]]),
                                   view(cst, CST["yg"], [[0, KG], [1, NR]]), ALU.subtract).then_inc(dxy_ready, 1)

            def masked(turn, b, half):
                n = 2 * b + half
                pool.wait_ge(hxy_ready, 16 * turn + n + 1)
                after(pool, prod_used, 9 * (16 * turn + n - 1))
                pool.tensor_tensor(view(HYM, half * HYN, [[NR, KG], [1, NR]]),
                                   view(HXY, half * HATS + HXN, [[NR, KG], [1, NR]]),
                                   view(OM, n * 3 * KG + 2 * KG, [[1, KG], [0, NR]]), ALU.mult).then_inc(hym_ready, 1)

            def bias(turn):
                pool.wait_ge(bias_ready, turn + 1)
                pool.tensor_tensor(XT[:, :], XT[:, :], SQ[:, :], ALU.add).then_inc(xt_biased, 1)

            pool.wait_ge(pool_set, 3)
            bias(0)
            for turn in range(2):
                pool.wait_ge(lxa_ready, turn + 1)
                for half in range(2):
                    distances(turn, 0, half)

                def pairs(b, half):
                    n = 2 * b + half
                    pool.wait_ge(prod_used, 9 * (16 * turn + n) + 2 * PAIRS)
                    first, second = (view(PRD, (half * K9 + k) * 288, [[1, PAIRS * 288]]) for k in (0, PAIRS))
                    pool.tensor_tensor(second, second, first, ALU.add).then_inc(paired, 1)

                def body(b, ahead):
                    masked(turn, b, 1)
                    if ahead >= 1:
                        distances(turn, b + 1, 1)
                    pairs(b, 0)
                    if ahead >= 1:
                        masked(turn, b + 1, 0)
                    if ahead == 2:
                        distances(turn, b + 2, 0)
                    pairs(b, 1)
                masked(turn, 0, 0)
                distances(turn, 1, 0)
                body(0, 2)
                with pool.Fori(1, B - 2) as b:
                    body(b, 2)
                body(B - 2, 1)
                body(B - 1, 0)
            pool.wait_ge(prod_done, 2 * 16 * K9)
            pool.memset(view(KM, 0, [[1, B * NPIX]]), 0.0).then_inc(km_clear, 1)
            bias(1)

        @block.scalar
        def _(act):
            tables = [0]

            def table(func):
                act.activation(spare[:, tables[0]:tables[0] + 1], cv("one", 1), func)
                tables[0] += 1

            def norm(n, eps, padded=False, then=None):
                table(ACT.Sqrt)
                act.wait_ge(var_ready, n + 1)
                act.activation(sd[:, :], var[:, :], ACT.Sqrt, scale=1.0 / C, bias=cv(eps, 1)).then_inc(sd_ready, 1)
                if then is not None:
                    table(then)
                act.wait_ge(xn_turned, n + 1)
                if not padded:
                    act.activation(XNC[:, :], bank[0][:, :], ACT.Copy).then_inc(xnc_ready, 1)
                    return
                act.wait_ge(pool_set, 3)
                for bh in range(NBH):
                    ins = act.activation(view(XP, bh * PADW * PADW + PADW + 1, [[PADW, HH], [1, WW]]),
                                         view(bank[0], bh * NPIX, [[WW, HH], [1, WW]]), ACT.Copy)
                ins.then_inc(xp_ready, 1)
                for bh in range(NBH):
                    ins = act.activation(view(SQP, bh * PADW * PADW + PADW + 1, [[PADW, HH], [1, WW]]),
                                         view(bank[0], bh * NPIX, [[WW, HH], [1, WW]]), ACT.Square)
                ins.then_inc(sqp_ready, 1)
                ins = None

            def attend(first, steps):
                for s in range(first, first + steps + 4):
                    if s < first + steps:
                        act.wait_ge(nm_ready, s + 1)
                        for j in range(2):
                            u = 2 * (s - first) + j
                            at = (s % 3) * 512 + j * 256
                            ins = act.activation(SM[:, at:at + 256], SM[:, at:at + 256], ACT.Exp, scale=-1.0,
                                                 bias=nm[:, u:u + 1], accum_out=rs[:, u:u + 1])
                        ins.then_inc(p_ready, 1)
                    if s - 4 >= first and s % 4 == 3:
                        gr = s // 4 - 1
                        act.wait_ge(av_done, gr + 1)
                        act.activation(view(YG, (gr - first // 4) * NPIX, [[1, NPIX]]), bank[1 + 2 * (gr % 2)][:, 0:NPIX],
                                       ACT.Copy).then_inc(yg_ready, 1)

            def top2(turn):
                act.wait_ge(gate_ready, turn + 1)
                act.activation(EX[:, :], LG[:, :], ACT.Exp).then_inc(ex_ready, 1)
                act.wait_ge(gw_turned, turn + 1)
                act.activation(GT[:, 0:P], bank[6][:, 0:P], ACT.Copy).then_inc(gwt_ready, 1)
                act.wait_ge(bias_done, turn + 1)
                act.activation(SQ[:, :], bank[7][:, :], ACT.Copy).then_inc(bias_ready, 1)

            def expert_choice(turn):
                act.wait_ge(ec_max, turn + 1)
                act.activation(PB[:, :], MK[:, :], ACT.Exp, bias=nm[:, 0:1], accum_out=rs[:, 0:1]).then_inc(ec_exp, 1)
                table(ACT.Gelu)
                act.wait_ge(g_turned, turn + 1)
                act.activation(GT[:, :], bank[2][:, 0:NPIX], ACT.Copy).then_inc(gt_ready, 1)
                act.wait_ge(pooled, turn + 1)
                act.activation(PA[0:C, :], bank[3][0:C, 0:P], ACT.Copy).then_inc(pa_ready, 1)
                act.wait_ge(h_done, turn + 1)
                act.activation(HB[:, :], bank[4][:, 0:P], ACT.Gelu).then_inc(h_ready, 1)

            act.wait_ge(cst_s, 16)
            norm(0, "eps6", then=ACT.Exp)
            act.wait_ge(wa_s, 16)
            act.wait_ge(q_done, 1)
            act.activation(QC[:, 0:F], bank[1][:, :], ACT.Identity, bias=wa[:, WA["bq0"]:WA["bq0"] + 1]).then_inc(qc_ready, 1)
            attend(0, 8)
            act.wait_ge(pad_asked, 1)
            act.activation(e0[:, 0:NT], den[:, 0:NT], ACT.Exp).then_inc(pad_ready, 1)
            norm(1, "eps5", then=ACT.Exp)
            top2(0)

            norm(2, "eps6", padded=True)
            act.wait_ge(wb_s, 16)
            act.wait_ge(xp_ready, 1)

            def distances(i):
                k = 0
                for n in range(UNITS):
                    if ON_DVE[n]:
                        continue
                    tap, j = divmod(n, 4)
                    after(act, a_used, ACT_UNITS * i + k + 1 - ARING)
                    slot = (DRING + k % ARING) * F
                    w_at = WB["lw"] + i * UNITS + n
                    act.activation(view(RINGS, slot, [[NPIX, NBH], [WW, HH], [1, WW]]),
                                   view(XP, tap // 3 * PADW + tap % 3, [[PADW * PADW, NBH], [PADW, HH], [1, WW]]),
                                   ACT.Abs, scale=-1.0, bias=view(wb, w_at, [[1, 1]])).then_inc(a_ready, 1)
                    k += 1

            distances(0)
            with act.Fori(1, 8) as i:
                distances(i)
            table(ACT.Sqrt)
            act.wait_ge(d2_ready, 1)
            act.activation(D2[:, :], D2[:, :], ACT.Sqrt).then_inc(l2_ready, 1)
            norm(3, "eps5", then=ACT.Exp)
            expert_choice(0)

            norm(4, "eps6")

            def hats(turn, b, half):
                n = 2 * b + half
                o = half * HATS
                act.wait_ge(dxy_ready, 16 * turn + n + 1)
                act.activation(view(DXY, o, [[1, HATS]]), view(DXY, o, [[1, HATS]]), ACT.Abs).then_inc(abs_done, 1)
                act.wait_ge(abs_done, 16 * turn + n + 1)
                after(act, hx_turned, 3 * (16 * turn + n - 1))
                after(act, hym_ready, 16 * turn + n - 1)
                act.activation(view(HXY, o, [[1, HATS]]), view(DXY, o, [[1, HATS]]), ACT.Relu, scale=-1.0,
                               bias=cv("one", 1)).then_inc(hxy_ready, 1)

            def turned(turn, b, half):
                n = 2 * b + half
                after(act, prod_done, 9 * (16 * turn + n - 1))
                for g in range(3):
                    act.wait_ge(hx_turned, 3 * (16 * turn + n) + g + 1)
                    o = (half * K9 + 3 * g) * P
                    act.activation(view(HXT, o, [[1, 3 * P]]), bank[(3 * half + g) % 2][:, 0:3 * P], ACT.Copy).then_inc(hxt_ready, 1)

            def deform(turn, src, src_ready, count):
                act.wait_ge(src_ready, count)
                after(act, val_done, 6 * turn)
                for bh in range(NBH):
                    for g in range(G):
                        ins = act.activation(view(XW, bh * NR * P + g * NA * WW, [[P, NR], [WW, NA], [1, WW]]),
                                             view(src, bh * NPIX, [[WW, NR], [7 * WW, NA], [1, WW]]), ACT.Copy)
                ins.then_inc(xw_ready, 1)
                hats(turn, 0, 0)
                hats(turn, 0, 1)

                def body(b):
                    for half in range(2):
                        turned(turn, b, half)
                        hats(turn, b + 1, half)
                body(0)
                with act.Fori(1, B - 1) as b:
                    body(b)
                for half in range(2):
                    turned(turn, B - 1, half)
                act.wait_ge(smp_turned, turn + 1)
                act.activation(YC[:, :], bank[0][:, :], ACT.Copy).then_inc(sc_ready, 1)
                act.wait_ge(cen_ready, turn + 1)
                act.activation(D2[:, :], ACC[:, :], ACT.Square, accum_out=c2[:, 0:1]).then_inc(sq_ready, 1)
                table(ACT.Sqrt)
                act.wait_ge(bnv_ready, turn + 1)
                act.activation(c2[:, 1:2], c2[:, 2:3], ACT.Sqrt).then_inc(bsd_ready, 1)
                act.wait_ge(bn_ready, turn + 1)
                if turn == 0:
                    act.activation(YC[:, :], ACC[:, :], ACT.Relu, scale=c1[:, 2:3],
                                   bias=wc[:, WC["beta"]:WC["beta"] + 1]).then_inc(dc_ready, 1)

            act.wait_ge(wc_s, 16)
            deform(0, XNC, xnc_ready, 4)
            deform(1, YC, dc_ready, 1)
            norm(5, "eps5", then=ACT.Exp)
            top2(1)

            norm(6, "eps6", then=ACT.Exp)
            act.wait_ge(q_done, 2)
            act.wait_ge(bqh_ready, 1)
            for h in range(HEADS):
                ins = act.activation(QC[:, h * F:(h + 1) * F], bank[1][:, :], ACT.Identity, scale=cv("hm", 1, h),
                                     bias=bqh[:, h:h + 1])
            ins.then_inc(qc_ready, 1)
            attend(8, 32)
            act.wait_ge(att_turned, 1)
            act.activation(YC[:, :], bank[0][:, :], ACT.Copy).then_inc(attc_ready, 1)
            norm(7, "eps5", then=ACT.Exp)
            expert_choice(1)

        @block.vector
        def _(dve):
            links = [0]

            def link(ins):
                links[0] += 1
                ins.then_inc(dve_chain, 1)
                dve.wait_ge(dve_chain, links[0])

            def tiles(t, col=0):
                return view(t, col, [[C, NT], [1, C]])

            def per_tile(t):
                return view(t, 0, [[1, NT], [0, C]])

            def norm(n):
                link(dve.tensor_reduce(s16[:, :], tiles(XT), AX.X, ALU.add))
                link(dve.tensor_scalar(mean[:, :], s16[:, :], 1.0 / C, None, ALU.mult))
                link(dve.tensor_tensor(tiles(XN), tiles(XT), per_tile(mean), ALU.subtract))
                link(dve.tensor_tensor(SQ[:, :], XN[:, :], XN[:, :], ALU.mult))
                dve.tensor_reduce(var[:, :], tiles(SQ), AX.X, ALU.add).then_inc(var_ready, 1)
                dve.wait_ge(sd_ready, n + 1)
                link(dve.reciprocal(rstd[:, :], sd[:, :]))
                dve.tensor_tensor(tiles(XN), tiles(XN), per_tile(rstd), ALU.mult).then_inc(xn_ready, 1)
                dve.wait_ge(xn_ready, n + 1)

            def keys(w, bias, clear):
                dve.wait_ge(km_clear, clear)
                for b in range(B):
                    bh, b4 = divmod(b, B4)
                    dve.tensor_scalar(view(KM, b * NPIX, [[1, NPIX]], C * b4, C),
                                      view(bank[2], bh * NPIX, [[1, NPIX]], C * b4, C),
                                      view(w, bias, [[1, 1]], C * b4, C), None, ALU.add)

            def attend(first, steps, l3):
                for s in range(first, first + steps + 2):
                    if s < first + steps:
                        r = s - first
                        dve.wait_ge(scored, s + 1)
                        after(dve, pt_done, s - 2)
                        for j in range(2):
                            u = 2 * r + j
                            at = (s % 3) * 512 + j * 256
                            if l3:
                                add = view(wd, WD["rel"] + (j * HEADS + r % HEADS) * NPIX, [[1, NPIX]])
                            else:
                                add = cv("mask", NPIX, j * NPIX)
                            start = -NEG if l3 else cv("floor", 1, j)
                            ins = dve.tensor_tensor_reduce(SM[:, at:at + 256], bank[4 + s % 2][:, j * 256:j * 256 + 256],
                                                           add, -1.0, start, ALU.add, ALU.min, nm[:, u:u + 1])
                        ins.then_inc(nm_ready, 1)
                    if s - 2 >= first:
                        dve.wait_ge(pt_done, s - 1)
                        after(dve, av_done, (s - 2) // 4 - 1)
                        dve.tensor_copy(view(PTS, (s - 2) % TURNED * 512, [[1, 512]]),
                                        bank[6 + s % 2][:, :]).then_inc(pts_ready, 1)

            def top2(turn, rb, w):
                by_e = lambda t: view(t, 0, [[E8, NT], [1, E8]])
                one = lambda t: view(t, 0, [[1, NT], [0, E8]])
                keys = view(cst, CST["keys"], [[0, NT], [1, E8]])
                dve.wait_ge(routed, turn + 1)
                link(dve.tensor_tensor(by_e(LG), view(bank[1], 0, [[E8, NT], [1, E8]]),
                                       view(w, rb, [[0, NT], [1, E8]]), ALU.add))
                link(dve.tensor_reduce(s16[:, :], by_e(LG), AX.X, ALU.max))
                dve.tensor_tensor(by_e(LG), by_e(LG), one(s16), ALU.subtract).then_inc(gate_ready, 1)
                dve.wait_ge(gate_ready, turn + 1)
                link(dve.scalar_tensor_tensor(by_e(KEY), by_e(LG), 0.0, keys, ALU.is_ge, ALU.mult))
                link(dve.tensor_reduce(s16[:, :], by_e(KEY), AX.X, ALU.max))
                link(dve.tensor_tensor(by_e(S1), by_e(KEY), one(s16), ALU.is_equal))
                link(dve.scalar_tensor_tensor(by_e(KEY), by_e(S1), -BIG, by_e(LG), ALU.mult, ALU.add))
                link(dve.tensor_reduce(s16[:, :], by_e(KEY), AX.X, ALU.max))
                link(dve.tensor_tensor(by_e(S2), by_e(KEY), one(s16), ALU.is_equal))
                link(dve.tensor_tensor(by_e(KEY), by_e(S2), keys, ALU.mult))
                link(dve.tensor_reduce(s16[:, :], by_e(KEY), AX.X, ALU.max))
                link(dve.tensor_tensor(by_e(S2), by_e(KEY), one(s16), ALU.is_equal))
                link(dve.tensor_tensor(by_e(S1), by_e(S1), by_e(S2), ALU.add))
                dve.wait_ge(ex_ready, turn + 1)
                link(dve.tensor_tensor(by_e(GW), by_e(S1), by_e(EX), ALU.mult))
                link(dve.tensor_reduce(s16[:, :], by_e(GW), AX.X, ALU.add))
                link(dve.reciprocal(mean[:, :], s16[:, :]))
                dve.tensor_tensor(by_e(GW), by_e(GW), one(mean), ALU.mult).then_inc(gw_ready, 1)
                dve.wait_ge(gw_ready, turn + 1)
                for s in range(NT // 2):
                    dve.wait_ge(expert_done, turn * 8 + s + 1)
                    dve.tensor_tensor(view(PR, (s % 2) * 512, [[256, 2], [E8, C], [1, E8]]),
                                      view(bank[2 + s % 4], 0, [[256, 2], [E8, C], [1, E8]]),
                                      view(GW, (s // 4 * 8 + s % 4) * E8, [[4 * E8, 2], [0, C], [1, E8]]), ALU.mult).then_inc(expert_used, 1)
                    dve.wait_ge(expert_used, turn * 8 + s + 1)
                    ins = dve.tensor_reduce(view(Y2, (s // 4 * 8 + s % 4) * C, [[4 * C, 2], [1, C]]),
                                            view(PR, (s % 2) * 512, [[256, 2], [E8, C], [1, E8]]), AX.X, ALU.add)
                link(ins)
                dve.wait_ge(xt_biased, turn + 1)
                link(dve.tensor_tensor(XT[:, :], XT[:, :], Y2[:, :], ALU.add))

            def expert_choice(turn, w, at):
                dve.wait_ge(ec_logits, turn + 1)
                link(dve.tensor_scalar(MK[:, :], bank[1][:, 0:NPIX], w[:, at["gb"]:at["gb"] + 1], None, ALU.add))
                link(dve.tensor_reduce(mx[:, 0:1], MK[:, :], AX.X, ALU.max))
                dve.tensor_scalar(nm[:, 0:1], mx[:, 0:1], -1.0, None, ALU.mult).then_inc(ec_max, 1)
                dve.wait_ge(ec_exp, turn + 1)
                link(dve.reciprocal(den[:, 0:1], rs[:, 0:1]))
                link(dve.tensor_scalar(PB[:, :], PB[:, :], den[:, 0:1], None, ALU.mult))
                link(dve.max(top8[:, :], PB[:, :]))
                link(dve.match_replace(out=MK[:, :], in_to_replace=top8[:, :], in_values=PB[:, :], imm_value=-1.0))
                dve.scalar_tensor_tensor(GX[:, :], MK[:, :], 0.0, PB[:, :], ALU.is_lt, ALU.mult).then_inc(g_ready, 1)
                dve.wait_ge(o_done, turn + 1)
                dve.tensor_tensor(view(OC, 0, [[1, E16], [E16, B]], n=C),
                                  view(bank[5], 0, [[B, E16], [1, B]], n=C),
                                  view(w, at["b2"], [[1, E16], [0, B]], n=C), ALU.add).then_inc(oc_ready, 1)
                dve.wait_ge(oc_turned, turn + 1)
                dve.tensor_tensor(view(OB, 0, [[C, B], [1, C]]), view(bank[6], 0, [[0, B], [1, C]]),
                                  view(cst, CST["ecmask"], [[1, B], [0, C]]), ALU.mult).then_inc(ob_ready, 1)
                dve.wait_ge(ec_out, turn + 1)
                link(dve.tensor_tensor(XT[:, :], XT[:, :], bank[7][:, :], ALU.add))

            dve.wait_ge(x_turned, 1)
            link(dve.tensor_copy(XT[:, :], bank[0][:, :]))

            norm(0)
            dve.wait_ge(wa_s, 16)
            dve.wait_ge(kv_done, 1)
            keys(wa, WA["bk0"], 1)
            dve.tensor_tensor(tiles(VT), tiles(bank[3]), view(wa, WA["bv0"], [[0, NT], [1, C]]), ALU.add)\
               .then_inc(kv_ready, 1)
            attend(0, 8, False)
            dve.wait_ge(p_ready, 8)
            dve.tensor_scalar(den[:, 0:NT], nm[:, 0:NT], 0.0, None, ALU.min).then_inc(pad_asked, 1)
            dve.wait_ge(pad_ready, 1)
            by_unit = lambda t, o=0: view(t, o, [[8, 2], [1, 2], [2, 4]])
            link(dve.tensor_tensor(by_unit(e0), by_unit(e0), view(cst, CST["npad"], [[0, 2], [1, 2], [0, 4]]), ALU.mult))
            link(dve.tensor_tensor(e0[:, 0:NT], e0[:, 0:NT], rs[:, 0:NT], ALU.add))
            link(dve.reciprocal(view(den, 0, [[8, 2], [4, 2], [1, 4]]), by_unit(e0)))
            dve.wait_ge(yg_turned, 1)
            link(dve.tensor_tensor(tiles(Y2), tiles(bank[0]), per_tile(den), ALU.mult))
            link(dve.tensor_tensor(XT[:, :], XT[:, :], Y2[:, :], ALU.add))
            norm(1)
            dve.wait_ge(wb_s, 16)
            top2(0, WB["rb0"], wb)

            norm(2)
            link(dve.tensor_tensor(view(RINGS, 0, [[1, 288]]), wb[:, WB["wf"]:WB["wf"] + 288],
                                   wb[:, WB["wf"]:WB["wf"] + 288], ALU.mult))
            link(dve.tensor_reduce(w2s[:, :], view(RINGS, 0, [[1, 288]]), AX.X, ALU.add))
            link(dve.tensor_tensor(view(RINGS, 0, [[C, 9], [1, C]]), view(wb, WB["wf"], [[C, 9], [1, C]]),
                                   view(cst, CST["dtaps"], [[1, 9], [0, C]]), ALU.mult))
            link(dve.tensor_reduce(wsd[:, :], view(RINGS, 0, [[1, 288]]), AX.X, ALU.add))
            dve.wait_ge(xp_ready, 1)

            def maxima(i):
                k = 0
                for n in range(UNITS):
                    if not ON_DVE[n]:
                        continue
                    tap, j = divmod(n, 4)
                    after(dve, d_used, DVE_UNITS * i + k + 1 - DRING)
                    w_at = WB["lw"] + i * UNITS + n
                    dve.tensor_scalar(view(RINGS, (k % DRING) * F, [[NPIX, NBH], [WW, HH], [1, WW]]),
                                      view(XP, tap // 3 * PADW + tap % 3, [[PADW * PADW, NBH], [PADW, HH], [1, WW]]),
                                      view(wb, w_at, [[1, 1]]), None, ALU.max).then_inc(d_ready, 1)
                    k += 1

            def drain(i, b):
                dve.wait_ge(d_used, DVE_UNITS * (i + 1))
                dve.wait_ge(a_used, ACT_UNITS * (i + 1))
                dve.wait_ge(drained, i + 1)
                dve.scalar_tensor_tensor(ACC[:, :], bank[2 + b][:, :], view(cst, CST["sel"] + i, [[1, 1]]), ACC[:, :],
                                         ALU.mult, ALU.add).then_inc(drained, 1)

            maxima(0)
            dve.wait_ge(cor_done, 1)
            dve.tensor_scalar(ACC[:, :], bank[4][:, :], wsd[:, 0:1], None, ALU.subtract).then_inc(drained, 1)
            with dve.Fori(0, 3) as m:
                maxima(2 * m + 1)
                drain(2 * m, 0)
                maxima(2 * m + 2)
                drain(2 * m + 1, 1)
            maxima(7)
            drain(6, 0)
            dve.wait_ge(l2_done, 1)
            link(dve.tensor_scalar(D2[:, :], bank[5][:, :], -2.0, w2s[:, 0:1], ALU.mult, ALU.add))
            dve.tensor_scalar(D2[:, :], D2[:, :], 1e-12, None, ALU.max).then_inc(d2_ready, 1)
            drain(7, 1)
            dve.wait_ge(drained, 9)
            dve.wait_ge(l2_ready, 1)
            link(dve.tensor_tensor(ACC[:, :], D2[:, :], ACC[:, :], ALU.subtract))
            dve.tensor_tensor(ACC[:, :], ACC[:, :], D2[:, :], ALU.subtract).then_inc(lo_ready, 1)
            dve.wait_ge(lo_turned, 1)
            for g in range(4):
                ins = dve.tensor_tensor(view(XT, g * P, [[C, B4], [1, C]]), view(XT, g * P, [[C, B4], [1, C]]),
                                        view(bank[0], g * P, [[1, B4], [B4, C]]), ALU.add)
            link(ins)
            norm(3)
            expert_choice(0, wb, {"gb": WB["gb0"], "b2": WB["b20"]})

            norm(4)
            dve.wait_ge(wc_s, 16)
            link(dve.tensor_tensor(view(base, 0, [[3 * KG, 2], [1, 3 * KG]]), view(cst, CST["geo"], [[3 * KG, 2], [1, 3 * KG]]),
                                   view(wc, WC["bom"], [[0, 2], [1, 3 * KG]]), ALU.add))

            def points(turn):
                for g in range(4):
                    bh, half = divmod(g, 2)
                    dve.wait_ge(om_done, 4 * turn + g + 1)
                    dve.tensor_tensor(view(OM, (8 * bh + half) * 3 * KG, [[2 * 3 * KG, B4], [1, 3 * KG]]),
                                      view(bank[1 + g % 2], 0, [[3 * KG, B4], [1, 3 * KG]]),
                                      view(base, half * 3 * KG, [[0, B4], [1, 3 * KG]]), ALU.add).then_inc(om_used, 1)
                dve.wait_ge(om_used, 4 * turn + 4)
                lx = view(OM, 0, [[3 * KG, NT], [1, KG]])
                ly = view(OM, KG, [[3 * KG, NT], [1, KG]])
                am = view(AM, 0, [[KG, NT], [1, KG]])
                link(dve.tensor_scalar(am, ly, 8.0, None, ALU.is_ge))
                link(dve.scalar_tensor_tensor(view(LXA, 0, [[2 * KG, NT], [2, KG]]), am, BIG, lx, ALU.mult, ALU.add))
                link(dve.scalar_tensor_tensor(ly, am, -7.0, ly, ALU.mult, ALU.add))
                link(dve.tensor_scalar(am, am, -1.0, 1.0, ALU.mult, ALU.add))
                dve.scalar_tensor_tensor(view(LXA, 1, [[2 * KG, NT], [2, KG]]), am, BIG, lx, ALU.mult, ALU.add)\
                   .then_inc(lxa_ready, 1)
                n = 0
                for bh in range(NBH):
                    for r0 in range(0, NR, 4):
                        rows = min(4, NR - r0)
                        dve.wait_ge(val_done, 6 * turn + n + 1)
                        ins = dve.tensor_tensor(view(VB, bh * B4 * 288 + r0, [[1, rows], [NR, P]]),
                                                view(bank[3 + n % 2], 0, [[P, rows], [1, P]]),
                                                view(cst, CST["gmask"], [[0, rows], [1, P]]), ALU.mult)
                        ins.then_inc(val_used, 1)
                        n += 1

            def sample(turn, b, half):
                n = 2 * b + half
                dve.wait_ge(hym_ready, 16 * turn + n + 1)
                after(dve, smp_ready, 16 * turn + n - 1)
                after(dve, paired, 16 * turn + n - 1)
                for k in range(K9):
                    idx = 9 * (16 * turn + n) + k
                    dve.wait_ge(prod_done, idx + 1)
                    dve.tensor_tensor(view(PRD, (half * K9 + k) * 288, [[72, G], [NR, CG], [1, NR]]),
                                      view(bank[2 + (9 * half + k) % LOOK], 0, [[72, G], [NR, CG], [1, NR]]),
                                      view(HYM, half * HYN + k * G * NR, [[NR, G], [0, CG], [1, NR]]), ALU.mult).then_inc(prod_used, 1)

            def sums(turn, b, half):
                n = 2 * b + half
                dve.wait_ge(prod_used, 9 * (16 * turn + n) + 9)
                dve.wait_ge(paired, 16 * turn + n + 1)
                dve.tensor_reduce(view(SMP, n * C, [[1, C]]),
                                  view(PRD, (half * K9 + PAIRS) * 288, [[NR, C], [288, K9 - PAIRS], [1, NR]]), AX.XY,
                                  ALU.add).then_inc(smp_ready, 1)

            def deform(turn):
                points(turn)
                sample(turn, 0, 0)
                sample(turn, 0, 1)
                sums(turn, 0, 0)
                with dve.Fori(1, B) as b:
                    sample(turn, b, 0)
                    sums(turn, b - 1, 1)
                    sample(turn, b, 1)
                    sums(turn, b, 0)
                sums(turn, B - 1, 1)
                dve.wait_ge(smp_ready, 16 * turn + 16)
                for bh in range(NBH):
                    ins = dve.tensor_copy(view(SMT, bh * NPIX, [[P, 2], [C, B4], [1, C]]),
                                          view(SMP, bh * NPIX, [[C, 2], [2 * C, B4], [1, C]]))
                ins.then_inc(smt_ready, 1)
                dve.wait_ge(y_done, turn + 1)
                dve.tensor_reduce(c1[:, 0:1], bank[1][:, :], AX.X, ALU.add).then_inc(sum_ready, 1)
                dve.wait_ge(sum_done, turn + 1)
                link(dve.tensor_copy(c1[:, 1:2], bank[2][:, 0:1]))
                dve.tensor_scalar(ACC[:, :], bank[1][:, :], c1[:, 1:2], None, ALU.subtract).then_inc(cen_ready, 1)
                dve.wait_ge(sq_done, turn + 1)
                dve.tensor_scalar(c2[:, 2:3], bank[3][:, 0:1], 1e-5, None, ALU.add).then_inc(bnv_ready, 1)
                dve.wait_ge(bsd_ready, turn + 1)
                link(dve.reciprocal(c1[:, 3:4], c2[:, 1:2]))
                link(dve.tensor_tensor(c1[:, 2:3], c1[:, 3:4], wc[:, WC["gamma"]:WC["gamma"] + 1], ALU.mult))

            deform(0)
            dve.tensor_copy(c1[:, 0:1], c1[:, 2:3]).then_inc(bn_ready, 1)
            deform(1)
            link(dve.tensor_scalar(ACC[:, :], ACC[:, :], c1[:, 2:3], wc[:, WC["beta"]:WC["beta"] + 1], ALU.mult, ALU.add))
            dve.tensor_tensor(YC[:, :], ACC[:, :], XNC[:, :], ALU.add).then_inc(yc_ready, 1)
            dve.tensor_copy(c1[:, 0:1], c1[:, 2:3]).then_inc(bn_ready, 1)
            dve.wait_ge(wc_done, 1)
            link(dve.tensor_tensor(XT[:, :], XT[:, :], bank[4][:, :], ALU.add))
            norm(5)
            top2(1, WC["rb1"], wc)

            norm(6)
            dve.wait_ge(wd_s, 16)
            dve.tensor_scalar(bqh[:, :], cv("hm", HEADS), wd[:, WD["bq1"]:WD["bq1"] + 1], None, ALU.mult)\
               .then_inc(bqh_ready, 1)
            dve.wait_ge(kv_done, 2)
            keys(wd, WD["bk1"], 2)
            dve.tensor_tensor(tiles(VT), tiles(bank[3]), view(wd, WD["bv1"], [[0, NT], [1, C]]), ALU.add)\
               .then_inc(kv_ready, 1)
            attend(8, 32, True)
            dve.wait_ge(p_ready, 40)
            link(dve.reciprocal(den[:, :], rs[:, :]))
            dve.wait_ge(yg_turned, 2)
            for b in range(B):
                ins = dve.tensor_tensor(view(Y2, (b // B4 * 8 + b % B4) * C, [[B4 * C, 2], [HC, HEADS], [1, HC]]),
                                        view(bank[4 + b // 2], b % 2 * 256, [[P, 2], [C + HC, HEADS], [1, HC]]),
                                        view(den, b * 8, [[1, 2], [2, HEADS], [0, HC]]), ALU.mult)
            ins.then_inc(att_ready, 1)
            link(dve.tensor_tensor(tiles(XT), tiles(XT), view(wd, WD["bu1"], [[0, NT], [1, C]]), ALU.add))
            dve.wait_ge(u_done, 1)
            link(dve.tensor_tensor(XT[:, :], XT[:, :], bank[2][:, :], ALU.add))
            norm(7)
            expert_choice(1, wd, {"gb": WD["gb1"], "b2": WD["b21"]})
            dve.tensor_copy(XT[:, 0:1], XT[:, 0:1]).then_inc(x_ready, 1)
            dve.wait_ge(fin_turned, 1)
            dve.tensor_copy(XC[:, :], bank[0][:, :]).then_inc(fin_ready, 1)

        @block.tensor
        def _(pe):
            def turn4(dst, src, s):
                for g in range(4):
                    ins = pe.transpose(dst[:, g * P:(g + 1) * P], src[:, g * P:(g + 1) * P], ident)
                ins.then_inc(s, 1)

            def norm(n):
                pe.wait_ge(xn_ready, n + 1)
                turn4(bank[0], XN, xn_turned)

            def w_(t, at, n=P, p0=0, np_=P):
                return t[p0:p0 + np_, at:at + n]

            def project(turn, t, at):
                pe.wait_ge(xnc_ready, {0: 1, 1: 6}[turn])
                pe.matmul(bank[1][:, :], w_(t, at["q"]), XNC[:, :], start=True, stop=True).then_inc(q_done, 1)
                pe.matmul(bank[2][:, :], w_(t, at["k"]), XNC[:, :], start=True, stop=True)
                for g in range(4):
                    ins = pe.matmul(bank[3][:, g * P:(g + 1) * P], XNC[:, g * P:(g + 1) * P], w_(t, at["v"]),
                                    start=True, stop=True)
                ins.then_inc(kv_done, 1)
                pe.wait_ge(qc_ready, turn + 1)
                pe.wait_ge(kv_ready, turn + 1)

            def attend(first, steps, l3):
                def image(s):
                    return divmod(s - first, HEADS) if l3 else (s - first, 0)

                def scores(s):
                    after(pe, nm_ready, s - 1)
                    b, h = image(s)
                    bh, b4 = divmod(b, B4)
                    for j in range(2):
                        q0 = h * F + bh * NPIX + j * P
                        ins = pe.matmul(bank[4 + s % 2][:, j * 256:j * 256 + 256],
                                        QC[:, q0:q0 + P], view(KM, b * NPIX, [[1, NPIX]]), start=True, stop=True)
                    ins.then_inc(scored, 1)

                def turn(s):
                    pe.wait_ge(p_ready, s + 1)
                    after(pe, pts_ready, s - 1)
                    for j in range(2):
                        for kt in range(2):
                            ins = pe.transpose(bank[6 + s % 2][:, (2 * kt + j) * P:(2 * kt + j + 1) * P],
                                               view(SM, (s % 3) * 512 + (2 * j + kt) * P, [[1, P]]), ident)
                    ins.then_inc(pt_done, 1)

                def values(gr):
                    pe.wait_ge(pts_ready, 4 * gr + 4)
                    after(pe, yg_ready, gr - 1)
                    for kt in range(2):
                        for i in range(4):
                            s = 4 * gr + i
                            bh, b4 = divmod(image(s)[0], B4)
                            ins = pe.matmul(bank[1 + 2 * (gr % 2)][32 * i:32 * i + 32, 0:NPIX],
                                            view(VT, ((2 * bh + kt) * B4 + b4) * C, [[1, C]]),
                                            view(PTS, s % TURNED * 512 + kt * NPIX, [[1, NPIX]]),
                                            start=(kt == 0), stop=(kt == 1), skip_group_check=True)
                    ins.then_inc(av_done, 1)

                for s in range(first, first + steps + 4):
                    if s < first + steps:
                        scores(s)
                    if first <= s - 2 < first + steps:
                        turn(s - 2)
                    if s - 3 >= first and (s - 3) % 4 == 3:
                        values((s - 3) // 4)

            def top2(turn, w, at, nx):
                pe.wait_ge(xnc_ready, nx)
                for g in range(4):
                    ins = pe.matmul(bank[1][:, g * 32:g * 32 + 32], XNC[:, g * P:(g + 1) * P], w_(w, at["r"], 32),
                                    start=True, stop=True)
                ins.then_inc(routed, 1)
                for s in range(NT // 2):
                    after(pe, expert_used, 8 * turn + s - 3)
                    bk = bank[2 + s % 4]
                    bh, b4 = divmod(s, B4)
                    for j in range(2):
                        g = 2 * bh + j
                        ins = pe.matmul(bk[:, j * 256:j * 256 + 256], XNC[C * b4:C * b4 + C, g * P:(g + 1) * P],
                                        w[C * b4:C * b4 + C, at["ew"]:at["ew"] + 256], start=True, stop=True)
                    ins.then_inc(expert_done, 1)
                    if s == 3:
                        pe.wait_ge(gw_ready, turn + 1)
                        pe.transpose(bank[6][:, 0:P], GW[:, :], ident).then_inc(gw_turned, 1)
                        pe.wait_ge(gwt_ready, turn + 1)
                        pe.matmul(bank[7][:, :], GT[:, 0:P], w[:, at["eb"]:at["eb"] + 512], start=True,
                                  stop=True).then_inc(bias_done, 1)

            def expert_choice(turn, w, at, nx):
                pe.wait_ge(xnc_ready, nx)
                for bh in range(NBH):
                    ins = pe.matmul(bank[1][:, 0:NPIX], w_(w, at["gw"] + bh * P), XNC[:, bh * NPIX:(bh + 1) * NPIX],
                                    start=(bh == 0), stop=(bh == NBH - 1))
                ins.then_inc(ec_logits, 1)
                pe.wait_ge(g_ready, turn + 1)
                for half in range(2):
                    ins = pe.transpose(bank[2][:, half * P:(half + 1) * P], GX[:, half * P:(half + 1) * P], ident)
                ins.then_inc(g_turned, 1)
                pe.wait_ge(gt_ready, turn + 1)
                for b in range(B):
                    for half in range(2):
                        t = b // 4 * 8 + half * 4 + b % 4
                        ins = pe.matmul(bank[3][0:C, b * E16:(b + 1) * E16], XN[:, t * C:(t + 1) * C],
                                        GT[:, half * P + b * E16:half * P + (b + 1) * E16],
                                        start=(half == 0), stop=(half == 1))
                ins.then_inc(pooled, 1)
                pe.wait_ge(pa_ready, turn + 1)
                pe.wait_ge(pool_set, 3)
                for e in range(E16):
                    ins = pe.matmul(bank[4][:, e * B:(e + 1) * B], w[0:C + 1, at["w1"] + e * HID:at["w1"] + (e + 1) * HID],
                                    view(PA, e, [[E16, B]], n=C + 1), start=True, stop=True)
                ins.then_inc(h_done, 1)
                pe.wait_ge(h_ready, turn + 1)
                for e in range(E16):
                    ins = pe.matmul(bank[5][0:C, e * B:(e + 1) * B], w[:, at["w2"] + e * C:at["w2"] + (e + 1) * C],
                                    HB[:, e * B:(e + 1) * B], start=True, stop=True)
                ins.then_inc(o_done, 1)
                pe.wait_ge(oc_ready, turn + 1)
                pe.transpose(bank[6][:, 0:C], OC[:, :], cst[0:C, CST["ident"]:CST["ident"] + C]).then_inc(oc_turned, 1)
                pe.wait_ge(ob_ready, turn + 1)
                for g in range(4):
                    bh, half = divmod(g, 2)
                    ins = pe.matmul(bank[7][:, g * P:(g + 1) * P], GX[:, half * P:(half + 1) * P],
                                    OB[:, bh * P:(bh + 1) * P], start=True, stop=True)
                ins.then_inc(ec_out, 1)

            pe.wait_ge(x_in_s, 16 * NBH)
            pe.wait_ge(cst_s, 16)
            turn4(bank[0], XC, x_turned)

            norm(0)
            pe.wait_ge(wa_s, 16)
            project(0, wa, {"q": WA["q0"], "k": WA["k0"], "v": WA["v0"]})
            attend(0, 8, False)
            pe.wait_ge(yg_ready, 2)
            for g in range(4):
                ins = pe.transpose(bank[0][:, g * P:(g + 1) * P], view(YG, g * P, [[1, P]]), ident)
            ins.then_inc(yg_turned, 1)
            norm(1)
            pe.wait_ge(wb_s, 16)
            top2(0, wb, {"r": WB["r0"], "eb": WB["eb0"], "ew": WB["ew0"]}, 2)

            norm(2)
            pe.wait_ge(xp_ready, 1)

            def tap_of(t, tap):
                return view(t, tap // 3 * PADW + tap % 3, [[PADW * PADW, NBH], [PADW, HH], [1, WW]])

            first = [min(n // 4 for n in range(UNITS) if ON_DVE[n] and n % 4 == j) for j in range(4)]
            last = [max(n // 4 for n in range(UNITS) if ON_DVE[n] and n % 4 == j) for j in range(4)]
            for n in range(UNITS):
                if ON_DVE[n]:
                    tap, j = divmod(n, 4)
                    ins = pe.matmul(bank[4][32 * j:32 * j + 32, :], cv("nrep", 32), tap_of(XP, tap),
                                    start=(tap == first[j]), stop=(tap == last[j]), skip_group_check=True)
            ins.then_inc(cor_done, 1)

            def sums(i, b):
                after(pe, drained, i)
                kd = ka = 0
                for n in range(UNITS):
                    tap, j = divmod(n, 4)
                    if ON_DVE[n]:
                        pe.wait_ge(d_ready, DVE_UNITS * i + kd + 1)
                        slot, rep, used = (kd % DRING) * F, "rep2", d_used
                        kd += 1
                    else:
                        pe.wait_ge(a_ready, ACT_UNITS * i + ka + 1)
                        slot, rep, used = (DRING + ka % ARING) * F, "rep1", a_used
                        ka += 1
                    pe.matmul(bank[2 + b][32 * j:32 * j + 32, :], cv(rep, 32), RINGS[:, slot:slot + F],
                              start=(tap == 0), stop=(tap == 8), skip_group_check=True).then_inc(used, 1)

            sums(0, 0)
            sums(1, 1)
            with pe.Fori(1, 4) as m:
                sums(2 * m, 0)
                sums(2 * m + 1, 1)
            pe.wait_ge(sqp_ready, 1)
            for tap in range(9):
                pe.matmul(bank[5][:, :], w_(wb, WB["w9"] + tap * P), tap_of(XP, tap), start=(tap == 0), stop=False)
            for tap in range(9):
                ins = pe.matmul(bank[5][:, :], cv("nhalf", P), tap_of(SQP, tap), start=False, stop=(tap == 8))
            ins.then_inc(l2_done, 1)
            pe.wait_ge(lo_ready, 1)
            turn4(bank[0], ACC, lo_turned)
            norm(3)
            expert_choice(0, wb, {"gw": WB["gw0"], "w1": WB["w10"], "w2": WB["w20"]}, 3)

            norm(4)
            pe.wait_ge(wc_s, 16)

            def turn_hats(turn, b, half, groups=range(3)):
                n = 2 * b + half
                pe.wait_ge(hxy_ready, 16 * turn + n + 1)
                for g in groups:
                    after(pe, hxt_ready, 3 * (16 * turn + n) + g - 1)
                    bk = bank[(3 * half + g) % 2]
                    for k in range(3):
                        at = half * HATS + (3 * g + k) * P
                        ins = pe.transpose(bk[:, k * P:(k + 1) * P], view(HXY, at, [[1, P]]), ident)
                    ins.then_inc(hx_turned, 1)

            def products(turn, b, half, more):
                n = 2 * b + half
                for k in range(K9):
                    if more and k in TURN_AT:
                        turn_hats(turn, b + half, 1 - half, TURN_AT[k])
                    if k % 3 == 0:
                        pe.wait_ge(hxt_ready, 3 * (16 * turn + n) + k // 3 + 1)
                    after(pe, prod_used, 9 * (16 * turn + n) + k + 1 - LOOK)
                    pe.matmul(bank[2 + (9 * half + k) % LOOK][:, 0:288], view(HXT, (half * K9 + k) * P, [[1, P]]),
                              view(VB, b * 288, [[1, 288]]), start=True, stop=True).then_inc(prod_done, 1)

            def deform(turn, src):
                for g in range(4):
                    after(pe, om_used, 4 * turn + g - 1)
                    pe.matmul(bank[1 + g % 2][:, 0:B4 * 3 * KG], src[:, g * P:(g + 1) * P], w_(wc, WC["om"], B4 * 3 * KG),
                              start=True, stop=True).then_inc(om_done, 1)
                n = 0
                pe.wait_ge(xw_ready, turn + 1)
                for bh in range(NBH):
                    for r0 in range(0, NR, 4):
                        rows = min(4, NR - r0)
                        after(pe, val_used, 6 * turn + n - 1)
                        bk = bank[3 + n % 2]
                        pe.matmul(bk[:, 0:rows * P], cst[0:1, CST["ones"]:CST["ones"] + P],
                                  wc[0:1, WC["bval"]:WC["bval"] + rows * P], start=True, stop=False, skip_group_check=True)
                        for r in range(rows):
                            ins = pe.matmul(bk[:, r * P:(r + 1) * P],
                                            view(XW, (bh * NR + r0 + r) * P, [[1, P]]),
                                            w_(wc, WC["val"]), start=False, stop=True, skip_group_check=True)
                        ins.then_inc(val_done, 1)
                        n += 1
                turn_hats(turn, 0, 0)
                pe.wait_ge(val_used, 6 * turn + 6)

                def body(b, more):
                    products(turn, b, 0, True)
                    products(turn, b, 1, more)
                body(0, True)
                with pe.Fori(1, B - 1) as b:
                    body(b, True)
                body(B - 1, False)
                pe.wait_ge(smt_ready, turn + 1)
                turn4(bank[0], SMT, smp_turned)
                pe.wait_ge(sc_ready, turn + 1)
                pe.matmul(bank[1][:, :], w_(wc, WC["wo"]), YC[:, :], start=True, stop=True).then_inc(y_done, 1)
                pe.wait_ge(sum_ready, turn + 1)
                pe.matmul(bank[2][:, 0:1], cv("avg", P), c1[:, 0:1], start=True, stop=True).then_inc(sum_done, 1)
                pe.wait_ge(sq_ready, turn + 1)
                pe.matmul(bank[3][:, 0:1], cv("avg", P), c2[:, 0:1], start=True, stop=True).then_inc(sq_done, 1)

            pe.wait_ge(xnc_ready, 4)
            deform(0, XNC)
            pe.wait_ge(dc_ready, 1)
            deform(1, YC)
            pe.wait_ge(yc_ready, 1)
            for g in range(4):
                ins = pe.matmul(bank[4][:, g * P:(g + 1) * P], YC[:, g * P:(g + 1) * P], w_(wc, WC["wc"]),
                                start=True, stop=True)
            ins.then_inc(wc_done, 1)
            norm(5)
            top2(1, wc, {"r": WC["r1"], "eb": WC["eb1"], "ew": WC["ew1"]}, 5)

            norm(6)
            pe.wait_ge(wd_s, 16)
            project(1, wd, {"q": WD["q1"], "k": WD["k1"], "v": WD["v1"]})
            attend(8, 32, True)
            pe.wait_ge(yg_ready, 10)
            pe.wait_ge(pts_ready, 40)
            for g in range(16):
                ins = pe.transpose(bank[4 + g // 4][:, g % 4 * P:(g % 4 + 1) * P], view(YG, g * P, [[1, P]]), ident)
            ins.then_inc(yg_turned, 1)
            pe.wait_ge(att_ready, 1)
            turn4(bank[0], Y2, att_turned)
            pe.wait_ge(attc_ready, 1)
            for g in range(4):
                ins = pe.matmul(bank[2][:, g * P:(g + 1) * P], YC[:, g * P:(g + 1) * P], w_(wd, WD["u1"]),
                                start=True, stop=True)
            ins.then_inc(u_done, 1)
            norm(7)
            expert_choice(1, wd, {"gw": WD["gw1"], "w1": WD["w11"], "w2": WD["w21"]}, 7)
            pe.wait_ge(x_ready, 1)
            turn4(bank[0], XT, fin_turned)


def _constants(np):
    c = np.zeros((P, NCST), np.float32)

    def put(name, a):
        c[:, CST[name]:CST[name] + a.shape[1]] = a

    p = np.arange(P)
    pix = np.arange(NPIX)
    put("ident", np.eye(P))
    ky, kx = pix // WW, pix % WW
    for half in range(2):
        qy, qx = half * 8 + p // WW, p % WW
        near = (abs(qy[:, None] - ky) <= 3) & (abs(qx[:, None] - kx) <= 3)
        c[:, CST["mask"] + half * NPIX:CST["mask"] + (half + 1) * NPIX] = np.where(near, 0.0, -BIG)
        npad = 49 - near.sum(1)
        c[:, CST["floor"] + half] = np.where(npad > 0, 0.0, -NEG)
        c[:, CST["npad"] + half] = npad
        geo = np.zeros((P, 3, K9, G))
        k = np.arange(K9)
        geo[:, 0] = (qx[:, None] + k % 3 - 1)[:, :, None]
        geo[:, 1] = (qy[:, None] + k // 3 - 1)[:, :, None]
        c[:, CST["geo"] + half * 3 * KG:CST["geo"] + (half + 1) * 3 * KG] = geo.reshape(P, -1)
    put("one", np.ones((P, 1)))
    put("eps6", np.full((P, 1), 1e-6))
    put("eps5", np.full((P, 1), 1e-5))
    put("hm", (p[:, None] % C // HC == np.arange(HEADS)) * np.float32(HC ** -0.5))
    put("ones", np.ones((P, 512)))
    put("xg", np.tile(np.arange(WW), (P, 1)))
    put("yg", np.tile(np.arange(NR), (P, 1)))
    put("gmask", p[:, None] // 32 == p[None] % C // CG)
    rep = p[:, None] // C == p[None, :32] % B4
    put("rep1", rep)
    put("rep2", 2.0 * rep)
    put("nrep", -1.0 * rep)
    put("nhalf", -0.5 * (p[:, None] // C == p[None] % B4))
    put("avg", (p[:, None] % C == p[None] % C) / (B * NPIX))
    put("ecmask", p[:, None] // E16 == np.arange(B))
    put("sel", p[:, None] // B4 % 8 == np.arange(8))
    put("keys", np.tile(E8 - np.arange(E8), (P, 1)))
    dt = np.array([[ON_DVE[4 * t + j] for t in range(9)] for j in range(4)])
    put("dtaps", dt[p // 32])
    return c


def _layouts(np, a):
    f = np.float32

    def blocks(w):
        r = np.zeros((P, B4 * w.shape[1]), f)
        for b in range(B4):
            r[b * C:(b + 1) * C, b * w.shape[1]:(b + 1) * w.shape[1]] = w
        return r

    def rows(v):
        return np.tile(v.reshape(1, -1), (P, 1))

    def pack(spec, n, parts):
        out = np.zeros((P, n), f)
        for name, width in spec.items():
            v = parts[name]
            out[0:v.shape[0], width:width + v.shape[1]] = v
        return out

    def top2(i):
        l = f"L{i}_ffn_"
        ew = a[l + "expert_w"].transpose(1, 2, 0).reshape(C, C * E8)
        eb = np.zeros((NT, E8, NT, C), f)
        for t in range(NT):
            eb[t, :, t] = a[l + "expert_b"]
        return blocks(a[l + "router_w"]), rows(a[l + "router_b"]), np.tile(ew, (B4, 1)), eb.reshape(P, NT * C)

    def ec(i):
        l = f"L{i}_ffn_"
        gw = np.zeros((P, NBH, B, E16), f)
        for b in range(B):
            gw[b % B4 * C:(b % B4 + 1) * C, b // B4, b] = a[l + "gate_w"].T
        gb = np.tile(a[l + "gate_b"], B).reshape(P, 1)
        w1 = a[l + "weight1"].transpose(1, 0, 2).reshape(C + 1, E16 * HID)
        w2 = a[l + "weight2"][:, :HID].transpose(1, 0, 2).reshape(HID, E16 * C)
        b2 = a[l + "weight2"][:, HID].T
        return gw.reshape(P, NBH * P), gb, w1, w2, b2

    col4 = lambda v: np.tile(v, B4).reshape(P, 1)
    wa = pack(WA, NWA, {"q0": blocks(a["L0_conv_Wq"].T), "k0": blocks(a["L0_conv_Wk"].T),
                        "v0": blocks(a["L0_conv_Wv"].T), "bq0": col4(a["L0_conv_bq"]), "bk0": col4(a["L0_conv_bk"]),
                        "bv0": rows(a["L0_conv_bv"])})
    w = a["L1_conv_W"].reshape(C, C, 9)
    lw = w.reshape(4, 8, C, 9).transpose(2, 1, 3, 0).reshape(C, 288)
    wf = np.repeat(w.transpose(0, 2, 1).reshape(C, 288), B4, axis=0)
    w9 = np.zeros((B4, C, 9, C, B4), f)
    for b in range(B4):
        w9[b, :, :, :, b] = w.transpose(1, 2, 0)
    r0, rb0, ew0, eb0 = top2(0)
    gw, gb, w1, w2, b2 = ec(1)
    wb = pack(WB, NWB, {"r0": r0, "rb0": rb0, "ew0": ew0, "eb0": eb0, "lw": np.tile(lw, (B4, 1)), "wf": wf,
                        "w9": w9.reshape(P, 9 * P), "gw0": gw, "gb0": gb, "w10": w1, "w20": w2, "b20": b2})
    kinds = np.array([[g * 3 * K9 + (2 * k + t if t < 2 else 2 * K9 + k) for k in range(K9) for g in range(G)]
                      for t in range(3)]).reshape(-1)
    r1, rb1, ew1, eb1 = top2(2)
    wc = pack(WC, NWC, {"om": blocks(a["L2_conv_Wom"][:, kinds]), "bom": rows(a["L2_conv_bom"][kinds]),
                        "val": blocks(a["L2_conv_Wv"]), "bval": np.tile(a["L2_conv_bv"].reshape(1, -1), (1, 16)),
                        "wo": blocks(a["L2_conv_Wo"]), "gamma": col4(a["L2_conv_gamma"]),
                        "beta": col4(a["L2_conv_beta"]), "wc": blocks(a["L2_conv_Wc"].T),
                        "r1": r1, "rb1": rb1, "ew1": ew1, "eb1": eb1})
    p, pix = np.arange(P), np.arange(NPIX)
    span = 2 * WW - 1
    rel = np.zeros((P, 2, HEADS, NPIX), f)
    for half in range(2):
        q = half * P + p
        at = (pix[None] // WW - q[:, None] // WW + HH - 1) * span + pix[None] % WW - q[:, None] % WW + WW - 1
        rel[:, half] = a["L3_conv_pos_enc"][:, at].transpose(1, 0, 2)
    gw, gb, w1, w2, b2 = ec(3)
    wd = pack(WD, NWD, {"q1": blocks(a["L3_conv_Wq"].T), "k1": blocks(a["L3_conv_Wk"].T),
                        "v1": blocks(a["L3_conv_Wv"].T), "bq1": col4(a["L3_conv_bq"]), "bk1": col4(a["L3_conv_bk"]),
                        "bv1": rows(a["L3_conv_bv"]), "u1": blocks(a["L3_conv_Wu"].T), "bu1": rows(a["L3_conv_bu"]),
                        "rel": rel.reshape(P, -1), "gw1": gw, "gb1": gb, "w11": w1, "w21": w2, "b21": b2})
    return wa, wb, wc, wd


def kernel(**inputs):
    import numpy as _np
    import concourse.bacc as _bacc
    from concourse import mybir as _mybir
    from concourse.bass_utils import run_bass_kernel_spmd as _run

    a = {k: _np.asarray(v) for k, v in inputs.items()}
    arrays = {"x": _np.ascontiguousarray(a["x"]), "cst": _constants(_np)}
    arrays.update(zip(("wa", "wb", "wc", "wd"), _layouts(_np, a)))
    nc = _bacc.Bacc("TRN2", target_bir_lowering=False, num_devices=1)
    args = [nc.dram_tensor(f"in_{n}", v.shape, _mybir.dt.float32, kind="ExternalInput").ap() for n, v in arrays.items()]
    out = nc.dram_tensor("out_y", a["x"].shape, _mybir.dt.float32, kind="ExternalOutput").ap()
    metaformer(nc, *args, out)
    r = _run(nc, [{f"in_{n}": v for n, v in arrays.items()}], core_ids=[0])
    return r.results[0]["out_y"]
```

```python
import concourse.bass as bass
from concourse import mybir
from contextlib import ExitStack

B, C, HH, WW = 8, 32, 16, 16
NPIX = HH * WW
P = 128
B4 = P // C
NBH = B // B4
NT = B * NPIX // P
F = NT * C
E8 = 8
E16, HID = 16, 128
HEADS, HC = 4, 8
G, CG, K9 = 4, 8, 9
NA, NR = 2, 9
PADW = HH + 2
KG = K9 * G
HXN, HYN = KG * NA * WW, KG * NR
HATS = HXN + HYN
BIG = 1e30
NEG = -3e38
TURNED = 8
TURN_AT = {2: (0,), 5: (1,), 8: (2,)}
ACT_KEYS = (2, 1)
NORM_BANKS = (7, 3, 1, 5, 5, 5, 1, 5)
FILL, FILL_EC, FILL_BN, FILL_TAIL, FILL_KEYS, FILL_GATES = (17, 23, 40, 20, 12, 22, 40, 20), 16, 6, 22, 3, 11
LOOK = 6
PAIRS = 3

SHARED = 7
D_TAPS, A_TAPS = (0, 2, 4, 6, 8), (1, 3, 5)
TAPS = (0, 1, 2, SHARED, 4, 3, 6, 5, 8)
UNITS = [(tap, j) for tap in TAPS for j in range(4)]
ON_DVE = [tap in D_TAPS or (tap == SHARED and j < 2) for tap, j in UNITS]
DVE_UNITS = sum(ON_DVE)
ACT_UNITS = len(UNITS) - DVE_UNITS
DRING, ARING = DVE_UNITS // 2, ACT_UNITS // 2


def columns(spec):
    at, out = 0, {}
    for name, n in spec:
        out[name] = at
        at += n
    return out, at


HEAD = 128 + 3
CST_SPEC = [("ident", 128), ("one", 1), ("eps6", 1), ("eps5", 1),
            ("mask", 512), ("floor", 2), ("npad", 2), ("hm", HEADS), ("ones", P), ("geo", 2 * 3 * KG), ("xg", WW), ("yg", NR),
            ("gmask", 128), ("rep1", 60), ("rep2", 60), ("nrep", 128), ("nhalf", 128), ("avg", 128),
            ("ecmask", B), ("keys", E8), ("dtaps", 9)]
CST, NCST = columns(CST_SPEC)
WA_SPEC = [("q0", 128), ("k0", 128), ("v0", 128), ("bq0", 1), ("bk0", 1), ("bv0", 32)]
WA, NWA = columns(WA_SPEC)
WB_SPEC = [("r0", 32), ("rb0", E8), ("ew0", B4 * 256), ("eb0", 512),
           ("lw", 288), ("wf", 288), ("w9", 9 * 128),
           ("gw0", 256), ("gb0", 1), ("w10", E16 * HID), ("w20", E16 * C), ("b20", E16)]
WB, NWB = columns(WB_SPEC)
WC_SPEC = [("om", B4 * 3 * KG), ("bom", 3 * KG), ("val", 128), ("bval", 512), ("wo", 128),
           ("gamma", 1), ("beta", 1), ("wc", 128),
           ("r1", 32), ("rb1", E8), ("ew1", B4 * 256), ("eb1", 512)]
WC, NWC = columns(WC_SPEC)
WD_SPEC = [("q1", 128), ("k1", 128), ("v1", 128), ("bq1", 1), ("bk1", 1), ("bv1", 32), ("u1", 128),
           ("bu1", 32), ("rel", 2 * HEADS * NPIX),
           ("gw1", 256), ("gb1", 1), ("w11", E16 * HID), ("w21", E16 * C), ("b21", E16)]
WD, NWD = columns(WD_SPEC)


def metaformer(nc, x_in, cst_in, wa_in, wb_in, wc_in, wd_in, out):
    fp32 = mybir.dt.float32
    ALU, ACT, AX = mybir.AluOpType, mybir.ActivationFunctionType, mybir.AxisListType

    with ExitStack() as ctx:
        widths = {}

        def sb(name, cols, parts=P):
            t = ctx.enter_context(nc.sbuf_tensor(name, [parts, cols], fp32))
            widths[name] = cols
            return t

        def view(t, col, dims, p0=0, n=P):
            if isinstance(t, tuple):
                t, first = t
                col = first + col
            w = t.shape[1]
            return bass.AP(t, p0 * w + col, [[w, n]] + [list(d) for d in dims])

        sem = lambda name: ctx.enter_context(nc.semaphore(name))

        XT, XN, XNC, YC = sb("XT", F), sb("XN", F), sb("XNC", F), sb("YC", F)
        SQ = sb("SQ", F)
        XC = sb("XC", F)
        cst, wa, wb, wc, wd = sb("cst", NCST), sb("wa", NWA), sb("wb", NWB), sb("wc", NWC), sb("wd", NWD)
        s16, mean, var, sd, rstd = (sb(n, NT) for n in ("s16", "mean", "var", "sd", "rstd"))
        QC, VT = sb("QC", HEADS * F), sb("VT", F)
        SM = sb("SM", 3 * 512)
        mx, nm, rs, den, e0 = (sb(n, 64) for n in ("mx", "nm", "rs", "den", "e0"))
        bqh = sb("bqh", HEADS)
        spare = sb("spare", 32)
        LG, EX, KEY, S1, S2, GW = (sb(n, NT * E8) for n in ("LG", "EX", "KEY", "S1", "S2", "GW"))
        PR = sb("PR", 3 * 512)
        Y2 = sb("Y2", F)
        XP, SQP = sb("XP", NBH * PADW * PADW), sb("SQP", NBH * PADW * PADW)
        BX = sb("BX", NBH * PADW * WW)
        RINGS = sb("RINGS", (DRING + ARING) * F)
        PTS, YG = (RINGS, 0), (RINGS, TURNED * 512)
        KM = (RINGS, TURNED * 512 + 10 * NPIX)
        ACC, D2 = sb("ACC", F), sb("D2", F)
        w2s, wsd = sb("w2s", 1), sb("wsd", 1)
        PB, MK, GX = sb("PB", NPIX), sb("MK", NPIX), sb("GX", NPIX)
        top8 = sb("top8", 8)
        GT = sb("GT", NPIX)
        HB, HT, PA = (QC, 0), (QC, F), (QC, 2 * F)
        OC = sb("OC", P, C)
        OB = sb("OB", B * C)
        c1, c2 = sb("c1", 4), sb("c2", 4)
        base = sb("base", 2 * 3 * KG)
        OM = sb("OM", NT * 3 * KG)
        AM = (BX, 0)
        LXA = sb("LXA", NT * KG * NA)
        VB = sb("VB", B * G * CG * NR)
        DXY, HXY, HXT = (RINGS, 0), (RINGS, 2 * HATS), (RINGS, 4 * HATS)
        HYM = sb("HYM", 2 * HYN)
        PRD = sb("PRD", 2 * K9 * 288)
        SMT = sb("SMT", F)
        XW = (PRD, 0)

        bank = [ctx.enter_context(nc.psum_tensor(f"bank{i}", [P, 512], fp32)) for i in range(8)]

        scores_bank = (bank[4], bank[5], bank[2])

        def cv(name, n, c=0, p0=0, np_=P):
            return cst[p0:p0 + np_, CST[name] + c:CST[name] + c + n]

        ident = cv("ident", 128)

        head_s = sem("head_loaded")
        x_in_s, cst_s, wa_s, wb_s, wc_s, wd_s, out_s = (
            sem(n) for n in ("x_loaded", "cst_loaded", "wa_loaded", "wb_loaded", "wc_loaded", "wd_loaded", "stored"))
        dve_chain, pool_set, km_clear = sem("dve_chain"), sem("pool_set"), sem("km_clear")
        x_turned, x_ready = sem("x_turned"), sem("x_ready")
        var_ready, sd_ready, xn_ready, xn_turned, xnc_ready = (
            sem(n) for n in ("var_ready", "sd_ready", "xn_ready", "xn_turned", "xnc_ready"))
        q_done, k_done, v_done, qc_ready, keys_ready, vt_ready, bqh_ready = (
            sem(n) for n in ("q_done", "k_done", "v_done", "qc_ready", "keys_ready", "vt_ready", "bqh_ready"))
        act_keys_ready = sem("act_keys_ready")
        scored, nm_ready, p_ready, pt_done, pts_ready, av_done = (
            sem(n) for n in ("scored", "nm_ready", "p_ready", "pt_done", "pts_ready", "av_done"))
        yg_ready, yg_turned = sem("yg_ready"), sem("yg_turned")
        pad_asked, pad_ready = sem("pad_asked"), sem("pad_ready")
        att_ready, att_turned, attc_ready, u_done = (
            sem(n) for n in ("att_ready", "att_turned", "attc_ready", "u_done"))
        routed, gate_ready, ex_ready, expert_done, expert_used = (
            sem(n) for n in ("routed", "gate_ready", "ex_ready", "expert_done", "expert_used"))
        halved = sem("halved")
        pa_set, h_turned, ht_ready = sem("pa_set"), sem("h_turned"), sem("ht_ready")
        gw_ready, gw_turned, gwt_ready, bias_done, bias_ready, xt_biased = (
            sem(n) for n in ("gw_ready", "gw_turned", "gwt_ready", "bias_done", "bias_ready", "xt_biased"))
        xp_ready, dsum_ready, box_ready, pool_chain, l2_done, d2_ready, l2_ready, lo_ready, lo_turned = (
            sem(n) for n in ("xp_ready", "dsum_ready", "box_ready", "pool_chain", "l2_done", "d2_ready", "l2_ready",
                             "lo_ready", "lo_turned"))
        d_ready, d_used, a_ready, a_used = (
            sem(n) for n in ("d_ready", "d_used", "a_ready", "a_used"))
        ec_logits, ec_max, ec_exp, g_ready, g_turned, gt_ready, pooled, pa_ready = (
            sem(n) for n in ("ec_logits", "ec_max", "ec_exp", "g_ready", "g_turned", "gt_ready", "pooled", "pa_ready"))
        h_done, h_ready, o_done, oc_ready, oc_turned, ob_ready, ec_out = (
            sem(n) for n in ("h_done", "h_ready", "o_done", "oc_ready", "oc_turned", "ob_ready", "ec_out"))
        om_done, om_used, val_done, val_used, lxa_ready, xw_ready = (
            sem(n) for n in ("om_done", "om_used", "val_done", "val_used", "lxa_ready", "xw_ready"))
        dxy_ready, abs_done, hxy_ready, hym_ready, hx_turned, hxt_ready, prod_done, prod_used = (
            sem(n) for n in ("dxy_ready", "abs_done", "hxy_ready", "hym_ready", "hx_turned", "hxt_ready", "prod_done",
                             "prod_used"))
        paired = sem("paired")
        smp_ready, smp_turned, sc_ready, mean_done, mean_ready, sum_ready, sum_done, cen_ready, sq_ready, sq_done, bn_ready, dc_ready = (
            sem(n) for n in ("smp_ready", "smp_turned", "sc_ready", "mean_done", "mean_ready", "sum_ready", "sum_done", "cen_ready",
                             "sq_ready", "sq_done", "bn_ready", "dc_ready"))
        bnv_ready, bsd_ready, yc_ready, wc_done = (sem(n) for n in ("bnv_ready", "bsd_ready", "yc_ready", "wc_done"))
        fin_turned, fin_ready = sem("fin_turned"), sem("fin_ready")

        block = ctx.enter_context(nc.Block())

        def after(eng, s, value):
            if not isinstance(value, int) or value > 0:
                eng.wait_ge(s, value)

        @block.sync
        def _(sp):
            for bh in range(NBH):
                sp.dma_start(XC[:, bh * NPIX:(bh + 1) * NPIX],
                             x_in[bh * B4:(bh + 1) * B4].rearrange("b c y x -> (b c) (y x)")).then_inc(x_in_s, 16)
            sp.dma_start(cst[:, HEAD:], cst_in[:, HEAD:]).then_inc(cst_s, 16)
            sp.dma_start(wa[:, :], wa_in).then_inc(wa_s, 16)
            sp.dma_start(wb[:, :], wb_in).then_inc(wb_s, 16)
            sp.dma_start(wc[:, :], wc_in).then_inc(wc_s, 16)
            sp.dma_start(wd[:, :], wd_in).then_inc(wd_s, 16)
            for bh in range(NBH):
                sp.wait_ge(fin_ready, bh + 1)
                sp.dma_start(out[bh * B4:(bh + 1) * B4].rearrange("b c y x -> (b c) (y x)"),
                             XC[:, bh * NPIX:(bh + 1) * NPIX]).then_inc(out_s, 16)
            sp.wait_ge(out_s, 16 * NBH)

        @block.gpsimd
        def _(pool):
            def ones_row(turn):
                pool.memset(view(PA, 0, [[1, F]], n=C), 0.0).then_inc(pa_set, 1)
                pool.wait_ge(pa_set, 2 * turn + 1)
                pool.memset(view(PA, 0, [[1, F]], C, 1), 1.0).then_inc(pa_set, 1)

            pool.memset(view(KM, 0, [[1, B * NPIX]]), 0.0).then_inc(km_clear, 1)
            pool.memset(XP[:, :], 0.0).then_inc(pool_set, 1)
            pool.memset(SQP[:, :], 0.0).then_inc(pool_set, 1)
            pool.wait_ge(pool_set, 2)
            ones_row(0)

            def distances(turn, b, half):
                n = 2 * b + half
                after(pool, hxy_ready, 16 * turn + n - 1)
                o = half * HATS
                pool.tensor_tensor(view(DXY, o, [[WW, KG * NA], [1, WW]]),
                                   view(LXA, n * KG * NA, [[1, KG * NA], [0, WW]]),
                                   view(cst, CST["xg"], [[0, KG * NA], [1, WW]]), ALU.subtract)
                pool.tensor_tensor(view(DXY, o + HXN, [[NR, KG], [1, NR]]),
                                   view(OM, n * 3 * KG + KG, [[1, KG], [0, NR]]),
                                   view(cst, CST["yg"], [[0, KG], [1, NR]]), ALU.subtract).then_inc(dxy_ready, 1)

            def masked(turn, b, half):
                n = 2 * b + half
                pool.wait_ge(hxy_ready, 16 * turn + n + 1)
                after(pool, prod_used, 9 * (16 * turn + n - 1))
                pool.tensor_tensor(view(HYM, half * HYN, [[NR, KG], [1, NR]]),
                                   view(HXY, half * HATS + HXN, [[NR, KG], [1, NR]]),
                                   view(OM, n * 3 * KG + 2 * KG, [[1, KG], [0, NR]]), ALU.mult).then_inc(hym_ready, 1)

            def top2(turn):
                for s in range(NT // 2):
                    pool.wait_ge(expert_used, turn * 8 + s + 1)
                    first, last = (view(PR, (s % 3) * 512 + o, [[256, 2], [E8, C], [1, E8 // 2]]) for o in (0, E8 // 2))
                    pool.tensor_tensor(first, first, last, ALU.add).then_inc(halved, 1)
                    if s == 4:
                        pool.wait_ge(bias_ready, turn + 1)
                        pool.tensor_tensor(XT[:, :], XT[:, :], SQ[:, :], ALU.add).then_inc(xt_biased, 1)

            pool.wait_ge(pa_set, 2)
            top2(0)

            links = [0]

            def add(out, a, b, op=ALU.add):
                links[0] += 1
                pool.tensor_tensor(out, a, b, op).then_inc(pool_chain, 1)
                pool.wait_ge(pool_chain, links[0])

            def tap_of(tap):
                return view(XP, tap // 3 * PADW + tap % 3, [[PADW * PADW, NBH], [PADW, HH], [1, WW]])

            pool.wait_ge(cst_s, 16)
            pool.wait_ge(xp_ready, 1)
            total = view(SQ, 0, [[NPIX, NBH], [WW, HH], [1, WW]])
            add(total, tap_of(D_TAPS[0]), tap_of(D_TAPS[1]))
            for tap in D_TAPS[2:-1]:
                add(total, total, tap_of(tap))
            pool.tensor_tensor(total, total, tap_of(D_TAPS[-1]), ALU.add).then_inc(dsum_ready, 1)
            inner = lambda t: view(t, PADW + 1, [[PADW * PADW, NBH], [PADW, HH], [1, WW]])
            add(inner(SQP), inner(XP), inner(XP), ALU.mult)
            rows = lambda d: view(SQP, d, [[PADW * PADW, NBH], [PADW, PADW], [1, WW]])
            across = view(BX, 0, [[PADW * WW, NBH], [WW, PADW], [1, WW]])
            add(across, rows(0), rows(1))
            add(across, across, rows(2))
            down = lambda d: view(BX, d * WW, [[PADW * WW, NBH], [WW, HH], [1, WW]])
            box = view(YC, 0, [[NPIX, NBH], [WW, HH], [1, WW]])
            add(box, down(0), down(1))
            pool.tensor_tensor(box, box, down(2), ALU.add).then_inc(box_ready, 1)

            for turn in range(2):
                pool.wait_ge(lxa_ready, 2 * turn + 1)
                for half in range(2):
                    distances(turn, 0, half)

                def pairs(b, half):
                    n = 2 * b + half
                    pool.wait_ge(prod_used, 9 * (16 * turn + n) + 2 * PAIRS)
                    first, second = (view(PRD, (half * K9 + k) * 288, [[1, PAIRS * 288]]) for k in (0, PAIRS))
                    pool.tensor_tensor(second, second, first, ALU.add).then_inc(paired, 1)

                def body(b, ahead):
                    masked(turn, b, 1)
                    if ahead >= 1:
                        distances(turn, b + 1, 1)
                    pairs(b, 0)
                    if ahead >= 1:
                        masked(turn, b + 1, 0)
                    if ahead == 2:
                        distances(turn, b + 2, 0)
                    pairs(b, 1)
                masked(turn, 0, 0)
                distances(turn, 1, 0)
                body(0, 2)
                with pool.Fori(1, B - 2) as b:
                    body(b, 2)
                body(B - 2, 1)
                body(B - 1, 0)
            pool.wait_ge(prod_done, 2 * 16 * K9)
            pool.memset(view(KM, 0, [[1, B * NPIX]]), 0.0).then_inc(km_clear, 1)
            top2(1)
            pool.wait_ge(scored, 40)
            ones_row(1)

        @block.scalar
        def _(act):
            tables = [0]

            def table(func):
                act.activation(spare[:, tables[0]:tables[0] + 1], cv("one", 1), func)
                tables[0] += 1

            def norm(n, eps, padded=False, then=None):
                table(ACT.Sqrt)
                for bh in range(NBH):
                    act.wait_ge(var_ready, NBH * n + bh + 1)
                    act.activation(sd[:, 8 * bh:8 * bh + 8], var[:, 8 * bh:8 * bh + 8], ACT.Sqrt, scale=1.0 / C,
                                   bias=cv(eps, 1)).then_inc(sd_ready, 1)
                if padded:
                    act.wait_ge(pool_set, 2)
                for bh in range(NBH):
                    act.wait_ge(xn_turned, NBH * n + bh + 1)
                    src = bank[NORM_BANKS[n] if bh else 0]
                    if padded:
                        ins = act.activation(view(XP, bh * PADW * PADW + PADW + 1, [[PADW, HH], [1, WW]]),
                                             view(src, 0, [[WW, HH], [1, WW]]), ACT.Copy)
                    else:
                        ins = act.activation(XNC[:, bh * NPIX:(bh + 1) * NPIX], src[:, 0:NPIX], ACT.Copy)
                ins.then_inc(xp_ready if padded else xnc_ready, 1)
                if then is not None:
                    table(then)

            def keys(w, bias, clear):
                act.wait_ge(km_clear, clear)
                act.wait_ge(k_done, clear)
                for bh in range(NBH):
                    for b4 in range(B4 - ACT_KEYS[clear - 1], B4):
                        act.activation(view(KM, (bh * B4 + b4) * NPIX, [[1, NPIX]], C * b4, C),
                                       view(bank[0], bh * NPIX, [[1, NPIX]], C * b4, C), ACT.Identity,
                                       bias=view(w, bias, [[1, 1]], C * b4, C)).then_inc(act_keys_ready, 1)

            def attend(first, steps):
                for s in range(first, first + steps + 4):
                    if s < first + steps:
                        act.wait_ge(nm_ready, s + 1)
                        for j in range(2):
                            u = 2 * (s - first) + j
                            at = (s % 3) * 512 + j * 256
                            ins = act.activation(SM[:, at:at + 256], SM[:, at:at + 256], ACT.Exp, scale=-1.0,
                                                 bias=nm[:, u:u + 1], accum_out=rs[:, u:u + 1])
                        ins.then_inc(p_ready, 1)
                    if s - 4 >= first and s % 4 == 3:
                        gr = s // 4 - 1
                        act.wait_ge(av_done, gr + 1)
                        act.activation(view(YG, (gr - first // 4) * NPIX, [[1, NPIX]]), bank[1 + 2 * (gr % 2)][:, 0:NPIX],
                                       ACT.Copy).then_inc(yg_ready, 1)

            def top2(turn):
                act.wait_ge(gate_ready, turn + 1)
                act.activation(EX[:, :], LG[:, :], ACT.Exp).then_inc(ex_ready, 1)
                act.wait_ge(gw_turned, turn + 1)
                act.activation(GT[:, 0:P], bank[6][:, 0:P], ACT.Copy).then_inc(gwt_ready, 1)
                act.wait_ge(bias_done, turn + 1)
                act.activation(SQ[:, :], bank[7][:, :], ACT.Copy).then_inc(bias_ready, 1)

            def expert_choice(turn):
                act.wait_ge(ec_max, turn + 1)
                act.activation(PB[:, :], MK[:, :], ACT.Exp, bias=nm[:, 0:1], accum_out=rs[:, 0:1]).then_inc(ec_exp, 1)
                table(ACT.Gelu)
                act.wait_ge(g_turned, turn + 1)
                act.activation(GT[:, :], bank[2][:, 0:NPIX], ACT.Copy).then_inc(gt_ready, 1)
                act.wait_ge(pooled, turn + 1)
                act.wait_ge(pa_set, 2 * turn + 1)
                act.activation(view(PA, 0, [[1, B], [C, E16]], n=C), view(bank[3], 0, [[E16, B], [1, E16]], n=C),
                               ACT.Copy).then_inc(pa_ready, 1)
                act.wait_ge(h_done, turn + 1)
                act.activation(view(HB, 0, [[1, F]]), bank[4][:, :], ACT.Gelu).then_inc(h_ready, 1)
                act.wait_ge(h_turned, turn + 1)
                act.activation(view(HT, 0, [[1, F]]), bank[6][:, :], ACT.Copy).then_inc(ht_ready, 1)

            act.dma_start(cst[:, 0:HEAD], cst_in[:, 0:HEAD]).then_inc(head_s, 16)
            act.wait_ge(head_s, 16)
            norm(0, "eps6", then=ACT.Exp)
            act.wait_ge(wa_s, 16)
            act.wait_ge(cst_s, 16)
            act.wait_ge(q_done, 1)
            act.activation(QC[:, 0:F], bank[1][:, :], ACT.Identity, bias=wa[:, WA["bq0"]:WA["bq0"] + 1]).then_inc(qc_ready, 1)
            keys(wa, WA["bk0"], 1)
            attend(0, 8)
            act.wait_ge(pad_asked, 1)
            act.activation(e0[:, 0:NT], den[:, 0:NT], ACT.Exp).then_inc(pad_ready, 1)
            norm(1, "eps5", then=ACT.Exp)
            top2(0)

            norm(2, "eps6", padded=True)
            act.wait_ge(wb_s, 16)
            act.wait_ge(xp_ready, 1)

            def distances(i):
                k = 0
                for n, (tap, j) in enumerate(UNITS):
                    if ON_DVE[n]:
                        continue
                    after(act, a_used, ACT_UNITS * i + k + 1 - ARING)
                    slot = (DRING + k % ARING) * F
                    w_at = WB["lw"] + i * len(UNITS) + 4 * tap + j
                    act.activation(view(RINGS, slot, [[NPIX, NBH], [WW, HH], [1, WW]]),
                                   view(XP, tap // 3 * PADW + tap % 3, [[PADW * PADW, NBH], [PADW, HH], [1, WW]]),
                                   ACT.Abs, scale=-1.0, bias=view(wb, w_at, [[1, 1]])).then_inc(a_ready, 1)
                    k += 1

            distances(0)
            with act.Fori(1, 8) as i:
                distances(i)
            table(ACT.Sqrt)
            act.wait_ge(d2_ready, 1)
            act.activation(D2[:, :], D2[:, :], ACT.Sqrt).then_inc(l2_ready, 1)
            norm(3, "eps5", then=ACT.Exp)
            expert_choice(0)

            norm(4, "eps6")

            def absolute(turn, b, half):
                n = 2 * b + half
                o = half * HATS
                act.wait_ge(dxy_ready, 16 * turn + n + 1)
                act.activation(view(DXY, o, [[1, HATS]]), view(DXY, o, [[1, HATS]]), ACT.Abs).then_inc(abs_done, 1)

            def hats(turn, b, half, begun=False):
                n = 2 * b + half
                o = half * HATS
                if not begun:
                    absolute(turn, b, half)
                act.wait_ge(abs_done, 16 * turn + n + 1)
                after(act, hx_turned, 3 * (16 * turn + n - 1))
                after(act, hym_ready, 16 * turn + n - 1)
                act.activation(view(HXY, o, [[1, HATS]]), view(DXY, o, [[1, HATS]]), ACT.Relu, scale=-1.0,
                               bias=cv("one", 1)).then_inc(hxy_ready, 1)

            def turned(turn, b, half):
                n = 2 * b + half
                after(act, prod_done, 9 * (16 * turn + n - 1))
                for g in range(3):
                    act.wait_ge(hx_turned, 3 * (16 * turn + n) + g + 1)
                    o = (half * K9 + 3 * g) * P
                    act.activation(view(HXT, o, [[1, 3 * P]]), bank[(3 * half + g) % 2][:, 0:3 * P], ACT.Copy).then_inc(hxt_ready, 1)

            def deform(turn, src, src_ready, count):
                act.wait_ge(src_ready, count)
                after(act, val_done, 6 * turn)
                for bh in range(NBH):
                    for g in range(G):
                        ins = act.activation(view(XW, bh * NR * P + g * NA * WW, [[P, NR], [WW, NA], [1, WW]]),
                                             view(src, bh * NPIX, [[WW, NR], [7 * WW, NA], [1, WW]]), ACT.Copy)
                    ins.then_inc(xw_ready, 1)
                hats(turn, 0, 0)
                absolute(turn, 0, 1)
                turned(turn, 0, 0)
                hats(turn, 0, 1, begun=True)

                def body(b, first=False):
                    for half in range(2):
                        if not (first and half == 0):
                            turned(turn, b, half)
                        hats(turn, b + 1, half)
                body(0, first=True)
                with act.Fori(1, B - 1) as b:
                    body(b)
                for half in range(2):
                    turned(turn, B - 1, half)
                act.wait_ge(smp_turned, turn + 1)
                act.activation(YC[:, :], bank[0][:, :], ACT.Copy, accum_out=c2[:, 3:4]).then_inc(sc_ready, 1)
                act.wait_ge(mean_ready, turn + 1)
                act.activation(D2[:, :], bank[1][:, :], ACT.Square, bias=c1[:, 0:1], accum_out=c2[:, 0:1]).then_inc(sq_ready, 1)
                table(ACT.Sqrt)
                act.wait_ge(bnv_ready, turn + 1)
                act.activation(c2[:, 1:2], c2[:, 2:3], ACT.Sqrt).then_inc(bsd_ready, 1)
                act.wait_ge(bn_ready, turn + 1)
                if turn == 0:
                    act.activation(YC[:, :], ACC[:, :], ACT.Relu, scale=c1[:, 2:3],
                                   bias=wc[:, WC["beta"]:WC["beta"] + 1]).then_inc(dc_ready, 1)

            act.wait_ge(wc_s, 16)
            deform(0, XNC, xnc_ready, 4)
            deform(1, YC, dc_ready, 1)
            norm(5, "eps5", then=ACT.Exp)
            top2(1)

            norm(6, "eps6", then=ACT.Exp)
            act.wait_ge(q_done, 2)
            act.wait_ge(bqh_ready, 1)
            for h in range(HEADS):
                act.activation(QC[:, h * F:(h + 1) * F], bank[1][:, :], ACT.Identity, scale=cv("hm", 1, h),
                               bias=bqh[:, h:h + 1]).then_inc(qc_ready, 1)
            keys(wd, WD["bk1"], 2)
            attend(8, 32)
            act.wait_ge(att_turned, 1)
            act.activation(YC[:, :], bank[0][:, :], ACT.Copy).then_inc(attc_ready, 1)
            norm(7, "eps5", then=ACT.Exp)
            expert_choice(1)

        @block.vector
        def _(dve):
            links = [0]

            def link(ins):
                links[0] += 1
                ins.then_inc(dve_chain, 1)
                dve.wait_ge(dve_chain, links[0])

            def tiles(t, col=0):
                return view(t, col, [[C, NT], [1, C]])

            def per_tile(t):
                return view(t, 0, [[1, NT], [0, C]])

            def norm(n):
                half = NT // 2
                of = lambda t, bh: view(t, bh * NPIX, [[C, half], [1, C]])
                per_tile = lambda t, bh: view(t, bh * half, [[1, half], [0, C]])
                one = lambda t, bh: t[:, bh * half:(bh + 1) * half]
                steps = (lambda bh: dve.tensor_reduce(one(s16, bh), of(XT, bh), AX.X, ALU.add),
                         lambda bh: dve.tensor_scalar(one(mean, bh), one(s16, bh), 1.0 / C, None, ALU.mult),
                         lambda bh: dve.tensor_tensor(of(XN, bh), of(XT, bh), per_tile(mean, bh), ALU.subtract),
                         lambda bh: dve.tensor_tensor(of(SQ, bh), of(XN, bh), of(XN, bh), ALU.mult),
                         lambda bh: dve.tensor_reduce(one(var, bh), of(SQ, bh), AX.X, ALU.add))
                for k, step in enumerate(steps):
                    for bh in range(NBH):
                        if k:
                            dve.wait_ge(dve_chain, links[0] - 1)
                        ins = step(bh)
                        if k < len(steps) - 1:
                            links[0] += 1
                            ins.then_inc(dve_chain, 1)
                        else:
                            ins.then_inc(var_ready, 1)
                            if bh == 0:
                                dve.wait_ge(dve_chain, links[0])
                for bh in range(NBH):
                    dve.wait_ge(sd_ready, NBH * n + bh + 1)
                    link(dve.reciprocal(one(rstd, bh), one(sd, bh)))
                    dve.tensor_tensor(of(XN, bh), of(XN, bh), per_tile(rstd, bh), ALU.mult).then_inc(xn_ready, 1)
                dve.wait_ge(xn_ready, NBH * (n + 1))

            def keys(w, bias, clear):
                dve.wait_ge(km_clear, clear)
                for b in range(B):
                    bh, b4 = divmod(b, B4)
                    if b4 >= B4 - ACT_KEYS[clear - 1]:
                        continue
                    dve.tensor_scalar(view(KM, b * NPIX, [[1, NPIX]], C * b4, C),
                                      view(bank[0], bh * NPIX, [[1, NPIX]], C * b4, C),
                                      view(w, bias, [[1, 1]], C * b4, C), None, ALU.add).then_inc(keys_ready, 1)

            def attend(first, steps, l3):
                for s in range(first, first + steps + 2):
                    if s < first + steps:
                        r = s - first
                        dve.wait_ge(scored, s + 1)
                        after(dve, pt_done, s - 2)
                        for j in range(2):
                            u = 2 * r + j
                            at = (s % 3) * 512 + j * 256
                            if l3:
                                add = view(wd, WD["rel"] + (j * HEADS + r % HEADS) * NPIX, [[1, NPIX]])
                            else:
                                add = cv("mask", NPIX, j * NPIX)
                            start = -NEG if l3 else cv("floor", 1, j)
                            ins = dve.tensor_tensor_reduce(SM[:, at:at + 256], scores_bank[s % 3][:, j * 256:j * 256 + 256],
                                                           add, -1.0, start, ALU.add, ALU.min, nm[:, u:u + 1])
                        ins.then_inc(nm_ready, 1)
                    if s - 2 >= first:
                        dve.wait_ge(pt_done, s - 1)
                        after(dve, av_done, (s - 2) // 4 - 1)
                        dve.tensor_copy(view(PTS, (s - 2) % TURNED * 512, [[1, 512]]),
                                        bank[6 + s % 2][:, :]).then_inc(pts_ready, 1)

            def top2(turn, rb, w):
                by_e = lambda t: view(t, 0, [[E8, NT], [1, E8]])
                one = lambda t: view(t, 0, [[1, NT], [0, E8]])
                keys = view(cst, CST["keys"], [[0, NT], [1, E8]])
                dve.wait_ge(routed, turn + 1)
                link(dve.tensor_tensor(by_e(LG), view(bank[1], 0, [[E8, NT], [1, E8]]),
                                       view(w, rb, [[0, NT], [1, E8]]), ALU.add))
                link(dve.tensor_reduce(s16[:, :], by_e(LG), AX.X, ALU.max))
                dve.tensor_tensor(by_e(LG), by_e(LG), one(s16), ALU.subtract).then_inc(gate_ready, 1)
                dve.wait_ge(gate_ready, turn + 1)
                link(dve.scalar_tensor_tensor(by_e(KEY), by_e(LG), 0.0, keys, ALU.is_ge, ALU.mult))
                link(dve.tensor_reduce(s16[:, :], by_e(KEY), AX.X, ALU.max))
                link(dve.tensor_tensor(by_e(S1), by_e(KEY), one(s16), ALU.is_equal))
                link(dve.scalar_tensor_tensor(by_e(KEY), by_e(S1), -BIG, by_e(LG), ALU.mult, ALU.add))
                link(dve.tensor_reduce(s16[:, :], by_e(KEY), AX.X, ALU.max))
                link(dve.tensor_tensor(by_e(S2), by_e(KEY), one(s16), ALU.is_equal))
                link(dve.tensor_tensor(by_e(KEY), by_e(S2), keys, ALU.mult))
                link(dve.tensor_reduce(s16[:, :], by_e(KEY), AX.X, ALU.max))
                link(dve.tensor_tensor(by_e(S2), by_e(KEY), one(s16), ALU.is_equal))
                link(dve.tensor_tensor(by_e(S1), by_e(S1), by_e(S2), ALU.add))
                dve.wait_ge(ex_ready, turn + 1)
                link(dve.tensor_tensor(by_e(GW), by_e(S1), by_e(EX), ALU.mult))
                link(dve.tensor_reduce(s16[:, :], by_e(GW), AX.X, ALU.add))
                link(dve.reciprocal(mean[:, :], s16[:, :]))
                dve.tensor_tensor(by_e(GW), by_e(GW), one(mean), ALU.mult).then_inc(gw_ready, 1)
                dve.wait_ge(gw_ready, turn + 1)
                def weighted(s):
                    dve.wait_ge(expert_done, turn * 8 + s + 1)
                    dve.tensor_tensor(view(PR, (s % 3) * 512, [[256, 2], [E8, C], [1, E8]]),
                                      view(bank[2 + s % 4], 0, [[256, 2], [E8, C], [1, E8]]),
                                      view(GW, (s // 4 * 8 + s % 4) * E8, [[4 * E8, 2], [0, C], [1, E8]]), ALU.mult).then_inc(expert_used, 1)

                weighted(0)
                weighted(1)
                for s in range(NT // 2):
                    dve.wait_ge(halved, turn * 8 + s + 1)
                    link(dve.tensor_reduce(view(Y2, (s // 4 * 8 + s % 4) * C, [[4 * C, 2], [1, C]]),
                                           view(PR, (s % 3) * 512, [[256, 2], [E8, C], [1, E8 // 2]]), AX.X, ALU.add))
                    if s + 2 < NT // 2:
                        weighted(s + 2)
                dve.wait_ge(xt_biased, turn + 1)
                link(dve.tensor_tensor(XT[:, :], XT[:, :], Y2[:, :], ALU.add))

            def expert_choice(turn, w, at):
                dve.wait_ge(ec_logits, turn + 1)
                link(dve.tensor_scalar(MK[:, :], bank[1][:, 0:NPIX], w[:, at["gb"]:at["gb"] + 1], None, ALU.add))
                link(dve.tensor_reduce(mx[:, 0:1], MK[:, :], AX.X, ALU.max))
                dve.tensor_scalar(nm[:, 0:1], mx[:, 0:1], -1.0, None, ALU.mult).then_inc(ec_max, 1)
                dve.wait_ge(ec_exp, turn + 1)
                link(dve.reciprocal(den[:, 0:1], rs[:, 0:1]))
                link(dve.tensor_scalar(PB[:, :], PB[:, :], den[:, 0:1], None, ALU.mult))
                link(dve.max(top8[:, :], PB[:, :]))
                link(dve.match_replace(out=MK[:, :], in_to_replace=top8[:, :], in_values=PB[:, :], imm_value=-1.0))
                dve.scalar_tensor_tensor(GX[:, :], MK[:, :], 0.0, PB[:, :], ALU.is_lt, ALU.mult).then_inc(g_ready, 1)
                dve.wait_ge(o_done, turn + 1)
                dve.tensor_tensor(view(OC, 0, [[1, E16], [E16, B]], n=C),
                                  view(bank[5], 0, [[B, E16], [1, B]], n=C),
                                  view(w, at["b2"], [[1, E16], [0, B]], n=C), ALU.add).then_inc(oc_ready, 1)
                dve.wait_ge(oc_turned, turn + 1)
                dve.tensor_tensor(view(OB, 0, [[C, B], [1, C]]), view(bank[6], 0, [[0, B], [1, C]]),
                                  view(cst, CST["ecmask"], [[1, B], [0, C]]), ALU.mult).then_inc(ob_ready, 1)
                dve.wait_ge(ec_out, turn + 1)
                ins = dve.tensor_tensor(XT[:, :], XT[:, :], bank[7][:, :], ALU.add)
                if turn:
                    ins.then_inc(x_ready, 1)
                else:
                    link(ins)

            dve.wait_ge(x_turned, 1)
            link(dve.tensor_copy(XT[:, :], bank[0][:, :]))

            norm(0)
            dve.wait_ge(cst_s, 16)
            dve.wait_ge(wa_s, 16)
            dve.wait_ge(k_done, 1)
            keys(wa, WA["bk0"], 1)
            dve.wait_ge(v_done, 1)
            dve.tensor_tensor(tiles(VT), tiles(bank[3]), view(wa, WA["bv0"], [[0, NT], [1, C]]), ALU.add)\
               .then_inc(vt_ready, 1)
            attend(0, 8, False)
            dve.wait_ge(p_ready, 8)
            dve.tensor_scalar(den[:, 0:NT], nm[:, 0:NT], 0.0, None, ALU.min).then_inc(pad_asked, 1)
            dve.wait_ge(pad_ready, 1)
            by_unit = lambda t, o=0: view(t, o, [[8, 2], [1, 2], [2, 4]])
            link(dve.tensor_tensor(by_unit(e0), by_unit(e0), view(cst, CST["npad"], [[0, 2], [1, 2], [0, 4]]), ALU.mult))
            link(dve.tensor_tensor(e0[:, 0:NT], e0[:, 0:NT], rs[:, 0:NT], ALU.add))
            link(dve.reciprocal(view(den, 0, [[8, 2], [4, 2], [1, 4]]), by_unit(e0)))
            dve.wait_ge(yg_turned, 1)
            link(dve.tensor_tensor(tiles(Y2), tiles(bank[0]), per_tile(den), ALU.mult))
            link(dve.tensor_tensor(XT[:, :], XT[:, :], Y2[:, :], ALU.add))
            norm(1)
            dve.wait_ge(wb_s, 16)
            link(dve.tensor_tensor(view(RINGS, 0, [[1, 288]]), wb[:, WB["wf"]:WB["wf"] + 288],
                                   wb[:, WB["wf"]:WB["wf"] + 288], ALU.mult))
            link(dve.tensor_reduce(w2s[:, :], view(RINGS, 0, [[1, 288]]), AX.X, ALU.add))
            link(dve.tensor_tensor(view(RINGS, 0, [[C, 9], [1, C]]), view(wb, WB["wf"], [[C, 9], [1, C]]),
                                   view(cst, CST["dtaps"], [[1, 9], [0, C]]), ALU.mult))
            link(dve.tensor_reduce(wsd[:, :], view(RINGS, 0, [[1, 288]]), AX.X, ALU.add))
            top2(0, WB["rb0"], wb)

            norm(2)
            dve.wait_ge(xp_ready, 1)

            def maxima(i):
                k = 0
                for n, (tap, j) in enumerate(UNITS):
                    if not ON_DVE[n]:
                        continue
                    after(dve, d_used, DVE_UNITS * i + k + 1 - DRING)
                    w_at = WB["lw"] + i * len(UNITS) + 4 * tap + j
                    dve.tensor_scalar(view(RINGS, (k % DRING) * F, [[NPIX, NBH], [WW, HH], [1, WW]]),
                                      view(XP, tap // 3 * PADW + tap % 3, [[PADW * PADW, NBH], [PADW, HH], [1, WW]]),
                                      view(wb, w_at, [[1, 1]]), None, ALU.max).then_inc(d_ready, 1)
                    k += 1

            maxima(0)
            with dve.Fori(1, 8) as i:
                maxima(i)
            dve.wait_ge(l2_done, 1)
            link(dve.tensor_scalar(D2[:, :], bank[5][:, :], -2.0, w2s[:, 0:1], ALU.mult, ALU.add))
            dve.tensor_scalar(D2[:, :], D2[:, :], 1e-12, None, ALU.max).then_inc(d2_ready, 1)
            dve.wait_ge(l2_ready, 1)
            dve.wait_ge(d_used, 8 * DVE_UNITS)
            dve.wait_ge(a_used, 8 * ACT_UNITS)
            link(dve.scalar_tensor_tensor(ACC[:, :], bank[2][:, :], wsd[:, 0:1], D2[:, :], ALU.subtract, ALU.subtract))
            dve.scalar_tensor_tensor(ACC[:, :], ACC[:, :], -1.0, D2[:, :], ALU.mult, ALU.subtract).then_inc(lo_ready, 1)
            dve.wait_ge(lo_turned, 1)
            for g in range(4):
                ins = dve.tensor_tensor(view(XT, g * P, [[C, B4], [1, C]]), view(XT, g * P, [[C, B4], [1, C]]),
                                        view(bank[0], g * P, [[1, B4], [B4, C]]), ALU.add)
            link(ins)
            norm(3)
            expert_choice(0, wb, {"gb": WB["gb0"], "b2": WB["b20"]})

            norm(4)
            dve.wait_ge(wc_s, 16)
            link(dve.tensor_tensor(view(base, 0, [[3 * KG, 2], [1, 3 * KG]]), view(cst, CST["geo"], [[3 * KG, 2], [1, 3 * KG]]),
                                   view(wc, WC["bom"], [[0, 2], [1, 3 * KG]]), ALU.add))

            def points(turn, bh):
                for half in range(2):
                    dve.wait_ge(om_done, 4 * turn + 2 * bh + half + 1)
                    dve.tensor_tensor(view(OM, (8 * bh + half) * 3 * KG, [[2 * 3 * KG, B4], [1, 3 * KG]]),
                                      view(bank[1 + half], 0, [[3 * KG, B4], [1, 3 * KG]]),
                                      view(base, half * 3 * KG, [[0, B4], [1, 3 * KG]]), ALU.add).then_inc(om_used, 1)
                dve.wait_ge(om_used, 4 * turn + 2 * bh + 2)
                lx = view(OM, 8 * bh * 3 * KG, [[3 * KG, 8], [1, KG]])
                ly = view(OM, 8 * bh * 3 * KG + KG, [[3 * KG, 8], [1, KG]])
                am = view(AM, 8 * bh * KG, [[KG, 8], [1, KG]])
                lxa = [view(LXA, 8 * bh * 2 * KG + a, [[2 * KG, 8], [2, KG]]) for a in range(NA)]
                link(dve.tensor_scalar(am, ly, 8.0, None, ALU.is_ge))
                dve.scalar_tensor_tensor(lxa[0], am, BIG, lx, ALU.mult, ALU.add)
                link(dve.scalar_tensor_tensor(ly, am, -7.0, ly, ALU.mult, ALU.add))
                link(dve.tensor_scalar(am, am, -1.0, 1.0, ALU.mult, ALU.add))
                dve.scalar_tensor_tensor(lxa[1], am, BIG, lx, ALU.mult, ALU.add).then_inc(lxa_ready, 1)
                for n, r0 in enumerate(range(0, NR, 4)):
                    rows = min(4, NR - r0)
                    dve.wait_ge(val_done, 6 * turn + 3 * bh + n + 1)
                    dve.tensor_tensor(view(VB, bh * B4 * 288 + r0, [[1, rows], [NR, P]]),
                                      view(bank[3 + (3 * bh + n) % 2], 0, [[P, rows], [1, P]]),
                                      view(cst, CST["gmask"], [[0, rows], [1, P]]), ALU.mult).then_inc(val_used, 1)

            def sample(turn, b, half, taps=range(K9)):
                n = 2 * b + half
                dve.wait_ge(hym_ready, 16 * turn + n + 1)
                after(dve, smp_ready, 16 * turn + n - 1)
                after(dve, paired, 16 * turn + n - 1)
                for k in taps:
                    idx = 9 * (16 * turn + n) + k
                    dve.wait_ge(prod_done, idx + 1)
                    dve.tensor_tensor(view(PRD, (half * K9 + k) * 288, [[72, G], [NR, CG], [1, NR]]),
                                      view(bank[2 + (9 * half + k) % LOOK], 0, [[72, G], [NR, CG], [1, NR]]),
                                      view(HYM, half * HYN + k * G * NR, [[NR, G], [0, CG], [1, NR]]), ALU.mult).then_inc(prod_used, 1)

            def sums(turn, bh, b, half):
                n = 2 * b + half
                dve.wait_ge(prod_used, 9 * (16 * turn + n) + 9)
                dve.wait_ge(paired, 16 * turn + n + 1)
                dve.tensor_reduce(view(SMT, bh * NPIX + half * P + (b - B4 * bh) * C, [[1, C]]),
                                  view(PRD, (half * K9 + PAIRS) * 288, [[NR, C], [288, K9 - PAIRS], [1, NR]]), AX.XY,
                                  ALU.add).then_inc(smp_ready, 1)

            def deform(turn):
                points(turn, 0)
                points(turn, 1)
                for bh in range(NBH):
                    b0 = B4 * bh
                    sample(turn, b0, 0)
                    if bh:
                        sums(turn, 0, b0 - 1, 1)
                    sample(turn, b0, 1)
                    sums(turn, bh, b0, 0)
                    with dve.Fori(b0 + 1, b0 + B4 - bh) as b:
                        sample(turn, b, 0)
                        sums(turn, bh, b - 1, 1)
                        sample(turn, b, 1)
                        sums(turn, bh, b, 0)
                sample(turn, B - 1, 0)
                sums(turn, 1, B - 2, 1)
                sample(turn, B - 1, 1, range(2 * PAIRS))
                sums(turn, 1, B - 1, 0)
                sample(turn, B - 1, 1, range(2 * PAIRS, K9))
                sums(turn, 1, B - 1, 1)
                dve.wait_ge(sum_done, turn + 1)
                dve.tensor_copy(c1[:, 1:2], bank[2][:, 0:1]).then_inc(sum_ready, 1)
                dve.wait_ge(mean_done, turn + 1)
                dve.tensor_scalar(c1[:, 0:1], bank[3][:, 0:1], -1.0, None, ALU.mult).then_inc(mean_ready, 1)
                dve.wait_ge(sq_ready, turn + 1)
                dve.tensor_scalar(ACC[:, :], bank[1][:, :], c1[:, 0:1], None, ALU.add).then_inc(cen_ready, 1)
                dve.wait_ge(cen_ready, turn + 1)
                dve.wait_ge(sq_done, turn + 1)
                dve.tensor_scalar(c2[:, 2:3], bank[4][:, 0:1], 1e-5, None, ALU.add).then_inc(bnv_ready, 1)
                dve.wait_ge(bsd_ready, turn + 1)
                link(dve.reciprocal(c1[:, 3:4], c2[:, 1:2]))
                dve.tensor_tensor(c1[:, 2:3], c1[:, 3:4], wc[:, WC["gamma"]:WC["gamma"] + 1], ALU.mult).then_inc(bn_ready, 1)
                dve.wait_ge(bn_ready, turn + 1)

            deform(0)
            deform(1)
            link(dve.tensor_scalar(ACC[:, :], ACC[:, :], c1[:, 2:3], wc[:, WC["beta"]:WC["beta"] + 1], ALU.mult, ALU.add))
            dve.tensor_tensor(YC[:, :], ACC[:, :], XNC[:, :], ALU.add).then_inc(yc_ready, 1)
            dve.wait_ge(wc_done, 1)
            link(dve.tensor_tensor(XT[:, :], XT[:, :], bank[4][:, :], ALU.add))
            norm(5)
            top2(1, WC["rb1"], wc)

            norm(6)
            dve.wait_ge(wd_s, 16)
            dve.tensor_scalar(bqh[:, :], cv("hm", HEADS), wd[:, WD["bq1"]:WD["bq1"] + 1], None, ALU.mult)\
               .then_inc(bqh_ready, 1)
            dve.wait_ge(k_done, 2)
            keys(wd, WD["bk1"], 2)
            dve.wait_ge(v_done, 2)
            dve.tensor_tensor(tiles(VT), tiles(bank[3]), view(wd, WD["bv1"], [[0, NT], [1, C]]), ALU.add)\
               .then_inc(vt_ready, 1)
            attend(8, 32, True)
            dve.wait_ge(p_ready, 40)
            link(dve.reciprocal(den[:, :], rs[:, :]))
            dve.wait_ge(yg_turned, 2)
            for b in range(B):
                ins = dve.tensor_tensor(view(Y2, (b // B4 * 8 + b % B4) * C, [[B4 * C, 2], [HC, HEADS], [1, HC]]),
                                        view(bank[4 + b // 2], b % 2 * 256, [[P, 2], [C + HC, HEADS], [1, HC]]),
                                        view(den, b * 8, [[1, 2], [2, HEADS], [0, HC]]), ALU.mult)
            ins.then_inc(att_ready, 1)
            link(dve.tensor_tensor(tiles(XT), tiles(XT), view(wd, WD["bu1"], [[0, NT], [1, C]]), ALU.add))
            dve.wait_ge(u_done, 1)
            link(dve.tensor_tensor(XT[:, :], XT[:, :], bank[2][:, :], ALU.add))
            norm(7)
            expert_choice(1, wd, {"gb": WD["gb1"], "b2": WD["b21"]})
            for bh in range(NBH):
                dve.wait_ge(fin_turned, bh + 1)
                dve.tensor_copy(XC[:, bh * NPIX:(bh + 1) * NPIX], bank[bh][:, 0:NPIX]).then_inc(fin_ready, 1)

        @block.tensor
        def _(pe):
            def turn4(dst, src, s):
                for g in range(4):
                    ins = pe.transpose(dst[:, g * P:(g + 1) * P], src[:, g * P:(g + 1) * P], ident)
                ins.then_inc(s, 1)

            def keep_warm(bk, count):
                for _ in range(count):
                    pe.matmul(bk[:, 0:P], ident, ident, start=True, stop=True)

            def norm(n):
                keep_warm(bank[NORM_BANKS[n]], FILL[n])
                for bh in range(NBH):
                    pe.wait_ge(xn_ready, NBH * n + bh + 1)
                    for half in range(2):
                        g = 2 * bh + half
                        ins = pe.transpose(bank[NORM_BANKS[n] if bh else 0][:, half * P:(half + 1) * P],
                                           XN[:, g * P:(g + 1) * P], ident)
                    ins.then_inc(xn_turned, 1)

            def w_(t, at, n=P, p0=0, np_=P):
                return t[p0:p0 + np_, at:at + n]

            def project(turn, t, at):
                pe.wait_ge(xnc_ready, {0: 1, 1: 6}[turn])
                pe.matmul(bank[0][:, :], w_(t, at["k"]), XNC[:, :], start=True, stop=True).then_inc(k_done, 1)
                pe.matmul(bank[1][:, :], w_(t, at["q"]), XNC[:, :], start=True, stop=True).then_inc(q_done, 1)
                for g in range(4):
                    ins = pe.matmul(bank[3][:, g * P:(g + 1) * P], XNC[:, g * P:(g + 1) * P], w_(t, at["v"]),
                                    start=True, stop=True)
                ins.then_inc(v_done, 1)
                keep_warm(bank[6], FILL_KEYS)

            def attend(first, steps, l3):
                def image(s):
                    return divmod(s - first, HEADS) if l3 else (s - first, 0)

                def scores(s):
                    after(pe, nm_ready, s - 2)
                    b, h = image(s)
                    bh, b4 = divmod(b, B4)
                    if b == 0:
                        pe.wait_ge(qc_ready, 1 + h + 1 if l3 else 1)
                    if h == 0:
                        mine = ACT_KEYS[l3]
                        if b4 >= B4 - mine:
                            pe.wait_ge(act_keys_ready, l3 * NBH * ACT_KEYS[0] + bh * mine + b4 - (B4 - mine) + 1)
                        else:
                            pe.wait_ge(keys_ready, l3 * NBH * (B4 - ACT_KEYS[0]) + bh * (B4 - mine) + b4 + 1)
                    for j in range(2):
                        q0 = h * F + bh * NPIX + j * P
                        ins = pe.matmul(scores_bank[s % 3][:, j * 256:j * 256 + 256],
                                        QC[:, q0:q0 + P], view(KM, b * NPIX, [[1, NPIX]]), start=True, stop=True)
                    ins.then_inc(scored, 1)

                def turn(s):
                    pe.wait_ge(p_ready, s + 1)
                    after(pe, pts_ready, s - 1)
                    for j in range(2):
                        for kt in range(2):
                            ins = pe.transpose(bank[6 + s % 2][:, (2 * kt + j) * P:(2 * kt + j + 1) * P],
                                               view(SM, (s % 3) * 512 + (2 * j + kt) * P, [[1, P]]), ident)
                    ins.then_inc(pt_done, 1)

                def values(gr):
                    pe.wait_ge(pts_ready, 4 * gr + 4)
                    pe.wait_ge(vt_ready, l3 + 1)
                    after(pe, yg_ready, gr - 1)
                    for kt in range(2):
                        for i in range(4):
                            s = 4 * gr + i
                            bh, b4 = divmod(image(s)[0], B4)
                            ins = pe.matmul(bank[1 + 2 * (gr % 2)][32 * i:32 * i + 32, 0:NPIX],
                                            view(VT, ((2 * bh + kt) * B4 + b4) * C, [[1, C]]),
                                            view(PTS, s % TURNED * 512 + kt * NPIX, [[1, NPIX]]),
                                            start=(kt == 0), stop=(kt == 1), skip_group_check=True)
                    ins.then_inc(av_done, 1)

                scores(first)
                for s in range(first, first + steps + 4):
                    if s + 1 < first + steps:
                        scores(s + 1)
                    if first <= s - 2 < first + steps:
                        turn(s - 2)
                    if s - 3 >= first and (s - 3) % 4 == 3:
                        values((s - 3) // 4)

            def top2(turn, w, at, nx):
                pe.wait_ge(xnc_ready, nx)
                for g in range(4):
                    ins = pe.matmul(bank[1][:, g * 32:g * 32 + 32], XNC[:, g * P:(g + 1) * P], w_(w, at["r"], 32),
                                    start=True, stop=True)
                ins.then_inc(routed, 1)
                for s in range(NT // 2):
                    after(pe, expert_used, 8 * turn + s - 3)
                    bk = bank[2 + s % 4]
                    bh, b4 = divmod(s, B4)
                    for j in range(2):
                        g = 2 * bh + j
                        ins = pe.matmul(bk[:, j * 256:j * 256 + 256], XNC[:, g * P:(g + 1) * P],
                                        w_(w, at["ew"] + b4 * 256, 256), start=True, stop=True)
                    ins.then_inc(expert_done, 1)
                    if s == 3:
                        keep_warm(bank[7], FILL_GATES)
                        pe.wait_ge(gw_ready, turn + 1)
                        pe.transpose(bank[6][:, 0:P], GW[:, :], ident).then_inc(gw_turned, 1)
                        pe.wait_ge(gwt_ready, turn + 1)
                        pe.matmul(bank[7][:, :], GT[:, 0:P], w[:, at["eb"]:at["eb"] + 512], start=True,
                                  stop=True).then_inc(bias_done, 1)

            def expert_choice(turn, w, at, nx):
                pe.wait_ge(xnc_ready, nx)
                for bh in range(NBH):
                    ins = pe.matmul(bank[1][:, 0:NPIX], w_(w, at["gw"] + bh * P), XNC[:, bh * NPIX:(bh + 1) * NPIX],
                                    start=(bh == 0), stop=(bh == NBH - 1))
                ins.then_inc(ec_logits, 1)
                keep_warm(bank[6], FILL_EC)
                pe.wait_ge(g_ready, turn + 1)
                for half in range(2):
                    ins = pe.transpose(bank[2][:, half * P:(half + 1) * P], GX[:, half * P:(half + 1) * P], ident)
                ins.then_inc(g_turned, 1)
                pe.wait_ge(gt_ready, turn + 1)
                for b in range(B):
                    for half in range(2):
                        t = b // 4 * 8 + half * 4 + b % 4
                        ins = pe.matmul(bank[3][0:C, b * E16:(b + 1) * E16], XN[:, t * C:(t + 1) * C],
                                        GT[:, half * P + b * E16:half * P + (b + 1) * E16],
                                        start=(half == 0), stop=(half == 1))
                ins.then_inc(pooled, 1)
                pe.wait_ge(pa_ready, turn + 1)
                pe.wait_ge(pa_set, 2 * (turn + 1))
                for e in range(E16):
                    q, j = divmod(e, 4)
                    ins = pe.matmul(bank[4][C * j:C * (j + 1), q * HID:(q + 1) * HID], view(PA, e * C, [[1, C]], n=C + 1),
                                    w[0:C + 1, at["w1"] + e * HID:at["w1"] + (e + 1) * HID], start=True, stop=True,
                                    skip_group_check=True)
                ins.then_inc(h_done, 1)
                pe.wait_ge(h_ready, turn + 1)
                for q in range(4):
                    ins = pe.transpose(bank[6][:, q * P:(q + 1) * P], view(HB, q * HID, [[1, HID]]), ident)
                ins.then_inc(h_turned, 1)
                pe.wait_ge(ht_ready, turn + 1)
                for e in range(E16):
                    ins = pe.matmul(bank[5][0:C, e * B:(e + 1) * B], w[:, at["w2"] + e * C:at["w2"] + (e + 1) * C],
                                    view(HT, e * C, [[1, B]]), start=True, stop=True)
                ins.then_inc(o_done, 1)
                pe.wait_ge(oc_ready, turn + 1)
                pe.transpose(bank[6][:, 0:C], OC[:, :], cst[0:C, CST["ident"]:CST["ident"] + C]).then_inc(oc_turned, 1)
                pe.wait_ge(ob_ready, turn + 1)
                for g in range(4):
                    bh, half = divmod(g, 2)
                    ins = pe.matmul(bank[7][:, g * P:(g + 1) * P], GX[:, half * P:(half + 1) * P],
                                    OB[:, bh * P:(bh + 1) * P], start=True, stop=True)
                ins.then_inc(ec_out, 1)

            pe.wait_ge(head_s, 16)
            pe.wait_ge(x_in_s, 16 * NBH)
            turn4(bank[0], XC, x_turned)

            norm(0)
            pe.wait_ge(cst_s, 16)
            pe.wait_ge(wa_s, 16)
            project(0, wa, {"q": WA["q0"], "k": WA["k0"], "v": WA["v0"]})
            attend(0, 8, False)
            pe.wait_ge(yg_ready, 2)
            for g in range(4):
                ins = pe.transpose(bank[0][:, g * P:(g + 1) * P], view(YG, g * P, [[1, P]]), ident)
            ins.then_inc(yg_turned, 1)
            norm(1)
            pe.wait_ge(wb_s, 16)
            top2(0, wb, {"r": WB["r0"], "eb": WB["eb0"], "ew": WB["ew0"]}, 2)

            norm(2)
            pe.wait_ge(xp_ready, 1)

            def tap_of(t, tap):
                return view(t, tap // 3 * PADW + tap % 3, [[PADW * PADW, NBH], [PADW, HH], [1, WW]])

            def sums(i):
                kd = ka = 0
                for n, (tap, j) in enumerate(UNITS):
                    if ON_DVE[n]:
                        pe.wait_ge(d_ready, DVE_UNITS * i + kd + 1)
                        slot, rep, used = (kd % DRING) * F, "rep2", d_used
                        kd += 1
                    else:
                        pe.wait_ge(a_ready, ACT_UNITS * i + ka + 1)
                        slot, rep, used = (DRING + ka % ARING) * F, "rep1", a_used
                        ka += 1
                    pe.matmul(bank[2][32 * j:32 * j + 32, :], cv(rep, 32, 28 - 4 * i), RINGS[:, slot:slot + F],
                              start=(i == 0 and tap == TAPS[0]), stop=(i == 7 and tap == TAPS[-1]),
                              skip_group_check=True).then_inc(used, 1)

            def dot(tap):
                pe.matmul(bank[5][:, :], w_(wb, WB["w9"] + tap * P), tap_of(XP, tap), start=(tap == 0), stop=False)

            for i, dots in enumerate(((0,), (1, 2), (3,), (4,), (5, 6), (7,), (8,), ())):
                sums(i)
                for tap in dots:
                    dot(tap)
                if i == 6:
                    pe.wait_ge(box_ready, 1)
                    pe.matmul(bank[5][:, :], cv("nhalf", P), YC[:, :], start=False, stop=True).then_inc(l2_done, 1)
                    pe.wait_ge(dsum_ready, 1)
                    pe.matmul(bank[2][:, :], cv("nrep", P), SQ[:, :], start=False, stop=False, skip_group_check=True)
                    pe.matmul(bank[2][0:64, :], cv("nrep", 64), tap_of(XP, SHARED), start=False, stop=False,
                              skip_group_check=True)
            pe.wait_ge(lo_ready, 1)
            turn4(bank[0], ACC, lo_turned)
            norm(3)
            expert_choice(0, wb, {"gw": WB["gw0"], "w1": WB["w10"], "w2": WB["w20"]}, 3)

            norm(4)
            pe.wait_ge(wc_s, 16)

            def turn_hats(turn, b, half, groups=range(3)):
                n = 2 * b + half
                pe.wait_ge(hxy_ready, 16 * turn + n + 1)
                for g in groups:
                    after(pe, hxt_ready, 3 * (16 * turn + n) + g - 1)
                    bk = bank[(3 * half + g) % 2]
                    for k in range(3):
                        at = half * HATS + (3 * g + k) * P
                        ins = pe.transpose(bk[:, k * P:(k + 1) * P], view(HXY, at, [[1, P]]), ident)
                    ins.then_inc(hx_turned, 1)

            def products(turn, b, half, more):
                n = 2 * b + half
                for k in range(K9):
                    if more and k in TURN_AT:
                        turn_hats(turn, b + half, 1 - half, TURN_AT[k])
                    if k % 3 == 0:
                        pe.wait_ge(hxt_ready, 3 * (16 * turn + n) + k // 3 + 1)
                    after(pe, prod_used, 9 * (16 * turn + n) + k + 1 - LOOK)
                    pe.matmul(bank[2 + (9 * half + k) % LOOK][:, 0:288], view(HXT, (half * K9 + k) * P, [[1, P]]),
                              view(VB, b * 288, [[1, 288]]), start=True, stop=True).then_inc(prod_done, 1)

            def deform(turn, src):
                n = 0
                for bh in range(NBH):
                    for half in range(2):
                        after(pe, om_used, 4 * turn + 2 * bh + half - 1)
                        g = 2 * bh + half
                        pe.matmul(bank[1 + half][:, 0:B4 * 3 * KG], src[:, g * P:(g + 1) * P],
                                  w_(wc, WC["om"], B4 * 3 * KG), start=True, stop=True).then_inc(om_done, 1)
                    pe.wait_ge(xw_ready, NBH * turn + bh + 1)
                    for r0 in range(0, NR, 4):
                        rows = min(4, NR - r0)
                        after(pe, val_used, 6 * turn + n - 1)
                        bk = bank[3 + n % 2]
                        pe.matmul(bk[:, 0:rows * P], cst[0:1, CST["ones"]:CST["ones"] + P],
                                  wc[0:1, WC["bval"]:WC["bval"] + rows * P], start=True, stop=False, skip_group_check=True)
                        for r in range(rows):
                            ins = pe.matmul(bk[:, r * P:(r + 1) * P],
                                            view(XW, (bh * NR + r0 + r) * P, [[1, P]]),
                                            w_(wc, WC["val"]), start=False, stop=True, skip_group_check=True)
                        ins.then_inc(val_done, 1)
                        n += 1
                turn_hats(turn, 0, 0)
                pe.wait_ge(val_used, 6 * turn + 6)

                def body(b, more):
                    products(turn, b, 0, True)
                    products(turn, b, 1, more)
                body(0, True)
                with pe.Fori(1, B - 1) as b:
                    body(b, True)
                body(B - 1, False)
                keep_warm(bank[1], FILL_TAIL)
                pe.wait_ge(smp_ready, 16 * turn + 16)
                turn4(bank[0], SMT, smp_turned)
                pe.wait_ge(sc_ready, turn + 1)
                pe.matmul(bank[2][:, 0:1], cv("avg", P), c2[:, 3:4], start=True, stop=True).then_inc(sum_done, 1)
                pe.matmul(bank[1][:, :], w_(wc, WC["wo"]), YC[:, :], start=True, stop=True)
                pe.wait_ge(sum_ready, turn + 1)
                pe.matmul(bank[3][:, 0:1], w_(wc, WC["wo"]), c1[:, 1:2], start=True, stop=True).then_inc(mean_done, 1)
                keep_warm(bank[5], FILL_BN)
                pe.wait_ge(sq_ready, turn + 1)
                pe.matmul(bank[4][:, 0:1], cv("avg", P), c2[:, 0:1], start=True, stop=True).then_inc(sq_done, 1)
                keep_warm(bank[5], FILL_BN)

            pe.wait_ge(xnc_ready, 4)
            deform(0, XNC)
            pe.wait_ge(dc_ready, 1)
            deform(1, YC)
            pe.wait_ge(yc_ready, 1)
            for g in range(4):
                ins = pe.matmul(bank[4][:, g * P:(g + 1) * P], YC[:, g * P:(g + 1) * P], w_(wc, WC["wc"]),
                                start=True, stop=True)
            ins.then_inc(wc_done, 1)
            norm(5)
            top2(1, wc, {"r": WC["r1"], "eb": WC["eb1"], "ew": WC["ew1"]}, 5)

            norm(6)
            pe.wait_ge(wd_s, 16)
            project(1, wd, {"q": WD["q1"], "k": WD["k1"], "v": WD["v1"]})
            attend(8, 32, True)
            pe.wait_ge(yg_ready, 10)
            pe.wait_ge(pts_ready, 40)
            for g in range(16):
                ins = pe.transpose(bank[4 + g // 4][:, g % 4 * P:(g % 4 + 1) * P], view(YG, g * P, [[1, P]]), ident)
            ins.then_inc(yg_turned, 1)
            pe.wait_ge(att_ready, 1)
            turn4(bank[0], Y2, att_turned)
            pe.wait_ge(attc_ready, 1)
            for g in range(4):
                ins = pe.matmul(bank[2][:, g * P:(g + 1) * P], YC[:, g * P:(g + 1) * P], w_(wd, WD["u1"]),
                                start=True, stop=True)
            ins.then_inc(u_done, 1)
            norm(7)
            expert_choice(1, wd, {"gw": WD["gw1"], "w1": WD["w11"], "w2": WD["w21"]}, 7)
            pe.wait_ge(x_ready, 1)
            for bh in range(NBH):
                for half in range(2):
                    g = 2 * bh + half
                    ins = pe.transpose(bank[bh][:, half * P:(half + 1) * P], XT[:, g * P:(g + 1) * P], ident)
                ins.then_inc(fin_turned, 1)


def _constants(np):
    c = np.zeros((P, NCST), np.float32)

    def put(name, a):
        c[:, CST[name]:CST[name] + a.shape[1]] = a

    p = np.arange(P)
    pix = np.arange(NPIX)
    put("ident", np.eye(P))
    ky, kx = pix // WW, pix % WW
    for half in range(2):
        qy, qx = half * 8 + p // WW, p % WW
        near = (abs(qy[:, None] - ky) <= 3) & (abs(qx[:, None] - kx) <= 3)
        c[:, CST["mask"] + half * NPIX:CST["mask"] + (half + 1) * NPIX] = np.where(near, 0.0, -BIG)
        npad = 49 - near.sum(1)
        c[:, CST["floor"] + half] = np.where(npad > 0, 0.0, -NEG)
        c[:, CST["npad"] + half] = npad
        geo = np.zeros((P, 3, K9, G))
        k = np.arange(K9)
        geo[:, 0] = (qx[:, None] + k % 3 - 1)[:, :, None]
        geo[:, 1] = (qy[:, None] + k // 3 - 1)[:, :, None]
        c[:, CST["geo"] + half * 3 * KG:CST["geo"] + (half + 1) * 3 * KG] = geo.reshape(P, -1)
    put("one", np.ones((P, 1)))
    put("eps6", np.full((P, 1), 1e-6))
    put("eps5", np.full((P, 1), 1e-5))
    put("hm", (p[:, None] % C // HC == np.arange(HEADS)) * np.float32(HC ** -0.5))
    put("ones", np.ones((P, P)))
    put("xg", np.tile(np.arange(WW), (P, 1)))
    put("yg", np.tile(np.arange(NR), (P, 1)))
    put("gmask", p[:, None] // 32 == p[None] % C // CG)
    rep = p[:, None] // C == np.arange(60) - 28
    put("rep1", rep)
    put("rep2", 2.0 * rep)
    put("nrep", -1.0 * (p[:, None] // C == p[None] % B4))
    put("nhalf", -0.5 * (p[:, None] // C == p[None] % B4))
    put("avg", (p[:, None] % C == p[None] % C) / (B * NPIX))
    put("ecmask", p[:, None] // E16 == np.arange(B))
    put("keys", np.tile(E8 - np.arange(E8), (P, 1)))
    dt = np.array([[ON_DVE[UNITS.index((t, j))] for t in range(9)] for j in range(4)])
    put("dtaps", dt[p // 32])
    return c


def _layouts(np, a):
    f = np.float32

    def blocks(w):
        r = np.zeros((P, B4 * w.shape[1]), f)
        for b in range(B4):
            r[b * C:(b + 1) * C, b * w.shape[1]:(b + 1) * w.shape[1]] = w
        return r

    def rows(v):
        return np.tile(v.reshape(1, -1), (P, 1))

    def pack(spec, n, parts):
        out = np.zeros((P, n), f)
        for name, width in spec.items():
            v = parts[name]
            out[0:v.shape[0], width:width + v.shape[1]] = v
        return out

    def top2(i):
        l = f"L{i}_ffn_"
        ew = a[l + "expert_w"].transpose(1, 2, 0).reshape(C, C * E8)
        eb = np.zeros((NT, E8, NT, C), f)
        for t in range(NT):
            eb[t, :, t] = a[l + "expert_b"]
        return blocks(a[l + "router_w"]), rows(a[l + "router_b"]), blocks(ew), eb.reshape(P, NT * C)

    def ec(i):
        l = f"L{i}_ffn_"
        gw = np.zeros((P, NBH, B, E16), f)
        for b in range(B):
            gw[b % B4 * C:(b % B4 + 1) * C, b // B4, b] = a[l + "gate_w"].T
        gb = np.tile(a[l + "gate_b"], B).reshape(P, 1)
        w1 = a[l + "weight1"].transpose(1, 0, 2).reshape(C + 1, E16 * HID)
        w2 = a[l + "weight2"][:, :HID].transpose(1, 0, 2).reshape(HID, E16 * C)
        b2 = a[l + "weight2"][:, HID].T
        return gw.reshape(P, NBH * P), gb, w1, w2, b2

    col4 = lambda v: np.tile(v, B4).reshape(P, 1)
    wa = pack(WA, NWA, {"q0": blocks(a["L0_conv_Wq"].T), "k0": blocks(a["L0_conv_Wk"].T),
                        "v0": blocks(a["L0_conv_Wv"].T), "bq0": col4(a["L0_conv_bq"]), "bk0": col4(a["L0_conv_bk"]),
                        "bv0": rows(a["L0_conv_bv"])})
    w = a["L1_conv_W"].reshape(C, C, 9)
    lw = w.reshape(4, 8, C, 9).transpose(2, 1, 3, 0).reshape(C, 288)
    wf = np.repeat(w.transpose(0, 2, 1).reshape(C, 288), B4, axis=0)
    w9 = np.zeros((B4, C, 9, C, B4), f)
    for b in range(B4):
        w9[b, :, :, :, b] = w.transpose(1, 2, 0)
    r0, rb0, ew0, eb0 = top2(0)
    gw, gb, w1, w2, b2 = ec(1)
    wb = pack(WB, NWB, {"r0": r0, "rb0": rb0, "ew0": ew0, "eb0": eb0, "lw": np.tile(lw, (B4, 1)), "wf": wf,
                        "w9": w9.reshape(P, 9 * P), "gw0": gw, "gb0": gb, "w10": w1, "w20": w2, "b20": b2})
    kinds = np.array([[g * 3 * K9 + (2 * k + t if t < 2 else 2 * K9 + k) for k in range(K9) for g in range(G)]
                      for t in range(3)]).reshape(-1)
    r1, rb1, ew1, eb1 = top2(2)
    wc = pack(WC, NWC, {"om": blocks(a["L2_conv_Wom"][:, kinds]), "bom": rows(a["L2_conv_bom"][kinds]),
                        "val": blocks(a["L2_conv_Wv"]), "bval": np.tile(a["L2_conv_bv"].reshape(1, -1), (1, 16)),
                        "wo": blocks(a["L2_conv_Wo"]), "gamma": col4(a["L2_conv_gamma"]),
                        "beta": col4(a["L2_conv_beta"]), "wc": blocks(a["L2_conv_Wc"].T),
                        "r1": r1, "rb1": rb1, "ew1": ew1, "eb1": eb1})
    p, pix = np.arange(P), np.arange(NPIX)
    span = 2 * WW - 1
    rel = np.zeros((P, 2, HEADS, NPIX), f)
    for half in range(2):
        q = half * P + p
        at = (pix[None] // WW - q[:, None] // WW + HH - 1) * span + pix[None] % WW - q[:, None] % WW + WW - 1
        rel[:, half] = a["L3_conv_pos_enc"][:, at].transpose(1, 0, 2)
    gw, gb, w1, w2, b2 = ec(3)
    wd = pack(WD, NWD, {"q1": blocks(a["L3_conv_Wq"].T), "k1": blocks(a["L3_conv_Wk"].T),
                        "v1": blocks(a["L3_conv_Wv"].T), "bq1": col4(a["L3_conv_bq"]), "bk1": col4(a["L3_conv_bk"]),
                        "bv1": rows(a["L3_conv_bv"]), "u1": blocks(a["L3_conv_Wu"].T), "bu1": rows(a["L3_conv_bu"]),
                        "rel": rel.reshape(P, -1), "gw1": gw, "gb1": gb, "w11": w1, "w21": w2, "b21": b2})
    return wa, wb, wc, wd


def kernel(**inputs):
    import numpy as _np
    import concourse.bacc as _bacc
    from concourse import mybir as _mybir
    from concourse.bass_utils import run_bass_kernel_spmd as _run

    a = {k: _np.asarray(v) for k, v in inputs.items()}
    arrays = {"x": _np.ascontiguousarray(a["x"]), "cst": _constants(_np)}
    arrays.update(zip(("wa", "wb", "wc", "wd"), _layouts(_np, a)))
    nc = _bacc.Bacc("TRN2", target_bir_lowering=False, num_devices=1)
    args = [nc.dram_tensor(f"in_{n}", v.shape, _mybir.dt.float32, kind="ExternalInput").ap() for n, v in arrays.items()]
    out = nc.dram_tensor("out_y", a["x"].shape, _mybir.dt.float32, kind="ExternalOutput").ap()
    metaformer(nc, *args, out)
    r = _run(nc, [{f"in_{n}": v for n, v in arrays.items()}], core_ids=[0])
    return r.results[0]["out_y"]
```
